# Optimizing a Trainium2 kernel written in Bass

```python
import numpy as np
import jax
import jax.numpy as jnp

def _softmax(x, axis=-1):
    return jax.nn.softmax(x, axis=axis)

def _gelu(x):
    return jax.nn.gelu(x, approximate=True)

def _silu(x):
    return jax.nn.silu(x)

def _sigmoid(x):
    return jax.nn.sigmoid(x)

def _layernorm(x, axis=-1, eps=1e-05):
    m = jnp.mean(x, axis=axis, keepdims=True)
    v = jnp.var(x, axis=axis, keepdims=True)
    return (x - m) / jnp.sqrt(v + eps)

def _scatter_add(tgt, idx, src, axis=0):
    return tgt.at[idx].add(src)

def _segment_sum(src, seg, n):
    return jax.ops.segment_sum(src, seg, n)
kernel_name = 'mk_decoder_postln_d2_seqx_r4_74f06d'

def setup_inputs(seed: int=0):
    np.random.seed(seed)
    _w = jnp.asarray

    def _rec_inputs():
        import jax
        import jax.numpy as jnp
        _rk = jax.random.key(seed)
        x = -0.0003929 + 0.9999 * jax.random.normal(jax.random.fold_in(_rk, 1), (4, 512, 256), jnp.float32)
        _lenS = 512 - jax.random.randint(jax.random.fold_in(_rk, 7), (4,), 0, max(1, 512 // 4) + 1, jnp.int32)
        _lenS2 = 512 - jax.random.randint(jax.random.fold_in(_rk, 8), (4,), 0, max(1, 512 // 4) + 1, jnp.int32)
        _ctx_1024P = jax.random.normal(jax.random.fold_in(_rk, 11), (4, 16, 256), jnp.float32)
        _ctx_1024c = jax.random.dirichlet(jax.random.fold_in(_rk, 511), 0.3 * jnp.ones((16,), jnp.float32), (4, 512))
        _ctx_1024t = jnp.einsum('bsk,bkd->bsd', _ctx_1024c, _ctx_1024P)
        _ctx_1024t = _ctx_1024t * jax.lax.rsqrt(jnp.mean(jnp.square(_ctx_1024t)) + 1e-12) * 0.953939
        ctx_1024 = -1.39393e-06 + 0.999914 * (_ctx_1024t + 0.3 * jax.random.normal(jax.random.fold_in(_rk, 611), (4, 512, 256), jnp.float32))
        _validS = jnp.arange(512)[None, :] < _lenS[:, None]
        _validS2 = jnp.arange(512)[None, :] < _lenS2[:, None]
        _causal = jnp.tril(jnp.ones((512, 512), dtype=bool))
        mask_1x1xSxS2_ik0 = jnp.where(jnp.broadcast_to(_validS2[0:1, None, None, :], (1, 1, 512, 512)), 0, 1).astype(jnp.int32)
        return (x, ctx_1024, mask_1x1xSxS2_ik0)
    x, ctx_1024, mask_1x1xSxS2_ik0 = _rec_inputs()

    def _L0_attn_setup():
        import jax, jax.numpy as jnp
        import numpy as np
        B, T, C, H = (2, 1024, 256, 16)
        D = C // H
        SEGMENTS = ((128, 1), (256, 2), (512, 4))

        def _branch(q, k, v, w, r):
            b, h_, t, d = q.shape
            n_seg, eff = (t // w, w // r)
            h = jnp.arange(h_)
            idx = (h % r)[:, None] + jnp.arange(eff)[None, :] * r
            pos = jnp.arange(n_seg)[None, :, None] * w + idx[:, None, :]
            hh = h[:, None, None]
            qg = q[:, hh, pos]
            kg = k[:, hh, pos]
            vg = v[:, hh, pos]
            scores = jnp.einsum('bhsid,bhsjd->bhsij', qg, kg)
            causal = jnp.tril(jnp.ones((eff, eff), bool))
            scores = jnp.where(causal, scores, jnp.finfo(scores.dtype).min)
            m = scores.max(-1, keepdims=True)
            p = jnp.exp(scores - m)
            s = p.sum(-1, keepdims=True)
            o = jnp.einsum('bhsij,bhsjd->bhsid', p, vg) / s
            lse = m[..., 0] + jnp.log(s[..., 0])
            out_full = jnp.zeros((b, h_, t, d), q.dtype).at[:, hh, pos].set(o)
            lse_full = jnp.full((b, h_, t), -1e+30, q.dtype).at[:, hh, pos].set(lse)
            return (out_full, lse_full)

        def _forward(x, c_attn_w, c_attn_b, q_w, q_b, k_w, k_b, v_w, v_b, o_w, o_b):
            b, t, c = x.shape
            qkv = x @ c_attn_w + c_attn_b
            qx, kx, vx = jnp.split(qkv, 3, axis=-1)
            q = (qx @ q_w + q_b).reshape(b, t, H, D).transpose(0, 2, 1, 3) * D ** (-0.5)
            k = (kx @ k_w + k_b).reshape(b, t, H, D).transpose(0, 2, 1, 3)
            v = (vx @ v_w + v_b).reshape(b, t, H, D).transpose(0, 2, 1, 3)
            outs, lses = zip(*[_branch(q, k, v, w, r) for w, r in SEGMENTS])
            O = jnp.stack(outs)
            L = jnp.stack(lses)
            m = L.max(0)
            wts = jnp.exp(L - m)
            y = (wts[..., None] * O).sum(0) / wts.sum(0)[..., None]
            y = y.transpose(0, 2, 1, 3).reshape(b, t, c)
            return y @ o_w + o_b
        key = jax.random.key(seed)
        ks = jax.random.split(key, 12)
        s = 0.02
        return {'x': jax.random.normal(ks[0], (B, T, C), jnp.float32), 'c_attn_w': jax.random.normal(ks[1], (C, 3 * C), jnp.float32) * s, 'c_attn_b': jnp.zeros((3 * C,), jnp.float32), 'q_w': jax.random.normal(ks[2], (C, C), jnp.float32) * s, 'q_b': jnp.zeros((C,), jnp.float32), 'k_w': jax.random.normal(ks[3], (C, C), jnp.float32) * s, 'k_b': jnp.zeros((C,), jnp.float32), 'v_w': jax.random.normal(ks[4], (C, C), jnp.float32) * s, 'v_b': jnp.zeros((C,), jnp.float32), 'o_w': jax.random.normal(ks[5], (C, C), jnp.float32) * s, 'o_b': jnp.zeros((C,), jnp.float32)}
    _L0_attn_all = _L0_attn_setup()
    _L0_attn_in = {k: v for k, v in _L0_attn_all.items() if k in ('c_attn_w', 'c_attn_b', 'q_w', 'q_b', 'k_w', 'k_b', 'v_w', 'v_b', 'o_w', 'o_b')}
    del _L0_attn_all

    def _L0_xattn_setup():
        import jax, jax.numpy as jnp
        import numpy as np
        B, C_LEN, Q_LEN, D = (8, 512, 128, 256)
        key = jax.random.key(seed)
        ks = jax.random.split(key, 10)
        scale = 1.0 / np.sqrt(D)
        return {'c': jax.random.normal(ks[0], (B, C_LEN, D), dtype=jnp.float32), 'q': jax.random.normal(ks[1], (B, Q_LEN, D), dtype=jnp.float32), 'w_cq': jax.random.normal(ks[2], (D,), dtype=jnp.float32) * scale, 'b_cq': jax.random.normal(ks[3], (), dtype=jnp.float32) * scale, 'w_c': jax.random.normal(ks[4], (D,), dtype=jnp.float32) * scale, 'b_c': jax.random.normal(ks[5], (), dtype=jnp.float32) * scale, 'w_q': jax.random.normal(ks[6], (D,), dtype=jnp.float32) * scale, 'b_q': jax.random.normal(ks[7], (), dtype=jnp.float32) * scale, 'W_l': jax.random.normal(ks[8], (D, 4 * D), dtype=jnp.float32) * (1.0 / np.sqrt(4 * D)), 'b_l': jax.random.normal(ks[9], (D,), dtype=jnp.float32) * (1.0 / np.sqrt(4 * D))}
    _L0_xattn_all = _L0_xattn_setup()
    _L0_xattn_in = {k: v for k, v in _L0_xattn_all.items() if k in ('w_cq', 'b_cq', 'w_c', 'b_c', 'w_q', 'b_q', 'W_l', 'b_l')}
    del _L0_xattn_all

    def _L0_ffn_setup():
        import jax, jax.numpy as jnp
        import numpy as np
        B, P, D, D_MLP, E, K = (2, 512, 256, 1024, 8, 2)
        key = jax.random.key(seed)
        k_x, k_g, k_in, k_out = jax.random.split(key, 4)
        s_in = 1.0 / np.sqrt(D).astype(np.float32)
        s_out = 1.0 / np.sqrt(D_MLP).astype(np.float32)
        return {'x': jax.random.normal(k_x, (B, P, D), dtype=jnp.float32), 'W_gate': jax.random.normal(k_g, (D, E), dtype=jnp.float32) * s_in, 'W_in': jax.random.normal(k_in, (E, D, D_MLP), dtype=jnp.float32) * s_in, 'b_in': jnp.zeros((E, D_MLP), dtype=jnp.float32), 'W_out': jax.random.normal(k_out, (E, D_MLP, D), dtype=jnp.float32) * s_out, 'b_out': jnp.zeros((E, D), dtype=jnp.float32)}
    _L0_ffn_all = _L0_ffn_setup()
    _L0_ffn_in = {k: v for k, v in _L0_ffn_all.items() if k in ('W_gate', 'W_in', 'b_in', 'W_out', 'b_out')}
    del _L0_ffn_all

    def _L1_attn_setup():
        import jax, jax.numpy as jnp
        import numpy as np
        B, L, D = (4, 1024, 256)
        PHAZOR_SCALE_START = 32.0
        PHAZOR_SCALE_END = 2048.0
        key = jax.random.key(seed)
        ks = jax.random.split(key, 7)
        x = jax.random.normal(ks[0], (B, L, D), dtype=jnp.float32)
        phazor_init_re = jax.random.normal(ks[1], (D,), dtype=jnp.float32)
        phazor_init_im = jax.random.normal(ks[2], (D,), dtype=jnp.float32)
        phazor_angle = jax.random.normal(ks[3], (D,), dtype=jnp.float32)
        ln_minus_ln_phazor_abs = jax.random.normal(ks[4], (D,), dtype=jnp.float32)
        last_conv_re = jax.random.normal(ks[5], (D,), dtype=jnp.float32)
        last_conv_im = jax.random.normal(ks[6], (D,), dtype=jnp.float32)
        ln_phazor_scale = jnp.exp(jnp.linspace(np.log(1.0 / PHAZOR_SCALE_START), np.log(1.0 / PHAZOR_SCALE_END), D)).astype(jnp.float32)
        return {'x': x, 'phazor_init_re': phazor_init_re, 'phazor_init_im': phazor_init_im, 'phazor_angle': phazor_angle, 'ln_minus_ln_phazor_abs': ln_minus_ln_phazor_abs, 'last_conv_re': last_conv_re, 'last_conv_im': last_conv_im, 'ln_phazor_scale': ln_phazor_scale}
    _L1_attn_all = _L1_attn_setup()
    _L1_attn_in = {k: v for k, v in _L1_attn_all.items() if k in ('phazor_init_re', 'phazor_init_im', 'phazor_angle', 'ln_minus_ln_phazor_abs', 'last_conv_re', 'last_conv_im', 'ln_phazor_scale')}
    del _L1_attn_all

    def _L1_xattn_setup():
        import jax, jax.numpy as jnp
        import numpy as np
        import math
        D_MODEL = 256
        N_HEADS = 16
        D_K = D_MODEL // N_HEADS
        B, S = (2, 512)
        key = jax.random.key(seed)
        ks = jax.random.split(key, 11)
        sc = 1.0 / math.sqrt(D_MODEL)
        inp = {'q': jax.random.normal(ks[0], (B, S, D_MODEL), jnp.float32), 'k': jax.random.normal(ks[1], (B, S, D_MODEL), jnp.float32), 'v': jax.random.normal(ks[2], (B, S, D_MODEL), jnp.float32), 'mask': jnp.tril(jnp.ones((S, S), jnp.int32))[None, None], 'W_q': jax.random.normal(ks[3], (D_MODEL, D_MODEL), jnp.float32) * sc, 'b_q': jnp.zeros((D_MODEL,), jnp.float32), 'W_k': jax.random.normal(ks[4], (D_MODEL, D_MODEL), jnp.float32) * sc, 'b_k': jnp.zeros((D_MODEL,), jnp.float32), 'W_v': jax.random.normal(ks[5], (D_MODEL, D_MODEL), jnp.float32) * sc, 'b_v': jnp.zeros((D_MODEL,), jnp.float32), 'W_o': jax.random.normal(ks[6], (D_MODEL, D_MODEL), jnp.float32) * sc, 'b_o': jnp.zeros((D_MODEL,), jnp.float32)}
        return inp
    _L1_xattn_all = _L1_xattn_setup()
    _L1_xattn_in = {k: v for k, v in _L1_xattn_all.items() if k in ('W_q', 'b_q', 'W_k', 'b_k', 'W_v', 'b_v', 'W_o', 'b_o')}
    del _L1_xattn_all

    def _L1_ffn_setup():
        import jax, jax.numpy as jnp
        import numpy as np
        D_IN, D_HID = (256, 1024)

        def _ternary(key, shape):
            return jax.random.randint(key, shape, -1, 2).astype(jnp.float32)

        def _tlin(x, w, s):
            return jnp.einsum('bsi,oi->bso', x, w) * s
        key = jax.random.key(seed)
        ks = jax.random.split(key, 12)
        inv = lambda fan: 1.0 / np.sqrt(fan).astype(np.float32)
        return {'x': jax.random.normal(ks[0], (4, 512, D_IN), dtype=jnp.float32), 'w1_w': _ternary(ks[1], (D_HID, D_IN)), 'w1_s': jax.random.uniform(ks[2], (D_HID,), dtype=jnp.float32) * inv(D_IN), 'w2_w': _ternary(ks[3], (D_HID, D_IN)), 'w2_s': jax.random.uniform(ks[4], (D_HID,), dtype=jnp.float32) * inv(D_IN), 'h1_w': _ternary(ks[5], (D_HID, D_HID)), 'h1_s': jax.random.uniform(ks[6], (D_HID,), dtype=jnp.float32) * inv(D_HID), 'h2_w': _ternary(ks[7], (D_HID, D_HID)), 'h2_s': jax.random.uniform(ks[8], (D_HID,), dtype=jnp.float32) * inv(D_HID), 'w3_w': _ternary(ks[9], (D_IN, D_HID)), 'w3_s': jax.random.uniform(ks[10], (D_IN,), dtype=jnp.float32) * inv(D_HID)}
    _L1_ffn_all = _L1_ffn_setup()
    _L1_ffn_in = {k: v for k, v in _L1_ffn_all.items() if k in ('w1_w', 'w1_s', 'w2_w', 'w2_s', 'h1_w', 'h1_s', 'h2_w', 'h2_s', 'w3_w', 'w3_s')}
    del _L1_ffn_all
    return {'x': x, 'ctx_1024': ctx_1024, 'mask_1x1xSxS2_ik0': mask_1x1xSxS2_ik0, 'L0_attn_c_attn_w': _L0_attn_in['c_attn_w'], 'L0_attn_c_attn_b': _L0_attn_in['c_attn_b'], 'L0_attn_q_w': _L0_attn_in['q_w'], 'L0_attn_q_b': _L0_attn_in['q_b'], 'L0_attn_k_w': _L0_attn_in['k_w'], 'L0_attn_k_b': _L0_attn_in['k_b'], 'L0_attn_v_w': _L0_attn_in['v_w'], 'L0_attn_v_b': _L0_attn_in['v_b'], 'L0_attn_o_w': _L0_attn_in['o_w'], 'L0_attn_o_b': _L0_attn_in['o_b'], 'L0_xattn_w_cq': _L0_xattn_in['w_cq'], 'L0_xattn_b_cq': _L0_xattn_in['b_cq'], 'L0_xattn_w_c': _L0_xattn_in['w_c'], 'L0_xattn_b_c': _L0_xattn_in['b_c'], 'L0_xattn_w_q': _L0_xattn_in['w_q'], 'L0_xattn_b_q': _L0_xattn_in['b_q'], 'L0_xattn_W_l': _L0_xattn_in['W_l'], 'L0_xattn_b_l': _L0_xattn_in['b_l'], 'L0_ffn_W_gate': _L0_ffn_in['W_gate'], 'L0_ffn_W_in': _L0_ffn_in['W_in'], 'L0_ffn_b_in': _L0_ffn_in['b_in'], 'L0_ffn_W_out': _L0_ffn_in['W_out'], 'L0_ffn_b_out': _L0_ffn_in['b_out'], 'L1_attn_phazor_init_re': _L1_attn_in['phazor_init_re'], 'L1_attn_phazor_init_im': _L1_attn_in['phazor_init_im'], 'L1_attn_phazor_angle': _L1_attn_in['phazor_angle'], 'L1_attn_ln_minus_ln_phazor_abs': _L1_attn_in['ln_minus_ln_phazor_abs'], 'L1_attn_last_conv_re': _L1_attn_in['last_conv_re'], 'L1_attn_last_conv_im': _L1_attn_in['last_conv_im'], 'L1_attn_ln_phazor_scale': _L1_attn_in['ln_phazor_scale'], 'L1_xattn_W_q': _L1_xattn_in['W_q'], 'L1_xattn_b_q': _L1_xattn_in['b_q'], 'L1_xattn_W_k': _L1_xattn_in['W_k'], 'L1_xattn_b_k': _L1_xattn_in['b_k'], 'L1_xattn_W_v': _L1_xattn_in['W_v'], 'L1_xattn_b_v': _L1_xattn_in['b_v'], 'L1_xattn_W_o': _L1_xattn_in['W_o'], 'L1_xattn_b_o': _L1_xattn_in['b_o'], 'L1_ffn_w1_w': _L1_ffn_in['w1_w'], 'L1_ffn_w1_s': _L1_ffn_in['w1_s'], 'L1_ffn_w2_w': _L1_ffn_in['w2_w'], 'L1_ffn_w2_s': _L1_ffn_in['w2_s'], 'L1_ffn_h1_w': _L1_ffn_in['h1_w'], 'L1_ffn_h1_s': _L1_ffn_in['h1_s'], 'L1_ffn_h2_w': _L1_ffn_in['h2_w'], 'L1_ffn_h2_s': _L1_ffn_in['h2_s'], 'L1_ffn_w3_w': _L1_ffn_in['w3_w'], 'L1_ffn_w3_s': _L1_ffn_in['w3_s']}

def reference(x, ctx_1024, mask_1x1xSxS2_ik0, L0_attn_c_attn_w, L0_attn_c_attn_b, L0_attn_q_w, L0_attn_q_b, L0_attn_k_w, L0_attn_k_b, L0_attn_v_w, L0_attn_v_b, L0_attn_o_w, L0_attn_o_b, L0_xattn_w_cq, L0_xattn_b_cq, L0_xattn_w_c, L0_xattn_b_c, L0_xattn_w_q, L0_xattn_b_q, L0_xattn_W_l, L0_xattn_b_l, L0_ffn_W_gate, L0_ffn_W_in, L0_ffn_b_in, L0_ffn_W_out, L0_ffn_b_out, L1_attn_phazor_init_re, L1_attn_phazor_init_im, L1_attn_phazor_angle, L1_attn_ln_minus_ln_phazor_abs, L1_attn_last_conv_re, L1_attn_last_conv_im, L1_attn_ln_phazor_scale, L1_xattn_W_q, L1_xattn_b_q, L1_xattn_W_k, L1_xattn_b_k, L1_xattn_W_v, L1_xattn_b_v, L1_xattn_W_o, L1_xattn_b_o, L1_ffn_w1_w, L1_ffn_w1_s, L1_ffn_w2_w, L1_ffn_w2_s, L1_ffn_h1_w, L1_ffn_h1_s, L1_ffn_h2_w, L1_ffn_h2_s, L1_ffn_w3_w, L1_ffn_w3_s):
    import jax
    import jax.numpy as jnp

    def _L0_attn_ref(x, c_attn_w, c_attn_b, q_w, q_b, k_w, k_b, v_w, v_b, o_w, o_b):
        import jax, jax.numpy as jnp
        import numpy as np
        B, T, C, H = (2, 1024, 256, 16)
        D = C // H
        SEGMENTS = ((128, 1), (256, 2), (512, 4))

        def _branch(q, k, v, w, r):
            b, h_, t, d = q.shape
            n_seg, eff = (t // w, w // r)
            h = jnp.arange(h_)
            idx = (h % r)[:, None] + jnp.arange(eff)[None, :] * r
            pos = jnp.arange(n_seg)[None, :, None] * w + idx[:, None, :]
            hh = h[:, None, None]
            qg = q[:, hh, pos]
            kg = k[:, hh, pos]
            vg = v[:, hh, pos]
            scores = jnp.einsum('bhsid,bhsjd->bhsij', qg, kg)
            causal = jnp.tril(jnp.ones((eff, eff), bool))
            scores = jnp.where(causal, scores, jnp.finfo(scores.dtype).min)
            m = scores.max(-1, keepdims=True)
            p = jnp.exp(scores - m)
            s = p.sum(-1, keepdims=True)
            o = jnp.einsum('bhsij,bhsjd->bhsid', p, vg) / s
            lse = m[..., 0] + jnp.log(s[..., 0])
            out_full = jnp.zeros((b, h_, t, d), q.dtype).at[:, hh, pos].set(o)
            lse_full = jnp.full((b, h_, t), -1e+30, q.dtype).at[:, hh, pos].set(lse)
            return (out_full, lse_full)

        def _forward(x, c_attn_w, c_attn_b, q_w, q_b, k_w, k_b, v_w, v_b, o_w, o_b):
            b, t, c = x.shape
            qkv = x @ c_attn_w + c_attn_b
            qx, kx, vx = jnp.split(qkv, 3, axis=-1)
            q = (qx @ q_w + q_b).reshape(b, t, H, D).transpose(0, 2, 1, 3) * D ** (-0.5)
            k = (kx @ k_w + k_b).reshape(b, t, H, D).transpose(0, 2, 1, 3)
            v = (vx @ v_w + v_b).reshape(b, t, H, D).transpose(0, 2, 1, 3)
            outs, lses = zip(*[_branch(q, k, v, w, r) for w, r in SEGMENTS])
            O = jnp.stack(outs)
            L = jnp.stack(lses)
            m = L.max(0)
            wts = jnp.exp(L - m)
            y = (wts[..., None] * O).sum(0) / wts.sum(0)[..., None]
            y = y.transpose(0, 2, 1, 3).reshape(b, t, c)
            return y @ o_w + o_b
        return _forward(x, c_attn_w, c_attn_b, q_w, q_b, k_w, k_b, v_w, v_b, o_w, o_b)

    def _L0_xattn_ref(c, q, w_cq, b_cq, w_c, b_c, w_q, b_q, W_l, b_l):
        import jax, jax.numpy as jnp
        import numpy as np
        B, C_LEN, Q_LEN, D = (8, 512, 128, 256)
        cq = jnp.einsum('bcd,bqd,d->bcq', c, q, w_cq) + b_cq
        s = (c @ w_c + b_c)[:, :, None] + (q @ w_q + b_q)[:, None, :] + cq
        a = jax.nn.softmax(s, axis=2)
        c2q_att = jnp.einsum('bcq,bqd->bcd', a, q)
        b_att = jax.nn.softmax(jnp.max(s, axis=2), axis=1)
        q2c_att = jnp.einsum('bc,bcd->bd', b_att, c)[:, None, :]
        x = jnp.concatenate([c, c2q_att, c * c2q_att, c * q2c_att], axis=-1)
        z = x @ W_l.T + b_l
        return z

    def _L0_ffn_ref(x, W_gate, W_in, b_in, W_out, b_out):
        import jax, jax.numpy as jnp
        import numpy as np
        B, P, D, D_MLP, E, K = (2, 512, 256, 1024, 8, 2)
        gate_logits = jnp.einsum('bpd,de->bpe', x, W_gate)
        top_w, top_idx = jax.lax.top_k(gate_logits, K)
        top_w = jax.nn.softmax(top_w, axis=-1)
        combine = jnp.einsum('bpke,bpk->bpe', jax.nn.one_hot(top_idx, E, dtype=x.dtype), top_w)
        out = jnp.zeros_like(x)
        for e in range(E):
            h = jax.nn.gelu(jnp.einsum('bpd,dm->bpm', x, W_in[e]) + b_in[e], approximate=False)
            y = jnp.einsum('bpm,md->bpd', h, W_out[e]) + b_out[e]
            out = out + combine[..., e, None] * y
        return out

    def _L1_attn_ref(x, phazor_init_re, phazor_init_im, phazor_angle, ln_minus_ln_phazor_abs, last_conv_re, last_conv_im, ln_phazor_scale):
        import jax, jax.numpy as jnp
        import numpy as np
        B, L, D = (4, 1024, 256)
        PHAZOR_SCALE_START = 32.0
        PHAZOR_SCALE_END = 2048.0
        b, length, d = x.shape
        dtype = x.dtype
        xc = x.astype(jnp.complex64)
        decay = jnp.exp(ln_minus_ln_phazor_abs)
        phazor = jnp.exp((phazor_angle * 1j - decay) * ln_phazor_scale)
        t = jnp.arange(length, dtype=jnp.float32)[:, None]
        phazor_progression = phazor[None, :] ** t
        phazor_init = phazor_init_re + 1j * phazor_init_im
        filt = phazor_progression * phazor_init[None, :]
        filter_fft = jnp.fft.fft(filt, n=2 * length, axis=0)
        x_fft = jnp.fft.fft(xc, n=2 * length, axis=1)
        conv_filter_x = jnp.fft.ifft(filter_fft[None] * x_fft, axis=1)[:, :length]
        last_conv = (last_conv_re + 1j * last_conv_im)[None, None, :]
        conv_with_past = conv_filter_x + last_conv * phazor_progression[None] * phazor[None, None, :]
        gate = 1.0 - jnp.exp(-decay * ln_phazor_scale)
        y = conv_with_past * gate
        return y.real.astype(dtype)

    def _L1_xattn_ref(q, k, v, mask, W_q, b_q, W_k, b_k, W_v, b_v, W_o, b_o):
        import jax, jax.numpy as jnp
        import numpy as np
        import math
        D_MODEL = 256
        N_HEADS = 16
        D_K = D_MODEL // N_HEADS
        B, S = (2, 512)

        def split_heads(x):
            b, s, _ = x.shape
            return x.reshape(b, s, N_HEADS, D_K).transpose(0, 2, 1, 3)
        Q = split_heads(q @ W_q + b_q)
        K = split_heads(k @ W_k + b_k)
        V = split_heads(v @ W_v + b_v)
        scores = jnp.einsum('bhqd,bhkd->bhqk', Q, K) / math.sqrt(D_K)
        scores = jnp.where(mask == 0, jnp.float32(-1000000000.0), scores)
        attn = jax.nn.softmax(scores, axis=-1)
        out = jnp.einsum('bhqk,bhkd->bhqd', attn, V)
        out = out.transpose(0, 2, 1, 3).reshape(q.shape[0], -1, D_MODEL)
        return out @ W_o + b_o

    def _L1_ffn_ref(x, w1_w, w1_s, w2_w, w2_s, h1_w, h1_s, h2_w, h2_s, w3_w, w3_s):
        import jax, jax.numpy as jnp
        import numpy as np
        D_IN, D_HID = (256, 1024)

        def _ternary(key, shape):
            return jax.random.randint(key, shape, -1, 2).astype(jnp.float32)

        def _tlin(x, w, s):
            return jnp.einsum('bsi,oi->bso', x, w) * s
        h = jax.nn.silu(_tlin(x, w1_w, w1_s)) * _tlin(x, w2_w, w2_s)
        h = jax.nn.gelu(_tlin(h, h1_w, h1_s), approximate=False)
        h = jax.nn.gelu(_tlin(h, h2_w, h2_s), approximate=False)
        return _tlin(h, w3_w, w3_s)
    x = _layernorm(x + _L0_attn_ref(x, L0_attn_c_attn_w, L0_attn_c_attn_b, L0_attn_q_w, L0_attn_q_b, L0_attn_k_w, L0_attn_k_b, L0_attn_v_w, L0_attn_v_b, L0_attn_o_w, L0_attn_o_b), axis=-1)
    x = _layernorm(x + _L0_xattn_ref(x, ctx_1024, L0_xattn_w_cq, L0_xattn_b_cq, L0_xattn_w_c, L0_xattn_b_c, L0_xattn_w_q, L0_xattn_b_q, L0_xattn_W_l, L0_xattn_b_l), axis=-1)
    x = _layernorm(x + _L0_ffn_ref(x, L0_ffn_W_gate, L0_ffn_W_in, L0_ffn_b_in, L0_ffn_W_out, L0_ffn_b_out), axis=-1)
    x = _layernorm(x + _L1_attn_ref(x, L1_attn_phazor_init_re, L1_attn_phazor_init_im, L1_attn_phazor_angle, L1_attn_ln_minus_ln_phazor_abs, L1_attn_last_conv_re, L1_attn_last_conv_im, L1_attn_ln_phazor_scale), axis=-1)
    x = _layernorm(x + _L1_xattn_ref(x, ctx_1024, ctx_1024, mask_1x1xSxS2_ik0, L1_xattn_W_q, L1_xattn_b_q, L1_xattn_W_k, L1_xattn_b_k, L1_xattn_W_v, L1_xattn_b_v, L1_xattn_W_o, L1_xattn_b_o), axis=-1)
    x = _layernorm(x + _L1_ffn_ref(x, L1_ffn_w1_w, L1_ffn_w1_s, L1_ffn_w2_w, L1_ffn_w2_s, L1_ffn_h1_w, L1_ffn_h1_s, L1_ffn_h2_w, L1_ffn_h2_s, L1_ffn_w3_w, L1_ffn_w3_s), axis=-1)
    return x

_drawn_inputs = setup_inputs


def setup_inputs(seed=0):
    import zlib

    import numpy as np

    out = dict(_drawn_inputs(seed))
    spreads = {'L0_attn_c_attn_b': (0.0, 0.1),
     'L0_attn_q_b': (0.0, 0.8),
     'L0_attn_k_b': (0.0, 2.0),
     'L0_attn_v_b': (0.0, 0.1),
     'L0_attn_o_b': (0.0, 0.1),
     'L0_ffn_b_in': (0.0, 0.1),
     'L0_ffn_b_out': (0.0, 0.1),
     'L1_xattn_b_q': (0.0, 0.354),
     'L1_xattn_b_k': (0.0, 2.0),
     'L1_xattn_b_v': (0.0, 0.1),
     'L1_xattn_b_o': (0.0, 0.1)}
    factors = {'L0_attn_c_attn_w': 2.771,
     'L0_attn_q_w': 8.0,
     'L0_attn_k_w': 8.0,
     'L1_attn_last_conv_re': 8.0,
     'L1_attn_last_conv_im': 42.478,
     'L1_ffn_w1_w': 8.0,
     'L1_ffn_w1_s': 8.0,
     'L1_ffn_w2_w': 8.0,
     'L1_ffn_w2_s': 8.0,
     'L1_ffn_h1_w': 8.0,
     'L1_ffn_h1_s': 8.0,
     'L1_ffn_h2_w': 8.0,
     'L1_ffn_h2_s': 8.0,
     'L1_ffn_w3_w': 8.0,
     'L1_ffn_w3_s': 8.0}
    for name, (base, spread) in spreads.items():
        noise = np.random.default_rng([zlib.crc32(name.encode()), seed]).standard_normal(out[name].shape)
        drawn = base * np.exp(spread * noise) if base else spread * noise
        out[name] = jnp.asarray(drawn.astype(out[name].dtype))
    for name, factor in factors.items():
        out[name] = (out[name] * factor).astype(out[name].dtype)
    return out
```

```python
from contextlib import ExitStack

import concourse.bass as bass
from concourse import mybir

F32 = mybir.dt.float32
F16 = mybir.dt.float16
BF16 = mybir.dt.bfloat16
I32 = mybir.dt.int32
ALU = mybir.AluOpType
ACT = mybir.ActivationFunctionType
AX = mybir.AxisListType

P = 128
B, SEQ, D = 4, 512, 256
TILES = SEQ // P
KD = D // P
H, DH = 16, 16
QUADS = H // 4
EPS = 1e-5
MASKED = -60000.0
PARTS = 4
ZERO_ROW = PARTS * DH
MAX_ROW = ZERO_ROW + 1
ROWS = MAX_ROW + 1


def wait_first(eng, sem, value, passed):
    eng.wait_ge(sem, value)
    eng.sem_inc(passed, 1)


class Stage(ExitStack):

    def __init__(self, nc):
        super().__init__()
        self.nc, self.semaphores = nc, []

    def semaphore(self, name):
        self.semaphores.append(self.nc.alloc_semaphore(name))
        return self.semaphores[-1]

    def __exit__(self, *error):
        closed = super().__exit__(*error)
        if self.semaphores and error[0] is None:
            self.nc.clear_and_free_semaphores(self.semaphores)
            self.nc.all_engine_barrier()
        return closed


class Signal:

    def __init__(self, ctx, nc, name, per):
        self.sem = ctx.semaphore(name)
        self.per = per

    def at(self, turn, n):
        return turn * self.per + n


class Chain:

    def __init__(self, ctx, nc, name, eng=None, per=0):
        self.sem = ctx.semaphore(name)
        self.eng, self.per, self.turn, self.n, self.base = eng, per, 0, 0, 0

    def start(self, turn):
        self.turn, self.n = turn, 0

    def do(self, ins):
        ins.then_inc(self.sem, 1)
        self.n += 1

    def settle(self):
        self.eng.wait_ge(self.sem, self.turn * self.per + self.base + self.n)

    def settle_first(self, passed):
        wait_first(self.eng, self.sem, self.turn * self.per + self.base + self.n, passed)

    def link(self, ins):
        self.do(ins)
        self.settle()

    def end(self):
        assert self.n == self.per, (self.n, self.per)


def batch_cols(turn):
    return bass.ds(turn * SEQ, SEQ)


class Norm:

    CHAIN = 2 * TILES

    def __init__(self, ctx, nc, k, tag):
        self.nc, self.k = nc, k
        self.xs = ctx.enter_context(nc.sbuf_tensor(f"{tag}_xs", [P, TILES, D], F32))
        self.xn = ctx.enter_context(nc.sbuf_tensor(f"{tag}_xn", [P, TILES, D], F32))
        self.kept = Signal(ctx, nc, f"{tag}_kept", 1)
        self.stats = ctx.enter_context(nc.sbuf_tensor(f"{tag}_stats", [P, TILES, 6], F32))
        self.mean_var = ctx.enter_context(nc.sbuf_tensor(f"{tag}_mean_var", [P, TILES, 2], F32))
        self.var_eps = ctx.enter_context(nc.sbuf_tensor(f"{tag}_var_eps", [P, TILES], F32))
        self.rstd = ctx.enter_context(nc.sbuf_tensor(f"{tag}_rstd", [P, TILES], F32))
        self.summed = Signal(ctx, nc, f"{tag}_summed", TILES)
        self.var_ready = Signal(ctx, nc, f"{tag}_var_ready", 1)
        self.rstd_ready = Signal(ctx, nc, f"{tag}_rstd_ready", 1)
        self.normed = Signal(ctx, nc, f"{tag}_normed", TILES)
        self.turned = Signal(ctx, nc, f"{tag}_turned", KD)
        self.xT_ready = Signal(ctx, nc, f"{tag}_xT_ready", KD)

    def start(self, act):
        act.sem_inc(self.xT_ready.sem, 2 * KD)

    def wait_finished(self, eng, turn, ago):
        eng.wait_ge(self.xT_ready.sem, self.xT_ready.at(turn, (3 - ago) * KD))

    def add_tile(self, dve, chain, turn, t, y):
        x = self.k["x"][:, bass.ds(turn * TILES + t, 1), :].rearrange("p a d -> p (a d)")
        if y is None:
            dve.tensor_copy(self.xs[:, t, :], x).then_inc(self.summed.sem, 1)
        else:
            dve.tensor_tensor(self.xs[:, t, :], y, x, ALU.add).then_inc(self.summed.sem, 1)
        dve.wait_ge(self.summed.sem, self.summed.at(turn, t + 1))
        chain.do(dve.bn_stats(self.stats[:, t, :], self.xs[:, t, :]))

    def vector_end(self, dve, chain, turn):
        chain.settle_first(self.k["passed"])
        for t in range(TILES):
            chain.do(dve.bn_aggr(self.mean_var[:, t, :], self.stats[:, t, :]))
        chain.settle()
        dve.tensor_scalar(self.var_eps[:, :], self.mean_var[:, :, 1], EPS, None, ALU.add).then_inc(self.var_ready.sem, 1)
        dve.wait_ge(self.rstd_ready.sem, self.rstd_ready.at(turn, 1))
        for t in range(TILES):
            dve.tensor_scalar(self.xn[:, t, :], self.xs[:, t, :], self.mean_var[:, t, 0:1], self.rstd[:, t:t + 1], ALU.subtract,
                              ALU.mult).then_inc(self.normed.sem, 1)

    def pool(self, pool, turn):
        pool.wait_ge(self.var_ready.sem, self.var_ready.at(turn, 1))
        pool.tensor_tensor(self.rstd[:, :], self.var_eps[:, :], self.k["minus_half"][:, 0:TILES],
                           ALU.pow).then_inc(self.rstd_ready.sem, 1)
        pool.wait_ge(self.normed.sem, self.normed.at(turn, TILES))
        pool.tensor_copy(self.k["x"][:, bass.ds(turn * TILES, TILES), :], self.xn[:, :, :]).then_inc(self.kept.sem, 1)

    def tensor(self, pe, turn, banks):
        for kk in range(KD):
            for t in range(TILES):
                pe.wait_ge(self.normed.sem, self.normed.at(turn, t + 1))
                last = pe.transpose(banks[kk][:, t * P:(t + 1) * P], self.xn[:, t, kk * P:(kk + 1) * P], self.k["ident"][:, :])
            last.then_inc(self.turned.sem, 1)

    def scalar(self, act, turn, banks):
        for kk in range(KD):
            act.wait_ge(self.turned.sem, self.turned.at(turn, kk + 1))
            act.copy(self.k["xT"][:, kk, batch_cols(turn)], banks[kk][:, :]).then_inc(self.xT_ready.sem, 1)

CAUSAL_W = 128
BRANCHES = ((128, 1), (256, 2), (512, 4))
BLOCKS = 7
MAX_SLOTS = 12


def block_columns(j, h):
    if j < 4:
        return slice(j * P, (j + 1) * P)
    if j < 6:
        first = (j - 4) * 256 + h % 2
        return slice(first, first + 255, 2)
    return slice(h % 4, h % 4 + 509, 4)


def max_slot(j, h):
    return j if j < 4 else (4 + 2 * (j - 4) + h % 2 if j < 6 else 8 + h % 4)


def slot_columns(s):
    return block_columns(s, 0) if s < 4 else (block_columns(4 + (s - 4) // 2, (s - 4) % 2) if s < 8 else block_columns(6, s - 8))


def split_projection(nc, k, tag, src_q, src_k, wq, wk, bias, q_dram, k_dram, q_scale=None):
    NM = 2 * KD
    STORES = 16 * 2 * NM
    with Stage(nc) as ctx:
        hi = ctx.enter_context(nc.sbuf_tensor(f"{tag}_hi", [P, 2, NM, SEQ], F16))
        lo = ctx.enter_context(nc.sbuf_tensor(f"{tag}_lo", [P, 2, NM, SEQ], F16))
        ps = [ctx.enter_context(nc.psum_tensor(f"{tag}_ps{j}", [P, SEQ], F32)) for j in range(NM)]
        product_done = Signal(ctx, nc, f"{tag}_product_done", NM)
        hi_ready = Signal(ctx, nc, f"{tag}_hi_ready", NM)
        lo_ready = Signal(ctx, nc, f"{tag}_lo_ready", NM)
        q_full = ctx.enter_context(nc.sbuf_tensor(f"{tag}_q_full", [P, KD, SEQ], F32))
        scaled = Signal(ctx, nc, f"{tag}_scaled", KD)
        bank_free = Signal(ctx, nc, f"{tag}_bank_free", NM)
        stored = [Signal(ctx, nc, f"{tag}_stored{n}", STORES) for n in range(2)]
        block = ctx.enter_context(nc.Block())

        @block.tensor
        def _(pe):
            with pe.Fori(0, B) as i:
                for j in range(NM):
                    w, s, m = (wq, src_q, j) if j < KD else (wk, src_k, j - KD)
                    pe.wait_ge(bank_free.sem, bank_free.at(i, j + 1))
                    for c in range(KD):
                        last = pe.matmul(ps[j][:, :], w[:, c, m * P:(m + 1) * P], s[:, c, batch_cols(i)],
                                         start=(c == 0), stop=(c == KD - 1))
                    last.then_inc(product_done.sem, 1)

        @block.scalar
        def _(act):
            with act.Fori(0, B // 2) as two:
                i2 = two * 2
                for half in range(2):
                    i = i2 + half
                    act.wait_ge(stored[half].sem, i2 * (STORES // 2) + STORES)
                    for j in range(NM):
                        if q_scale is not None and j < KD:
                            act.wait_ge(scaled.sem, scaled.at(i, j + 1))
                            act.copy(hi[:, half, j, :], q_full[:, j, :]).then_inc(hi_ready.sem, 1)
                            continue
                        act.wait_ge(product_done.sem, product_done.at(i, j + 1))
                        act.activation(hi[:, half, j, :], ps[j][:, :], ACT.Identity, bias=bias[:, j:j + 1]).then_inc(hi_ready.sem, 1)

        @block.vector
        def _(dve):
            dve.sem_inc(bank_free.sem, NM)
            with dve.Fori(0, B // 2) as two:
                i2 = two * 2
                for half in range(2):
                    i = i2 + half
                    for j in range(NM):
                        if q_scale is not None and j < KD:
                            dve.wait_ge(product_done.sem, product_done.at(i, j + 1))
                            dve.scalar_tensor_tensor(q_full[:, j, :], ps[j][:, :], bias[:, j:j + 1], q_scale[:, :],
                                                     ALU.add, ALU.mult).then_inc(scaled.sem, 1)
                            dve.wait_ge(hi_ready.sem, hi_ready.at(i, j + 1))
                            dve.tensor_tensor(lo[:, half, j, :], q_full[:, j, :], hi[:, half, j, :], ALU.subtract).then_inc(lo_ready.sem, 1)
                            dve.wait_ge(lo_ready.sem, lo_ready.at(i, j + 1))
                            dve.sem_inc(bank_free.sem, 1)
                            continue
                        dve.wait_ge(hi_ready.sem, hi_ready.at(i, j + 1))
                        dve.scalar_tensor_tensor(lo[:, half, j, :], ps[j][:, :], bias[:, j:j + 1], hi[:, half, j, :],
                                                 ALU.add, ALU.subtract).then_inc(lo_ready.sem, 1)
                        dve.wait_ge(lo_ready.sem, lo_ready.at(i, j + 1))
                        dve.sem_inc(bank_free.sem, 1)

        @block.sync
        def _(sp):
            for n in range(2):
                sp.sem_inc(stored[n].sem, STORES)
            with sp.Fori(0, B // 2) as two:
                i2 = two * 2
                for half in range(2):
                    i = i2 + half
                    for j in range(NM):
                        dst = q_dram if j < KD else k_dram
                        rows = slice((j % KD) * P, (j % KD + 1) * P)
                        sp.wait_ge(hi_ready.sem, hi_ready.at(i, j + 1))
                        sp.dma_start(dst[0, rows, batch_cols(i)], hi[:, half, j, :]).then_inc(stored[half].sem, 16)
                        sp.wait_ge(lo_ready.sem, lo_ready.at(i, j + 1))
                        sp.dma_start(dst[1, rows, batch_cols(i)], lo[:, half, j, :]).then_inc(stored[half].sem, 16)
            for n in range(2):
                sp.wait_ge(stored[n].sem, STORES * (B // 2 + 1))


class Stacks:

    LOADS = 16 * 2 * PARTS

    def __init__(self, ctx, nc, tag, q_dram, k_dram):
        self.q = ctx.enter_context(nc.sbuf_tensor(f"{tag}_qs", [ROWS, 2, H, SEQ], F16))
        self.kk = ctx.enter_context(nc.sbuf_tensor(f"{tag}_ks", [ROWS, 2, H, SEQ], F16))
        self.loaded = [Signal(ctx, nc, f"{tag}_stack_loaded{n}", self.LOADS) for n in range(2)]
        self.edges = Signal(ctx, nc, f"{tag}_stack_edges", 1)
        self.q_dram, self.k_dram = q_dram, k_dram

    def set_edges(self, dve, chain):
        chain.link(dve.memset(self.q[ZERO_ROW:ROWS, :, :, :], 0.0))
        chain.link(dve.memset(self.kk[ZERO_ROW:ROWS, :, :, :], -1.0))
        dve.memset(self.kk[ZERO_ROW:ZERO_ROW + 1, :, :, :], 0.0).then_inc(self.edges.sem, 1)

    def load(self, sp, i2, half, norm):
        norm.wait_finished(sp, i2 + half, 2)
        for part in range(PARTS):
            rows = slice(part * DH, (part + 1) * DH)
            for dst, src, which in ((self.q, self.q_dram, part // 2), (self.kk, self.k_dram, part % 2)):
                s = src[which].rearrange("(d h) t -> d h t", h=H)
                sp.dma_start(dst[rows, half, :, :], s[:, :, batch_cols(i2 + half)]).then_inc(self.loaded[half].sem, 16)

    def wait_loaded(self, eng, i2, half):
        eng.wait_ge(self.loaded[half].sem, i2 * (self.LOADS // 2) + self.LOADS)


class Attend:

    CHAIN = 0

    def __init__(self, ctx, nc, k, tag, wo, bank, misc):
        self.k, self.wo, self.bank, self.misc = k, wo, bank, misc
        self.us = ctx.enter_context(nc.sbuf_tensor(f"{tag}_us", [P, 2, SEQ], F32))
        self.recip = ctx.enter_context(nc.sbuf_tensor(f"{tag}_recip", [P, 2, SEQ], F32))
        self.yT = ctx.enter_context(nc.sbuf_tensor(f"{tag}_yT", [P, QUADS, SEQ], F32))
        self.u_kept = Signal(ctx, nc, f"{tag}_u_kept", QUADS)
        self.z_ready = Signal(ctx, nc, f"{tag}_z_ready", QUADS)
        self.recip_ready = Signal(ctx, nc, f"{tag}_recip_ready", QUADS)
        self.y_kept = Signal(ctx, nc, f"{tag}_y_kept", QUADS)
        self.out_ready = Signal(ctx, nc, f"{tag}_out_ready", TILES)
        self.norm = Norm(ctx, nc, k, tag)

    def tensor_denominators(self, pe, i, g):
        pe.wait_ge(self.u_kept.sem, self.u_kept.at(i, g + 1))
        if g >= 1:
            pe.wait_ge(self.recip_ready.sem, self.recip_ready.at(i, g))
        pe.matmul(self.misc[:, :], self.k["spread"][:, :], self.us[:, g % 2, :], start=True,
                  stop=True).then_inc(self.z_ready.sem, 1)

    def scalar_keep(self, act, i, g, ready, n):
        act.wait_ge(ready.sem, ready.at(i, n))
        if g >= 2:
            act.wait_ge(self.y_kept.sem, self.y_kept.at(i, g - 1))
        act.copy(self.us[:, g % 2, :], self.bank[:, :]).then_inc(self.u_kept.sem, 1)

    def vector_divide(self, dve, i, g):
        dve.wait_ge(self.z_ready.sem, self.z_ready.at(i, g + 1))
        dve.reciprocal(self.recip[:, g % 2, :], self.misc[:, :]).then_inc(self.recip_ready.sem, 1)
        dve.wait_ge(self.recip_ready.sem, self.recip_ready.at(i, g + 1))
        dve.tensor_tensor(self.yT[:, g, :], self.us[:, g % 2, :], self.recip[:, g % 2, :], ALU.mult).then_inc(self.y_kept.sem, 1)

    def tensor_out(self, pe, i):
        for t in range(TILES):
            bank = (self.bank, self.misc)[t % 2]
            if t == 0:
                pe.wait_ge(self.y_kept.sem, self.y_kept.at(i, QUADS))
            if t >= 2:
                pe.wait_ge(self.norm.summed.sem, self.norm.summed.at(i, t - 1))
            for g in range(QUADS):
                last = pe.matmul(bank[:, 0:D], self.yT[:, g, t * P:(t + 1) * P], self.wo[:, g, :],
                                 start=(g == 0), stop=(g == QUADS - 1))
            last.then_inc(self.out_ready.sem, 1)
        self.norm.tensor(pe, i, (self.bank, self.misc))

    def vector_out(self, dve, chain, i):
        for t in range(TILES):
            dve.wait_ge(self.out_ready.sem, self.out_ready.at(i, t + 1))
            self.norm.add_tile(dve, chain, i, t, (self.bank, self.misc)[t % 2][:, 0:D])
        self.norm.vector_end(dve, chain, i)


def dilated_attention(nc, k, q_dram, k_dram, wv, bv, wo):
    with Stage(nc) as ctx:
        xb = ctx.enter_context(nc.sbuf_tensor("a_xb", [P, KD, SEQ], F32))
        ve = ctx.enter_context(nc.sbuf_tensor("a_ve", [P, H, BLOCKS, 2 * DH], F32))
        mx = ctx.enter_context(nc.sbuf_tensor("a_mx", [P, MAX_SLOTS, H], F16))
        mrow = ctx.enter_context(nc.sbuf_tensor("a_mrow", [H, 2, SEQ], F32))
        mt = ctx.enter_context(nc.sbuf_tensor("a_mt", [H, SEQ], F16))
        probs = ctx.enter_context(nc.sbuf_tensor("a_probs", [P, 2, 2, 4, P], F32))
        banks = [ctx.enter_context(nc.psum_tensor(f"a_bank{n}", [P, SEQ], F32)) for n in range(2)]
        pair = [ctx.enter_context(nc.psum_tensor(f"a_pair{n}", [P, 2, 4, P], F32)) for n in range(2)]
        u_bank = ctx.enter_context(nc.psum_tensor("a_u", [P, SEQ], F32))
        misc = ctx.enter_context(nc.psum_tensor("a_misc", [P, SEQ], F32))
        stacks = Stacks(ctx, nc, "a", q_dram, k_dram)
        tail = Attend(ctx, nc, k, "a", wo, u_bank, misc)
        norm = tail.norm
        NA = QUADS * BLOCKS
        NB = QUADS * BLOCKS // 2
        xb_ready = Signal(ctx, nc, "a_xb_ready", 1)
        v_done = Signal(ctx, nc, "a_v_done", TILES)
        v_kept = Signal(ctx, nc, "a_v_kept", TILES)
        s_done = Signal(ctx, nc, "a_s_done", NA)
        s_max = Signal(ctx, nc, "a_s_max", NA)
        m_turned = Signal(ctx, nc, "a_m_turned", 3)
        m_first = Signal(ctx, nc, "a_m_first", 1)
        m_best = Signal(ctx, nc, "a_m_best", 2)
        m_row = [Signal(ctx, nc, f"a_m_row{n}", 16) for n in range(2)]
        t_done = Signal(ctx, nc, "a_t_done", NB)
        exp_done = Signal(ctx, nc, "a_exp_done", NB)
        exp_read = Signal(ctx, nc, "a_exp_read", NB)
        chain_sem = Chain(ctx, nc, "a_chain")
        half_quad = Signal(ctx, nc, "a_half_quad", QUADS // 2)
        block = ctx.enter_context(nc.Block())

        @block.sync
        def _(sp):
            with sp.Fori(0, B // 2) as two:
                i2 = two * 2
                for half in range(2):
                    stacks.load(sp, i2, half, norm)
                for half in range(2):
                    sp.wait_ge(m_best.sem, m_best.at(i2 + half, 2))
                    sp.wait_ge(stacks.edges.sem, 1)
                    sp.dma_start(stacks.q[MAX_ROW:ROWS, half, :, :], mt[:, :]).then_inc(m_row[half].sem, 16)

        @block.gpsimd
        def _(pool):
            with pool.Fori(0, B) as i:
                pool.tensor_copy(xb[:, :, :], k["xT"][:, :, batch_cols(i)]).then_inc(xb_ready.sem, 1)
                norm.pool(pool, i)

        @block.tensor
        def _(pe):
            def maxima(i, half):
                for u in range(NA):
                    j, g = u // QUADS, u % QUADS
                    bank = banks[u % 2]
                    if u >= 2:
                        pe.wait_ge(s_max.sem, s_max.at(i, u - 1))
                    pe.matmul(bank[:, :], k["ident16"][:, :], k["causal"][:, :], start=True, stop=False, skip_group_check=True)
                    for n in range(4):
                        h = 4 * g + n
                        c = block_columns(j, h)
                        last = pe.matmul(bank[:, n * P:(n + 1) * P], stacks.q[0:MAX_ROW, half, h, c],
                                         stacks.kk[0:MAX_ROW, half, h, c], start=False, stop=True, skip_group_check=True)
                    last.then_inc(s_done.sem, 1)

            def turn_maxima(i):
                pe.wait_ge(s_max.sem, s_max.at(i, NA))
                for branch, (slots, bank) in enumerate(((range(0, 4), banks[0]), (range(4, 8), banks[1]), (range(8, 12), misc))):
                    for n, s in enumerate(slots):
                        last = pe.matmul(bank[0:H, slot_columns(s)], mx[:, s, :], k["ident16"][:, :],
                                         start=(n == 0), stop=(n == 3), skip_group_check=True)
                    last.then_inc(m_turned.sem, 1)

            def values(i):
                norm.wait_finished(pe, i, 1)
                pe.wait_ge(xb_ready.sem, i + 1)
                for s in range(TILES):
                    bank = (misc, u_bank)[s % 2]
                    if s >= 2:
                        pe.wait_ge(v_kept.sem, v_kept.at(i, s - 1))
                    wh = wv[:, :, :].rearrange("p c (h d) -> p c h d", d=DH)
                    for cols, first, step, at in ((block_columns(s, 0), 0, 1, 0),
                                                  (block_columns(4 + s // 2, s % 2), s % 2, 2, D),
                                                  (block_columns(6, s), s, 4, D + D // 2)):
                        for c in range(KD):
                            last = pe.matmul(bank[:, at:at + D // step], xb[:, c, cols], wh[:, c, first::step, :],
                                             start=(c == 0), stop=(c == KD - 1), skip_group_check=True)
                    last.then_inc(v_done.sem, 1)

            def weighted(i, p):
                pe.wait_ge(exp_done.sem, exp_done.at(i, p + 1))
                for n in range(2):
                    g, j = (2 * p + n) // BLOCKS, (2 * p + n) % BLOCKS
                    if j == 0:
                        if g == 0:
                            pe.wait_ge(v_kept.sem, v_kept.at(i, TILES))
                        else:
                            pe.wait_ge(tail.u_kept.sem, tail.u_kept.at(i, g))
                    for m in range(4):
                        h = 4 * g + m
                        last = pe.matmul(u_bank[32 * m:32 * m + 32, block_columns(j, h)], ve[:, h, j, :], probs[:, p % 2, n, m, :],
                                         start=(j == 0), stop=(j == BLOCKS - 1), skip_group_check=True)
                    if n == 1:
                        last.then_inc(exp_read.sem, 1)
                    elif j == BLOCKS - 1:
                        last.then_inc(half_quad.sem, 1)

            def transposed(i, half):
                for p in range(NB + 1):
                    if p < NB:
                        if p >= 2:
                            pe.wait_ge(exp_done.sem, exp_done.at(i, p - 1))
                        for n in range(2):
                            g, j = (2 * p + n) // BLOCKS, (2 * p + n) % BLOCKS
                            pe.matmul(pair[p % 2][:, n, :, :], k["ident16"][:, :], k["causal_t"][:, :], start=True, stop=False,
                                      skip_group_check=True)
                            for m in range(4):
                                h = 4 * g + m
                                c = block_columns(j, h)
                                last = pe.matmul(pair[p % 2][:, n, m, :], stacks.kk[0:ROWS, half, h, c],
                                                 stacks.q[0:ROWS, half, h, c], start=False, stop=True, skip_group_check=True)
                        last.then_inc(t_done.sem, 1)
                    if p >= 1:
                        weighted(i, p - 1)
                        g, j = (2 * p - 1) // BLOCKS, (2 * p - 1) % BLOCKS
                        if j in (0, BLOCKS - 1) and (2 * p - 1) >= BLOCKS - 1:
                            tail.tensor_denominators(pe, i, g if j == BLOCKS - 1 else g - 1)

            pe.wait_ge(stacks.edges.sem, 1)
            with pe.Fori(0, B // 2) as two:
                i2 = two * 2
                for half in range(2):
                    i = i2 + half
                    values(i)
                    stacks.wait_loaded(pe, i2, half)
                    maxima(i, half)
                    turn_maxima(i)
                    pe.wait_ge(m_row[half].sem, i2 * 8 + 16)
                    transposed(i, half)
                    tail.tensor_out(pe, i)

        @block.scalar
        def _(act):
            def keep(i, g):
                if g % 2 == 0:
                    tail.scalar_keep(act, i, g, half_quad, g // 2 + 1)
                else:
                    tail.scalar_keep(act, i, g, exp_read, BLOCKS * (g + 1) // 2)

            norm.start(act)
            with act.Fori(0, B) as i:
                act.wait_ge(m_turned.sem, m_turned.at(i, 1))
                act.copy(mrow[:, 0, :], banks[0][0:H, :]).then_inc(m_first.sem, 1)
                for p in range(NB):
                    act.wait_ge(t_done.sem, t_done.at(i, p + 1))
                    if p >= 2:
                        act.wait_ge(exp_read.sem, exp_read.at(i, p - 1))
                    act.activation(probs[:, p % 2, :, :, :], pair[p % 2][:, :, :, :], ACT.Exp).then_inc(exp_done.sem, 1)
                    for g in range(QUADS - 1):
                        last_unit = BLOCKS * (g + 1) - 1
                        if last_unit // 2 + 1 == p:
                            keep(i, g)
                keep(i, QUADS - 1)
                norm.scalar(act, i, (u_bank, misc))

        @block.vector
        def _(dve):
            chain = chain_sem
            chain.eng = dve
            stacks.set_edges(dve, chain)
            for n in range(4):
                chain.do(dve.memset(ve[:, 4 * n:4 * n + 4, :, DH:2 * DH], 1.0))
            chain.link(dve.memset(mx[:, :, :], MASKED))
            done_before = chain.n
            chain.per = Norm.CHAIN
            with dve.Fori(0, B) as i:
                for s in range(TILES):
                    bank = (misc, u_bank)[s % 2]
                    dve.wait_ge(v_done.sem, v_done.at(i, s + 1))
                    bh = bv[:, :].rearrange("p (h d) -> p h d", d=DH)
                    for j, first, step, at in ((s, 0, 1, 0), (4 + s // 2, s % 2, 2, D), (6, s, 4, D + D // 2)):
                        v = bank[:, at:at + D // step].rearrange("p (h d) -> p h d", d=DH)
                        last = dve.tensor_tensor(ve[:, first::step, j, 0:DH], v, bh[:, first::step, :], ALU.add)
                    last.then_inc(v_kept.sem, 1)
                for u in range(NA):
                    j, g = u // QUADS, u % QUADS
                    dve.wait_ge(s_done.sem, s_done.at(i, u + 1))
                    s = banks[u % 2][:, :].rearrange("p (n c) -> p n c", n=4)
                    step = 1 if j < 4 else (2 if j < 6 else 4)
                    for first in range(step):
                        h = 4 * g + first
                        last = dve.tensor_reduce(mx[:, max_slot(j, h), h:4 * g + 4:step], s[:, first::step, :], AX.X, ALU.max)
                    last.then_inc(s_max.sem, 1)
                dve.wait_ge(m_first.sem, m_first.at(i, 1))
                dve.wait_ge(m_turned.sem, m_turned.at(i, 2))
                dve.tensor_tensor(mrow[:, 1, :], banks[1][0:H, :], mrow[:, 0, :], ALU.max).then_inc(m_best.sem, 1)
                dve.wait_ge(m_best.sem, m_best.at(i, 1))
                dve.wait_ge(m_turned.sem, m_turned.at(i, 3))
                dve.tensor_tensor(mt[:, :], misc[0:H, :], mrow[:, 1, :], ALU.max).then_inc(m_best.sem, 1)
                for g in range(QUADS):
                    tail.vector_divide(dve, i, g)
                chain.base = done_before
                chain.start(i)
                tail.vector_out(dve, chain, i)
                chain.end()


def merged_weights(nc, k, w):
    with Stage(nc) as ctx:
        caT = ctx.enter_context(nc.sbuf_tensor("w_caT", [P, 3 * KD, D], F32))
        second = ctx.enter_context(nc.sbuf_tensor("w_second", [P, 3, KD, D], F32))
        ca_b = ctx.enter_context(nc.sbuf_tensor("w_ca_b", [P, 3 * KD], F32))
        qk_b = ctx.enter_context(nc.sbuf_tensor("w_qk_b", [P, 2 * KD], F32))
        v_b = ctx.enter_context(nc.sbuf_tensor("w_v_b", [P, D], F32))
        vb_wide = ctx.enter_context(nc.sbuf_tensor("w_vb_wide", [P, KD, P], F32))
        zeros = ctx.enter_context(nc.sbuf_tensor("w_zeros", [P, P], F32))
        ps = [ctx.enter_context(nc.psum_tensor(f"w_ps{n}", [P, SEQ], F32)) for n in range(6)]
        psb = ctx.enter_context(nc.psum_tensor("w_psb", [P, SEQ], F32))
        psv = ctx.enter_context(nc.psum_tensor("w_psv", [P, SEQ], F32))
        loaded = ctx.semaphore("w_loaded")
        late = ctx.semaphore("w_late")
        consts = ctx.semaphore("w_consts")
        made = ctx.semaphore("w_made")
        wide = ctx.semaphore("w_wide")
        zero = ctx.semaphore("w_zero")
        block = ctx.enter_context(nc.Block())

        @block.sync
        def _(sp):
            sp.dma_start(caT[:, :, :], w["c_attn_wT"]).then_inc(loaded, 16)
            sp.dma_start(second[:, :, :, :], w["qkv_w"]).then_inc(loaded, 16)
            sp.dma_start(ca_b[:, :], w["c_attn_b"]).then_inc(loaded, 16)
            sp.dma_start(qk_b[:, :], w["qk_b"]).then_inc(loaded, 16)
            sp.dma_start(v_b[:, :], w["v_b"]).then_inc(loaded, 16)
            sp.dma_start(k["wo0"][:, :, :], w["wo0"]).then_inc(late, 16)
            sp.dma_start(k["xT"][:, :, :], w["xT"]).then_inc(late, 16)
            sp.dma_start(k["x"][:, :, :], w["x"]).then_inc(late, 16)
            sp.dma_start(k["ctxT"][:, :, :], w["ctxT"]).then_inc(late, 16)
            sp.wait_ge(late, 64)

        @block.gpsimd
        def _(pool):
            n = 0
            for t, val in ((k["ident"], 0.0), (k["ident16"], 0.0), (k["causal"], 0.0), (k["causal_t"], 0.0),
                           (k["spread"], 0.0), (k["minus_half"], -0.5), (k["ones"], 1.0)):
                pool.memset(t[:, :], val).then_inc(consts, 1)
                n += 1
            pool.wait_ge(consts, n)
            for t in (k["ident"], k["ident16"]):
                pool.affine_select(out=t[:, :], in_=t[:, :], compare_op=ALU.not_equal, fill=1.0, base=0,
                                   pattern=[[-1, P]], channel_multiplier=1).then_inc(consts, 1)
            c = k["causal"][:, :].rearrange("p (n c) -> p n c", n=4)
            pool.affine_select(out=c, in_=c, compare_op=ALU.is_ge, fill=MASKED, base=0, pattern=[[0, 4], [-1, P]],
                               channel_multiplier=1).then_inc(consts, 1)
            c = k["causal_t"][:, :].rearrange("p (n c) -> p n c", n=4)
            pool.affine_select(out=c, in_=c, compare_op=ALU.is_ge, fill=MASKED, base=0, pattern=[[0, 4], [1, P]],
                               channel_multiplier=-1).then_inc(consts, 1)
            c = k["spread"][:, :].rearrange("p (n c) -> p n c", n=4)
            pool.affine_select(out=c, in_=c, compare_op=ALU.not_equal, fill=1.0, base=-DH, pattern=[[-2 * DH, 4], [0, 2 * DH]],
                               channel_multiplier=1).then_inc(consts, 1)
            pool.wait_ge(consts, n + 5)

        @block.tensor
        def _(pe):
            pe.wait_ge(loaded, 80)
            for m in range(3):
                for it in range(KD):
                    for c in range(KD):
                        last = pe.matmul(ps[2 * m + it][:, 0:D], caT[:, KD * m + c, it * P:(it + 1) * P], second[:, m, c, :],
                                         start=(c == 0), stop=(c == KD - 1))
                    last.then_inc(made, 1)
            for j in range(2 * KD):
                m, mt = j // KD, j % KD
                for c in range(KD):
                    last = pe.matmul(psb[:, j:j + 1], second[:, m, c, mt * P:(mt + 1) * P], ca_b[:, KD * m + c:KD * m + c + 1],
                                     start=(c == 0), stop=(c == KD - 1))
            last.then_inc(made, 1)
            pe.wait_ge(wide, KD)
            for c in range(KD):
                last = pe.matmul(psv[:, 0:D], vb_wide[:, c, :], second[:, 2, c, :], start=(c == 0), stop=(c == KD - 1))
            last.then_inc(made, 1)

        @block.vector
        def _(dve):
            dve.memset(zeros[:, :], 0.0).then_inc(zero, 1)
            dve.wait_ge(zero, 1)
            dve.wait_ge(loaded, 80)
            for c in range(KD):
                dve.tensor_scalar(vb_wide[:, c, :], zeros[:, :], ca_b[:, 2 * KD + c:2 * KD + c + 1], None, ALU.add).then_inc(wide, 1)
            for m, name in enumerate(("wq0", "wk0", "wv0")):
                for it in range(KD):
                    dve.wait_ge(made, 2 * m + it + 1)
                    dve.tensor_scalar(k[name][:, it, :], ps[2 * m + it][:, 0:D], DH ** -0.5 if m == 0 else 1.0, None, ALU.mult)
            dve.wait_ge(made, 7)
            dve.tensor_tensor(k["qk_bias0"][:, :], psb[:, 0:2 * KD], qk_b[:, :], ALU.add).then_inc(zero, 1)
            dve.wait_ge(zero, 2)
            dve.tensor_scalar(k["qk_bias0"][:, 0:KD], k["qk_bias0"][:, 0:KD], DH ** -0.5, None, ALU.mult)
            dve.wait_ge(made, 8)
            dve.tensor_tensor(k["v_bias0"][:, :], psv[:, 0:D], v_b[:, :], ALU.add)


def two_way_attention(nc, k, w, q_dram, k_dram):
    with Stage(nc) as ctx:
        def sb(name, shape, dt=F32):
            return ctx.enter_context(nc.sbuf_tensor(f"x_{name}", shape, dt))

        def sig(name, per):
            return Signal(ctx, nc, f"x_{name}", per)

        xb = sb("xb", [P, KD, SEQ])
        ctxb = sb("ctxb", [P, 2, TILES, D])
        cw = sb("cw", [P, KD, SEQ])
        w_vec = sb("w_vec", [P, 3, KD])
        w_l = sb("w_l", [P, 4, KD, D])
        b_l = sb("b_l", [1, D])
        b_s = sb("b_s", [P, 3])
        b_sum = sb("b_sum", [P, 2])
        w14 = sb("w14", [P, KD, D])
        probs = sb("probs", [P, TILES, SEQ])
        probs_t = sb("probs_t", [P, TILES, SEQ])
        c2q = sb("c2q", [P, KD, SEQ])
        cc = sb("cc", [P, KD, SEQ])
        neg_max = sb("neg_max", [P, TILES])
        zs = sb("zs", [P, TILES])
        rz = sb("rz", [P, TILES])
        v = sb("v", [P, TILES])
        e = sb("e", [P, TILES])
        neg_top = sb("neg_top", [1, 1])
        neg_top_all = sb("neg_top_all", [P, 1])
        e_sum = sb("e_sum", [P, 1])
        r_sum = sb("r_sum", [P, 1])
        row = sb("row", [1, D])
        q2c = sb("q2c", [P, KD])
        bank = [ctx.enter_context(nc.psum_tensor(f"x_bank{n}", [P, SEQ], F32)) for n in range(8)]
        norm = Norm(ctx, nc, k, "x")
        xb_ready, cw_ready = sig("xb_ready", 1), sig("cw_ready", KD)
        loaded = [sig(f"ctx_loaded{n}", 16) for n in range(2)]
        weights = ctx.semaphore("x_weights")
        s_done, cwc_done, neg_ready = sig("s_done", TILES), sig("cwc_done", 1), sig("neg_ready", TILES)
        p_done, p_normed = sig("p_done", TILES), sig("p_normed", TILES)
        t_done, t_kept = sig("t_done", TILES), sig("t_kept", TILES)
        c_done, c_kept, cc_ready = sig("c_done", KD), sig("c_kept", KD), sig("cc_ready", KD)
        v_ready, v_row, top_ready, top_wide, top_kept = (sig(n, 1) for n in ("v_ready", "v_row", "top_ready", "top_wide", "top_kept"))
        e_done, sums_done, row_kept, col_done, w14_ready = (sig(n, 1) for n in ("e_done", "sums_done", "row_kept", "col_done", "w14_ready"))
        out_ready = sig("out_ready", TILES)
        chain = Chain(ctx, nc, "x_chain")
        block = ctx.enter_context(nc.Block())

        @block.sync
        def _(sp):
            sp.dma_start(w_vec[:, :, :], w["xa_vec"]).then_inc(weights, 16)
            sp.dma_start(w_l[:, :, :, :], w["xa_wl"]).then_inc(weights, 16)
            sp.dma_start(b_l[:, :], w["xa_bl"]).then_inc(weights, 16)
            sp.dma_start(b_s[:, :], w["xa_bs"]).then_inc(weights, 16)
            with sp.Fori(0, B // 2) as two:
                for half in range(2):
                    i = two * 2 + half
                    norm.wait_finished(sp, i, 2)
                    sp.dma_start(ctxb[:, half, :, :], w["ctx"][:, bass.ds(i * TILES, TILES), :]).then_inc(loaded[half].sem, 16)

        @block.gpsimd
        def _(pool):
            with pool.Fori(0, B) as i:
                pool.tensor_copy(xb[:, :, :], k["xT"][:, :, batch_cols(i)]).then_inc(xb_ready.sem, 1)
                norm.pool(pool, i)

        @block.tensor
        def _(pe):
            pe.wait_ge(weights, 64)
            with pe.Fori(0, B // 2) as two:
                for half in range(2):
                    i = two * 2 + half
                    norm.wait_finished(pe, i, 1)
                    pe.wait_ge(cw_ready.sem, cw_ready.at(i, KD))
                    for t in range(TILES):
                        for c in range(KD):
                            last = pe.matmul(bank[t][:, :], cw[:, c, t * P:(t + 1) * P], k["ctxT"][:, c, batch_cols(i)],
                                             start=(c == 0), stop=(c == KD - 1))
                        last.then_inc(s_done.sem, 1)
                    pe.wait_ge(xb_ready.sem, xb_ready.at(i, 1))
                    for t in range(TILES):
                        for c in range(KD):
                            last = pe.matmul(bank[7][:, t:t + 1], xb[:, c, t * P:(t + 1) * P], w_vec[:, 2, c:c + 1],
                                             start=(c == 0), stop=(c == KD - 1))
                    last.then_inc(cwc_done.sem, 1)
                    for qt in range(TILES):
                        if qt >= 2:
                            pe.wait_ge(t_kept.sem, t_kept.at(i, qt - 1))
                        for t in range(TILES):
                            pe.wait_ge(p_normed.sem, p_normed.at(i, t + 1))
                            last = pe.transpose(bank[4 + qt % 2][:, t * P:(t + 1) * P], probs[:, t, qt * P:(qt + 1) * P], k["ident"][:, :])
                        last.then_inc(t_done.sem, 1)
                    pe.wait_ge(v_ready.sem, v_ready.at(i, 1))
                    for t in range(TILES):
                        last = pe.matmul(bank[6][0:1, t * P:(t + 1) * P], v[:, t:t + 1], k["ident"][:, :], start=True, stop=True)
                    last.then_inc(v_row.sem, 1)
                    pe.wait_ge(loaded[half].sem, two * 16 + 16)
                    for m in range(KD):
                        for qt in range(TILES):
                            pe.wait_ge(t_kept.sem, t_kept.at(i, qt + 1))
                            last = pe.matmul(bank[m][:, :], ctxb[:, half, qt, m * P:(m + 1) * P], probs_t[:, qt, :],
                                             start=(qt == 0), stop=(qt == TILES - 1))
                        last.then_inc(c_done.sem, 1)
                        if m == 0:
                            pe.wait_ge(top_ready.sem, top_ready.at(i, 1))
                            pe.matmul(bank[7][:, 8:9], k["ones"][0:1, :], neg_top[:, :], start=True, stop=True).then_inc(top_wide.sem, 1)
                    pe.wait_ge(e_done.sem, e_done.at(i, 1))
                    pe.matmul(bank[7][:, 9:10], k["ones"][:, :], e_sum[:, :], start=True, stop=True)
                    for t in range(TILES):
                        last = pe.matmul(bank[6][0:1, 0:D], e[:, t:t + 1], k["x"][:, bass.ds(i * TILES + t, 1), :].rearrange("p a d -> p (a d)"),
                                         start=(t == 0), stop=(t == TILES - 1))
                    last.then_inc(sums_done.sem, 1)
                    pe.wait_ge(row_kept.sem, row_kept.at(i, 1))
                    for c in range(KD):
                        last = pe.matmul(bank[7][:, 10 + c:11 + c], row[:, c * P:(c + 1) * P], k["ones"][0:1, 0:1], start=True, stop=True)
                    last.then_inc(col_done.sem, 1)
                    for t in range(TILES):
                        out = bank[2 + t % 2][:, 0:D]
                        tok = slice(t * P, (t + 1) * P)
                        if t >= 2:
                            pe.wait_ge(norm.summed.sem, norm.summed.at(i, t - 1))
                        pe.matmul(out, k["ones"][0:1, :], b_l[:, :], start=True, stop=False)
                        for c in range(KD):
                            pe.wait_ge(c_kept.sem, c_kept.at(i, KD))
                            pe.matmul(out, c2q[:, c, tok], w_l[:, 1, c, :], start=False, stop=False)
                        for c in range(KD):
                            pe.wait_ge(cc_ready.sem, cc_ready.at(i, KD))
                            pe.matmul(out, cc[:, c, tok], w_l[:, 2, c, :], start=False, stop=False)
                        pe.wait_ge(w14_ready.sem, w14_ready.at(i, 1))
                        for c in range(KD):
                            last = pe.matmul(out, xb[:, c, tok], w14[:, c, :], start=False, stop=(c == KD - 1))
                        last.then_inc(out_ready.sem, 1)
                    norm.tensor(pe, i, (bank[4], bank[5]))

        @block.scalar
        def _(act):
            norm.start(act)
            with act.Fori(0, B) as i:
                for t in range(TILES):
                    act.wait_ge(neg_ready.sem, neg_ready.at(i, t + 1))
                    act.activation(probs[:, t, :], bank[t][:, :], ACT.Exp, bias=neg_max[:, t:t + 1],
                                   accum_out=zs[:, t:t + 1]).then_inc(p_done.sem, 1)
                for qt in range(TILES):
                    act.wait_ge(t_done.sem, t_done.at(i, qt + 1))
                    act.copy(probs_t[:, qt, :], bank[4 + qt % 2][:, :]).then_inc(t_kept.sem, 1)
                act.wait_ge(top_kept.sem, top_kept.at(i, 1))
                act.activation(e[:, :], v[:, :], ACT.Exp, bias=neg_top_all[:, 0:1], accum_out=e_sum[:, :]).then_inc(e_done.sem, 1)
                for m in range(KD):
                    act.wait_ge(c_done.sem, c_done.at(i, m + 1))
                    act.copy(c2q[:, m, :], bank[m][:, :]).then_inc(c_kept.sem, 1)
                norm.scalar(act, i, (bank[4], bank[5]))

        @block.vector
        def _(dve):
            chain.eng = dve
            dve.wait_ge(weights, 64)
            chain.link(dve.tensor_tensor(b_sum[:, 0:1], b_s[:, 0:1], b_s[:, 1:2], ALU.add))
            chain.link(dve.tensor_tensor(b_sum[:, 1:2], b_sum[:, 0:1], b_s[:, 2:3], ALU.add))
            chain.base, chain.per = chain.n, Norm.CHAIN + TILES + 3
            with dve.Fori(0, B) as i:
                chain.start(i)
                for c in range(KD):
                    dve.tensor_scalar(cw[:, c, :], k["xT"][:, c, batch_cols(i)], w_vec[:, 0, c:c + 1], w_vec[:, 1, c:c + 1],
                                      ALU.mult, ALU.add).then_inc(cw_ready.sem, 1)
                for t in range(TILES):
                    dve.wait_ge(s_done.sem, s_done.at(i, t + 1))
                    dve.tensor_reduce(neg_max[:, t:t + 1], bank[t][:, :], AX.X, ALU.max, negate=True).then_inc(neg_ready.sem, 1)
                for t in range(TILES):
                    dve.wait_ge(p_done.sem, p_done.at(i, t + 1))
                    chain.link(dve.reciprocal(rz[:, t:t + 1], zs[:, t:t + 1]))
                    dve.tensor_scalar(probs[:, t, :], probs[:, t, :], rz[:, t:t + 1], None, ALU.mult).then_inc(p_normed.sem, 1)
                dve.wait_ge(cwc_done.sem, cwc_done.at(i, 1))
                dve.scalar_tensor_tensor(v[:, :], bank[7][:, 0:TILES], b_sum[:, 1:2], neg_max[:, :], ALU.add,
                                         ALU.subtract).then_inc(v_ready.sem, 1)
                dve.wait_ge(v_row.sem, v_row.at(i, 1))
                dve.tensor_reduce(neg_top[:, :], bank[6][0:1, :], AX.X, ALU.max, negate=True).then_inc(top_ready.sem, 1)
                dve.wait_ge(top_wide.sem, top_wide.at(i, 1))
                dve.tensor_copy(neg_top_all[:, :], bank[7][:, 8:9]).then_inc(top_kept.sem, 1)
                for m in range(KD):
                    dve.wait_ge(c_kept.sem, c_kept.at(i, m + 1))
                    dve.wait_ge(xb_ready.sem, xb_ready.at(i, 1))
                    dve.tensor_tensor(cc[:, m, :], c2q[:, m, :], xb[:, m, :], ALU.mult).then_inc(cc_ready.sem, 1)
                dve.wait_ge(sums_done.sem, sums_done.at(i, 1))
                chain.link(dve.reciprocal(r_sum[:, :], bank[7][:, 9:10]))
                dve.tensor_copy(row[:, :], bank[6][0:1, 0:D]).then_inc(row_kept.sem, 1)
                dve.wait_ge(col_done.sem, col_done.at(i, 1))
                chain.link(dve.tensor_scalar(q2c[:, :], bank[7][:, 10:10 + KD], r_sum[:, 0:1], None, ALU.mult))
                for c in range(KD):
                    ins = dve.scalar_tensor_tensor(w14[:, c, :], w_l[:, 3, c, :], q2c[:, c:c + 1], w_l[:, 0, c, :], ALU.mult, ALU.add)
                    if c < KD - 1:
                        chain.do(ins)
                    else:
                        ins.then_inc(w14_ready.sem, 1)
                for t in range(TILES):
                    dve.wait_ge(out_ready.sem, out_ready.at(i, t + 1))
                    norm.add_tile(dve, chain, i, t, bank[2 + t % 2][:, 0:D])
                norm.vector_end(dve, chain, i)
                chain.end()


EXPERTS, HID = 8, 1024
HC = HID // P
W_IN = KD * HID
W_ALL = W_IN + HC * D
ALL_TILES = B * TILES


def gates(nc, k, w, comb, xh, xl):
    with Stage(nc) as ctx:
        def sb(name, shape, dt=F32):
            return ctx.enter_context(nc.sbuf_tensor(f"g_{name}", shape, dt))

        wg = sb("wg", [P, KD, EXPERTS])
        b_out = sb("b_out", [EXPERTS, D])
        logits = sb("logits", [P, ALL_TILES, EXPERTS])
        above = sb("above", [P, ALL_TILES, EXPERTS, EXPERTS])
        equal = sb("equal", [P, ALL_TILES, EXPERTS, EXPERTS])
        before = sb("before", [P, EXPERTS, EXPERTS])
        rank = sb("rank", [P, ALL_TILES, EXPERTS])
        first = sb("first", [P, ALL_TILES, EXPERTS])
        second = sb("second", [P, ALL_TILES, EXPERTS])
        tmp = sb("tmp", [P, ALL_TILES, EXPERTS])
        tops = sb("tops", [P, 2, ALL_TILES])
        gap = sb("gap", [P, ALL_TILES])
        ex = sb("ex", [P, ALL_TILES])
        den = sb("den", [P, ALL_TILES])
        share = sb("share", [P, 2, ALL_TILES])
        comb_t = sb("comb_t", [EXPERTS, B * SEQ])
        bank = [ctx.enter_context(nc.psum_tensor(f"g_bank{n}", [P, SEQ], F32)) for n in range(8)]
        loaded = ctx.semaphore("g_loaded")
        logits_done = ctx.semaphore("g_logits_done")
        ex_done = ctx.semaphore("g_ex_done")
        before_ready = ctx.semaphore("g_before")
        turned = ctx.semaphore("g_turned")
        kept = ctx.semaphore("g_kept")
        bias_done = ctx.semaphore("g_bias_done")
        added = ctx.semaphore("g_added")
        gap_ready = ctx.semaphore("g_gap_ready")
        comb_ready = ctx.semaphore("g_comb_ready")
        x_high = ctx.semaphore("g_x_high")
        chain = Chain(ctx, nc, "g_chain")
        block = ctx.enter_context(nc.Block())

        @block.sync
        def _(sp):
            sp.dma_start(wg[:, :, :], w["w_gate"]).then_inc(loaded, 16)
            sp.dma_start(b_out[:, :], w["moe_b_out"]).then_inc(loaded, 16)

        @block.gpsimd
        def _(pool):
            pool.memset(before[:, :, :], 0.0).then_inc(before_ready, 1)
            pool.wait_ge(before_ready, 1)
            pool.affine_select(out=before[:, :, :], in_=before[:, :, :], compare_op=ALU.is_ge, fill=1.0, base=0,
                               pattern=[[-1, EXPERTS], [1, EXPERTS]], channel_multiplier=0).then_inc(before_ready, 1)

        @block.tensor
        def _(pe):
            pe.wait_ge(loaded, 32)
            for t in range(ALL_TILES):
                for c in range(KD):
                    last = pe.matmul(bank[0][:, t * EXPERTS:(t + 1) * EXPERTS], k["xT"][:, c, t * P:(t + 1) * P], wg[:, c, :],
                                     start=(c == 0), stop=(c == KD - 1))
            last.then_inc(logits_done, 1)
            pe.wait_ge(comb_ready, 1)
            for b in range(B):
                for t in range(TILES):
                    last = pe.transpose(bank[1 + b][0:EXPERTS, t * P:(t + 1) * P], comb[:, b * TILES + t, :], k["ident"][:, :])
                last.then_inc(turned, 1)
            for t in range(ALL_TILES):
                pe.wait_ge(kept, t // TILES + 1)
                if t >= 2:
                    pe.wait_ge(added, t - 1)
                pe.matmul(bank[6 + t % 2][:, 0:D], comb_t[:, t * P:(t + 1) * P], b_out[:, :], start=True, stop=True).then_inc(bias_done, 1)

        @block.scalar
        def _(act):
            act.copy(xh[:, :, :], k["xT"][:, :, :]).then_inc(x_high, 1)
            act.wait_ge(gap_ready, 1)
            act.activation(ex[:, :], gap[:, :], ACT.Exp).then_inc(ex_done, 1)
            for b in range(B):
                act.wait_ge(turned, b + 1)
                act.copy(comb_t[:, b * SEQ:(b + 1) * SEQ], bank[1 + b][0:EXPERTS, :]).then_inc(kept, 1)

        @block.vector
        def _(dve):
            chain.eng = dve
            dve.wait_ge(logits_done, 1)
            chain.link(dve.tensor_copy(logits[:, :, :].rearrange("p t e -> p (t e)"), bank[0][:, 0:ALL_TILES * EXPERTS]))
            wide = [P, ALL_TILES, EXPERTS, EXPERTS]
            other = logits[:, :, :].unsqueeze(2).broadcast_to(wide)
            own = logits[:, :, :].unsqueeze(3).broadcast_to(wide)
            chain.do(dve.tensor_tensor(above[:, :, :, :], other, own, ALU.is_gt))
            chain.link(dve.tensor_tensor(equal[:, :, :, :], other, own, ALU.is_equal))
            dve.wait_ge(before_ready, 2)
            chain.link(dve.tensor_tensor(equal[:, :, :, :], equal[:, :, :, :], before[:, :, :].unsqueeze(1).broadcast_to(wide), ALU.mult))
            chain.link(dve.tensor_tensor(above[:, :, :, :], above[:, :, :, :], equal[:, :, :, :], ALU.add))
            chain.link(dve.tensor_reduce(rank[:, :, :], above[:, :, :, :], AX.X, ALU.add))
            for n, pick in enumerate((first, second)):
                chain.link(dve.tensor_scalar(pick[:, :, :], rank[:, :, :], float(n), None, ALU.is_equal))
                chain.link(dve.tensor_tensor(tmp[:, :, :], pick[:, :, :], logits[:, :, :], ALU.mult))
                chain.link(dve.tensor_reduce(tops[:, n, :], tmp[:, :, :], AX.X, ALU.add))
            dve.tensor_tensor(gap[:, :], tops[:, 1, :], tops[:, 0, :], ALU.subtract).then_inc(gap_ready, 1)
            dve.wait_ge(x_high, 1)
            chain.do(dve.tensor_tensor(xl[:, :, :], k["xT"][:, :, :], xh[:, :, :], ALU.subtract))
            dve.wait_ge(ex_done, 1)
            chain.link(dve.tensor_scalar(den[:, :], ex[:, :], 1.0, None, ALU.add))
            chain.link(dve.reciprocal(share[:, 0, :], den[:, :]))
            chain.link(dve.tensor_tensor(share[:, 1, :], ex[:, :], share[:, 0, :], ALU.mult))
            each = [P, ALL_TILES, EXPERTS]
            chain.do(dve.tensor_tensor(first[:, :, :], first[:, :, :], share[:, 0, :].unsqueeze(2).broadcast_to(each), ALU.mult))
            chain.link(dve.tensor_tensor(second[:, :, :], second[:, :, :], share[:, 1, :].unsqueeze(2).broadcast_to(each), ALU.mult))
            dve.tensor_tensor(comb[:, :, :], first[:, :, :], second[:, :, :], ALU.add).then_inc(comb_ready, 1)
            for t in range(ALL_TILES):
                dve.wait_ge(bias_done, t + 1)
                dve.tensor_tensor(k["x"][:, t, :], bank[6 + t % 2][:, 0:D], k["x"][:, t, :], ALU.add).then_inc(added, 1)


def experts(nc, k, w, comb, xh, xl):
    with Stage(nc) as ctx:
        def sb(name, shape, dt=F32):
            return ctx.enter_context(nc.sbuf_tensor(f"e_{name}", shape, dt))

        def sig(name, per):
            return Signal(ctx, nc, f"e_{name}", per)

        raw = sb("raw", [P, 2, W_ALL])
        wh = sb("wh", [P, 2, W_ALL], F16)
        wl = sb("wl", [P, 2, W_ALL], F16)
        b_in = sb("b_in", [P, EXPERTS * HC])
        hf = sb("hf", [P, 4, SEQ])
        hh = sb("hh", [P, HC, SEQ], F16)
        hl = sb("hl", [P, HC, SEQ], F16)
        hb = [ctx.enter_context(nc.psum_tensor(f"e_h{n}", [P, SEQ], F32)) for n in range(4)]
        yb = [ctx.enter_context(nc.psum_tensor(f"e_y{n}", [P, SEQ], F32)) for n in range(4)]
        b_loaded = ctx.semaphore("e_b_loaded")
        loaded = [sig(f"loaded{n}", 16) for n in range(2)]
        w_high, w_low = sig("w_high", 1), sig("w_low", 1)
        h_done = sig("h_done", HC)
        gelu_done, h_high, h_low = sig("gelu_done", HC), sig("h_high", HC), sig("h_low", HC)
        y_done = sig("y_done", 1)
        y_added = sig("y_added", TILES)
        block = ctx.enter_context(nc.Block())

        @block.sync
        def _(sp):
            sp.dma_start(b_in[:, :], w["moe_b_in"]).then_inc(b_loaded, 16)
            with sp.Fori(0, EXPERTS // 2) as two:
                for half in range(2):
                    e = two * 2 + half
                    sp.wait_ge(w_low.sem, e + 1)
                    sp.dma_start(raw[:, half, :], w["moe_w"][bass.ds(e, 1)].rearrange("e p n -> (e p) n")).then_inc(loaded[half].sem, 16)

        @block.gpsimd
        def _(pool):
            pool.sem_inc(w_low.sem, 2)
            with pool.Fori(0, EXPERTS // 2) as two:
                for half in range(2):
                    e = two * 2 + half
                    pool.wait_ge(loaded[half].sem, two * 16 + 16)
                    wait_first(pool, y_done.sem, e * B + B, k["passed"])
                    pool.tensor_copy(wh[:, half, :], raw[:, half, :]).then_inc(w_high.sem, 1)
                    pool.wait_ge(w_high.sem, e + 1)
                    pool.tensor_tensor(wl[:, half, :], raw[:, half, :], wh[:, half, :], ALU.subtract).then_inc(w_low.sem, 1)

        @block.tensor
        def _(pe):
            def up(turn, half, b, hc):
                pe.wait_ge(gelu_done.sem, gelu_done.at(turn, hc + 5))
                first = True
                for ws, xs in ((wh, xh), (wh, xl), (wl, xh)):
                    for c in range(KD):
                        at = c * HID + hc * P
                        last = pe.matmul(hb[hc % 4][:, :], ws[:, half, at:at + P], xs[:, c, batch_cols(b)], start=first,
                                         stop=(ws is wl and c == KD - 1))
                        first = False
                last.then_inc(h_done.sem, 1)

            def down(turn, half, hc):
                if hc == 0:
                    pe.wait_ge(y_added.sem, y_added.at(turn, TILES))
                pe.wait_ge(h_low.sem, h_low.at(turn, HC + hc + 1))
                at = W_IN + hc * D
                for t in range(TILES):
                    tok = slice(t * P, (t + 1) * P)
                    for hs, ws in ((hh, wh), (hl, wh), (hh, wl)):
                        last = pe.matmul(yb[t][:, 0:D], hs[:, hc, tok], ws[:, half, at:at + D],
                                         start=(hc == 0 and hs is hh and ws is wh), stop=(hc == HC - 1 and ws is wl))
                if hc == HC - 1:
                    last.then_inc(y_done.sem, 1)

            with pe.Fori(0, EXPERTS // 2) as two:
                for half in range(2):
                    e = two * 2 + half
                    with pe.Fori(0, B) as b:
                        turn = e * B + b
                        pe.wait_ge(w_low.sem, e + 3)
                        for hc in range(HC + 2):
                            if hc < HC:
                                up(turn, half, b, hc)
                            if hc >= 2:
                                down(turn, half, hc - 2)

        @block.scalar
        def _(act):
            act.sem_inc(gelu_done.sem, HC)
            act.wait_ge(b_loaded, 16)
            with act.Fori(0, EXPERTS) as e:
                with act.Fori(0, B) as b:
                    turn = e * B + b
                    for hc in range(HC):
                        act.wait_ge(h_done.sem, h_done.at(turn, hc + 1))
                        act.wait_ge(h_low.sem, h_low.at(turn, hc + 5))
                        act.activation(hf[:, hc % 4, :], hb[hc % 4][:, :], ACT.Gelu,
                                       bias=b_in[:, bass.ds(e * HC + hc, 1)]).then_inc(gelu_done.sem, 1)

        @block.vector
        def _(dve):
            dve.sem_inc(h_low.sem, HC)
            dve.sem_inc(y_done.sem, 2 * B)
            dve.sem_inc(y_added.sem, TILES)
            with dve.Fori(0, EXPERTS) as e:
                with dve.Fori(0, B) as b:
                    turn = e * B + b
                    for hc in range(HC):
                        dve.wait_ge(gelu_done.sem, gelu_done.at(turn, HC + hc + 1))
                        dve.tensor_copy(hh[:, hc, :], hf[:, hc % 4, :]).then_inc(h_high.sem, 1)
                        dve.wait_ge(h_high.sem, h_high.at(turn, hc + 1))
                        dve.tensor_tensor(hl[:, hc, :], hf[:, hc % 4, :], hh[:, hc, :], ALU.subtract).then_inc(h_low.sem, 1)
                    dve.wait_ge(y_done.sem, turn + 2 * B + 1)
                    for t in range(TILES):
                        x = k["x"][:, bass.ds(b * TILES + t, 1), :].rearrange("p a d -> p (a d)")
                        share = comb[:, bass.ds(b * TILES + t, 1), bass.ds(e, 1)].rearrange("p a e -> p (a e)")
                        dve.scalar_tensor_tensor(x, yb[t][:, 0:D], share, x, ALU.mult, ALU.add).then_inc(y_added.sem, 1)


def norm_only(nc, k, tag):
    with Stage(nc) as ctx:
        norm = Norm(ctx, nc, k, tag)
        banks = [ctx.enter_context(nc.psum_tensor(f"{tag}_bank{n}", [P, SEQ], F32)) for n in range(KD)]
        chain = Chain(ctx, nc, f"{tag}_chain")
        block = ctx.enter_context(nc.Block())

        @block.gpsimd
        def _(pool):
            with pool.Fori(0, B) as i:
                norm.pool(pool, i)

        @block.tensor
        def _(pe):
            with pe.Fori(0, B) as i:
                norm.wait_finished(pe, i, 1)
                norm.tensor(pe, i, banks)

        @block.scalar
        def _(act):
            norm.start(act)
            with act.Fori(0, B) as i:
                norm.scalar(act, i, banks)

        @block.vector
        def _(dve):
            chain.eng, chain.per = dve, Norm.CHAIN
            with dve.Fori(0, B) as i:
                chain.start(i)
                norm.wait_finished(dve, i, 1)
                for t in range(TILES):
                    norm.add_tile(dve, chain, i, t, None)
                norm.vector_end(dve, chain, i)
                chain.end()


def mixture(nc, k, w, q_dram, k_dram):
    with Stage(nc) as ctx:
        comb = ctx.enter_context(nc.sbuf_tensor("m_comb", [P, ALL_TILES, EXPERTS], F32))
        xh = ctx.enter_context(nc.sbuf_tensor("m_xh", [P, KD, B * SEQ], F16))
        xl = ctx.enter_context(nc.sbuf_tensor("m_xl", [P, KD, B * SEQ], F16))
        gates(nc, k, w, comb, xh, xl)
        experts(nc, k, w, comb, xh, xl)
    norm_only(nc, k, "n")


TWO_PI = 6.283185307179586
TURN_PARTS = (6.28125, 0.0019350051879882812, 3.0199159795e-07)
ROUND = 12582912.0
MAX_ANGLE = 3.1415925


def recurrence(nc, k, w, q_dram, k_dram):
    with Stage(nc) as ctx:
        def sb(name, shape, dt=F32):
            return ctx.enter_context(nc.sbuf_tensor(f"r_{name}", shape, dt))

        def sig(name, per):
            return Signal(ctx, nc, f"r_{name}", per)

        N = SEQ + 1
        par = sb("par", [P, 7, KD])
        decay = sb("decay", [P, KD])
        damp = sb("damp", [P, KD])
        neg_damp = sb("neg_damp", [P, KD])
        theta = sb("theta", [P, KD])
        half_tanh = sb("half_tanh", [P, KD])
        one_less = sb("one_less", [P, KD])
        one_more = sb("one_more", [P, KD])
        r = sb("r", [P, KD])
        gate = sb("gate", [P, KD])
        coef = sb("coef", [P, 4, KD])
        minus = sb("minus", [P, 2, KD])
        time = sb("time", [P, N])
        phase = sb("phase", [P, 2, KD, N])
        whole = sb("whole", [P, 2, KD, N])
        wave = sb("wave", [P, 2, KD, N])
        fade = sb("fade", [P, KD, N])
        rr = sb("rr", [P, KD, SEQ])
        wave_a = sb("wave_a", [P, KD, SEQ])
        wave_b = sb("wave_b", [P, KD, SEQ])
        wave_c = sb("wave_c", [P, KD, SEQ])
        u = sb("u", [P, KD, 2, SEQ])
        d = sb("d", [P, KD, 2, SEQ])
        m = sb("m", [P, KD, 2, SEQ])
        y1 = sb("y1", [P, KD, SEQ])
        y = sb("y", [P, KD, SEQ])
        bank = [ctx.enter_context(nc.psum_tensor(f"r_bank{n}", [P, SEQ], F32)) for n in range(6)]
        norm = Norm(ctx, nc, k, "r")
        loaded = ctx.semaphore("r_loaded")
        time_ready = ctx.semaphore("r_time_ready")
        to_act = ctx.semaphore("r_to_act")
        from_act = ctx.semaphore("r_from_act")
        tables = ctx.semaphore("r_tables")
        u_ready, scanned, m_ready, y1_ready, y_ready = (sig(n, KD) for n in ("u_ready", "scanned", "m_ready", "y1_ready", "y_ready"))
        out_ready = sig("out_ready", TILES)
        chain = Chain(ctx, nc, "r_chain")
        block = ctx.enter_context(nc.Block())

        @block.sync
        def _(sp):
            sp.dma_start(par[:, :, :], w["phazor"]).then_inc(loaded, 16)

        @block.gpsimd
        def _(pool):
            pool.iota(time[:, :], pattern=[[1, N]], base=0, channel_multiplier=0,
                      allow_small_or_imprecise_dtypes=True).then_inc(time_ready, 1)
            pool.wait_ge(from_act, 3)
            with pool.Fori(0, B) as i:
                for c in range(KD):
                    for n in range(2):
                        last = pool.tensor_tensor(u[:, c, n, :], k["xT"][:, c, batch_cols(i)], wave[:, n, c, 0:SEQ], ALU.mult)
                    last.then_inc(u_ready.sem, 1)
                for c in range(KD):
                    pool.wait_ge(m_ready.sem, m_ready.at(i, c + 1))
                    pool.tensor_tensor(y1[:, c, :], m[:, c, 0, :], m[:, c, 1, :], ALU.add).then_inc(y1_ready.sem, 1)
                    pool.wait_ge(y1_ready.sem, y1_ready.at(i, c + 1))
                    pool.tensor_tensor(y[:, c, :], y1[:, c, :], wave_c[:, c, :], ALU.add).then_inc(y_ready.sem, 1)
                norm.pool(pool, i)

        @block.scalar
        def _(act):
            norm.start(act)
            act.wait_ge(loaded, 16)
            act.activation(decay[:, :], par[:, 1, :], ACT.Exp).then_inc(from_act, 1)
            act.wait_ge(to_act, 1)
            act.wait_ge(time_ready, 1)
            act.activation(half_tanh[:, :], damp[:, :], ACT.Tanh, scale=0.5)
            for c in range(KD):
                last = act.activation(fade[:, c, :], time[:, :], ACT.Exp, scale=neg_damp[:, c:c + 1])
            last.then_inc(from_act, 1)
            act.wait_ge(to_act, 2)
            act.activation(wave[:, :, :, :], phase[:, :, :, :], ACT.Sin).then_inc(from_act, 1)
            with act.Fori(0, B) as i:
                norm.scalar(act, i, (bank[4], bank[5]))

        @block.tensor
        def _(pe):
            with pe.Fori(0, B) as i:
                norm.wait_finished(pe, i, 1)
                for c in range(KD):
                    pe.wait_ge(y_ready.sem, y_ready.at(i, c + 1))
                for t in range(TILES):
                    for c in range(KD):
                        last = pe.transpose(bank[t][:, c * P:(c + 1) * P], y[:, c, t * P:(t + 1) * P], k["ident"][:, :])
                    last.then_inc(out_ready.sem, 1)
                norm.tensor(pe, i, (bank[4], bank[5]))

        @block.vector
        def _(dve):
            chain.eng = dve
            dve.wait_ge(loaded, 16)
            chain.link(dve.tensor_tensor(theta[:, :], par[:, 0, :], par[:, 2, :], ALU.mult))
            dve.wait_ge(from_act, 1)
            chain.link(dve.tensor_tensor(damp[:, :], decay[:, :], par[:, 2, :], ALU.mult))
            dve.tensor_scalar(neg_damp[:, :], damp[:, :], -1.0, None, ALU.mult).then_inc(to_act, 1)
            dve.wait_ge(time_ready, 1)
            for c in range(KD):
                chain.do(dve.tensor_scalar(phase[:, 1, c, :], time[:, :], theta[:, c:c + 1], None, ALU.mult))
                chain.do(dve.tensor_scalar(phase[:, 0, c, :], time[:, :], theta[:, c:c + 1], TWO_PI / 4, ALU.mult, ALU.add))
            chain.settle()
            flat = lambda t: t[:, :, :, :].rearrange("p a c n -> p (a c n)")
            chain.link(dve.tensor_scalar(flat(whole), flat(phase), 1 / TWO_PI, ROUND, ALU.mult, ALU.add))
            chain.link(dve.tensor_scalar(flat(whole), flat(whole), ROUND, None, ALU.subtract))
            for part in TURN_PARTS:
                chain.link(dve.scalar_tensor_tensor(flat(phase), flat(whole), -part, flat(phase), ALU.mult, ALU.add))
            dve.tensor_scalar(flat(phase), flat(phase), MAX_ANGLE, -MAX_ANGLE, ALU.min, ALU.max).then_inc(to_act, 1)
            dve.wait_ge(from_act, 2)
            chain.do(dve.tensor_scalar(one_less[:, :], half_tanh[:, :], -1.0, 1.0, ALU.mult, ALU.add))
            chain.link(dve.tensor_scalar(one_more[:, :], half_tanh[:, :], 1.0, None, ALU.add))
            chain.link(dve.reciprocal(one_more[:, :], one_more[:, :]))
            chain.do(dve.tensor_tensor(r[:, :], one_less[:, :], one_more[:, :], ALU.mult))
            chain.link(dve.scalar_tensor_tensor(gate[:, :], half_tanh[:, :], 2.0, one_more[:, :], ALU.mult, ALU.mult))
            for n in range(4):
                chain.do(dve.tensor_tensor(coef[:, n, :], par[:, 3 + n, :], gate[:, :], ALU.mult))
            for c in range(KD):
                chain.do(dve.memset(rr[:, c, :], 0.0))
            chain.settle()
            for n in range(2):
                chain.do(dve.tensor_scalar(minus[:, n, :], coef[:, 2 * n + 1, :], -1.0, None, ALU.mult))
            for c in range(KD):
                chain.do(dve.tensor_scalar(rr[:, c, :], rr[:, c, :], r[:, c:c + 1], None, ALU.add))
            chain.settle()
            dve.wait_ge(from_act, 3)
            for c in range(KD):
                cos, sin = wave[:, 0, c, :], wave[:, 1, c, :]
                chain.do(dve.tensor_scalar(wave_a[:, c, :], cos[:, 0:SEQ], coef[:, 0, c:c + 1], None, ALU.mult))
                chain.do(dve.tensor_scalar(wave_b[:, c, :], cos[:, 0:SEQ], coef[:, 1, c:c + 1], None, ALU.mult))
                chain.link(dve.tensor_scalar(wave_c[:, c, :], cos[:, 1:N], coef[:, 2, c:c + 1], None, ALU.mult))
                chain.do(dve.scalar_tensor_tensor(wave_a[:, c, :], sin[:, 0:SEQ], minus[:, 0, c:c + 1], wave_a[:, c, :], ALU.mult, ALU.add))
                chain.do(dve.scalar_tensor_tensor(wave_b[:, c, :], sin[:, 0:SEQ], coef[:, 0, c:c + 1], wave_b[:, c, :], ALU.mult, ALU.add))
                chain.link(dve.scalar_tensor_tensor(wave_c[:, c, :], sin[:, 1:N], minus[:, 1, c:c + 1], wave_c[:, c, :], ALU.mult, ALU.add))
                chain.link(dve.tensor_tensor(wave_c[:, c, :], wave_c[:, c, :], fade[:, c, 1:N], ALU.mult))
            chain.base, chain.per = chain.n, Norm.CHAIN
            with dve.Fori(0, B) as i:
                chain.start(i)
                for c in range(KD):
                    dve.wait_ge(u_ready.sem, u_ready.at(i, c + 1))
                    for n in range(2):
                        last = dve.tensor_tensor_scan(d[:, c, n, :], rr[:, c, :], u[:, c, n, :], 0.0, ALU.mult, ALU.add)
                    last.then_inc(scanned.sem, 1)
                    dve.wait_ge(scanned.sem, scanned.at(i, c + 1))
                    dve.tensor_tensor(m[:, c, 0, :], d[:, c, 0, :], wave_a[:, c, :], ALU.mult)
                    dve.tensor_tensor(m[:, c, 1, :], d[:, c, 1, :], wave_b[:, c, :], ALU.mult).then_inc(m_ready.sem, 1)
                for t in range(TILES):
                    dve.wait_ge(out_ready.sem, out_ready.at(i, t + 1))
                    norm.add_tile(dve, chain, i, t, bank[t][:, 0:D])
                norm.vector_end(dve, chain, i)
                chain.end()


def read_mask(nc, k, w, mask_q, mask_k, q_scale):
    with Stage(nc) as ctx:
        raw = ctx.enter_context(nc.sbuf_tensor("k_raw", [P, 2, TILES, SEQ], I32))
        seen = ctx.enter_context(nc.sbuf_tensor("k_seen", [P, TILES, SEQ], F16))
        ones16 = ctx.enter_context(nc.sbuf_tensor("k_ones16", [P, P], F16))
        bank = ctx.enter_context(nc.psum_tensor("k_bank", [P, SEQ], F32))
        loaded = ctx.semaphore("k_loaded")
        ready = ctx.semaphore("k_ready")
        counted = ctx.semaphore("k_counted")
        block = ctx.enter_context(nc.Block())

        @block.sync
        def _(sp):
            for n in range(2):
                sp.dma_start(raw[:, n, :, :], w["mask"][:, n]).then_inc(loaded, 16)

        @block.vector
        def _(dve):
            dve.memset(ones16[:, :], 1.0)
            dve.wait_ge(loaded, 32)
            dve.tensor_scalar(seen[:, :, :], raw[:, 1, :, :], 0.0, None, ALU.not_equal).then_inc(ready, 1)
            for n, m in enumerate((mask_q, mask_k)):
                dve.tensor_scalar(m[:, :, :], raw[:, n, :, :], 0.0, MASKED, ALU.is_equal, ALU.mult)
            dve.wait_ge(counted, 1)
            dve.tensor_scalar(q_scale[:, :], bank[:, :], 1.0, DH ** -0.5, ALU.min, ALU.mult)

        @block.tensor
        def _(pe):
            pe.wait_ge(ready, 1)
            for kt in range(TILES):
                last = pe.matmul(bank[:, :], ones16[:, :], seen[:, kt, :], start=(kt == 0), stop=(kt == TILES - 1))
            last.then_inc(counted, 1)


def masked_attention(nc, k, w, q_dram, k_dram, mask_q, mask_k, wv, bv, wo):
    with Stage(nc) as ctx:
        def sb(name, shape, dt=F32):
            return ctx.enter_context(nc.sbuf_tensor(f"c_{name}", shape, dt))

        cb = sb("cb", [P, 2, KD, SEQ])
        ve = sb("ve", [P, TILES, H, 2 * DH])
        mx = sb("mx", [P, TILES, H], F16)
        mt = sb("mt", [H, SEQ], F16)
        probs = sb("probs", [P, 2, 4, SEQ])
        banks = [ctx.enter_context(nc.psum_tensor(f"c_bank{n}", [P, SEQ], F32)) for n in range(2)]
        pair = [ctx.enter_context(nc.psum_tensor(f"c_pair{n}", [P, 2, SEQ], F32)) for n in range(2)]
        u_bank = ctx.enter_context(nc.psum_tensor("c_u", [P, SEQ], F32))
        misc = ctx.enter_context(nc.psum_tensor("c_misc", [P, SEQ], F32))
        stacks = Stacks(ctx, nc, "c", q_dram, k_dram)
        tail = Attend(ctx, nc, k, "c", wo, u_bank, misc)
        norm = tail.norm
        NA = TILES * H
        NP_ = QUADS * TILES * 2
        loaded = [Signal(ctx, nc, f"c_loaded{n}", 16) for n in range(2)]
        v_done = Signal(ctx, nc, "c_v_done", TILES)
        v_kept = Signal(ctx, nc, "c_v_kept", TILES)
        s_done = Signal(ctx, nc, "c_s_done", NA)
        s_max = Signal(ctx, nc, "c_s_max", NA)
        m_turned = Signal(ctx, nc, "c_m_turned", 1)
        m_kept = Signal(ctx, nc, "c_m_kept", 1)
        m_row = [Signal(ctx, nc, f"c_m_row{n}", 16) for n in range(2)]
        t_done = Signal(ctx, nc, "c_t_done", NP_)
        exp_done = Signal(ctx, nc, "c_exp_done", NP_)
        exp_read = Signal(ctx, nc, "c_exp_read", NP_ // 2)
        chain = Chain(ctx, nc, "c_chain")
        block = ctx.enter_context(nc.Block())

        @block.sync
        def _(sp):
            with sp.Fori(0, B // 2) as two:
                i2 = two * 2
                for half in range(2):
                    stacks.load(sp, i2, half, norm)
                    sp.dma_start(cb[:, half, :, :], w["ctxT"][:, :, batch_cols(i2 + half)]).then_inc(loaded[half].sem, 16)
                for half in range(2):
                    sp.wait_ge(m_kept.sem, m_kept.at(i2 + half, 1))
                    sp.wait_ge(stacks.edges.sem, 1)
                    sp.dma_start(stacks.q[MAX_ROW:ROWS, half, :, :], mt[:, :]).then_inc(m_row[half].sem, 16)

        @block.gpsimd
        def _(pool):
            with pool.Fori(0, B) as i:
                norm.pool(pool, i)

        @block.tensor
        def _(pe):
            def values(i, two, half):
                norm.wait_finished(pe, i, 1)
                pe.wait_ge(loaded[half].sem, two * 16 + 16)
                for t in range(TILES):
                    if t >= 2:
                        pe.wait_ge(v_kept.sem, v_kept.at(i, t - 1))
                    for c in range(KD):
                        last = pe.matmul((misc, u_bank)[t % 2][:, 0:D], cb[:, half, c, t * P:(t + 1) * P], wv[:, c, :],
                                         start=(c == 0), stop=(c == KD - 1))
                    last.then_inc(v_done.sem, 1)

            def maxima(i, half):
                for u in range(NA):
                    t, h = u // H, u % H
                    if u >= 2:
                        pe.wait_ge(s_max.sem, s_max.at(i, u - 1))
                    pe.matmul(banks[u % 2][:, :], k["ident16"][:, :], mask_q[:, t, :], start=True, stop=False)
                    pe.matmul(banks[u % 2][:, :], stacks.q[0:MAX_ROW, half, h, t * P:(t + 1) * P],
                              stacks.kk[0:MAX_ROW, half, h, :], start=False, stop=True).then_inc(s_done.sem, 1)
                pe.wait_ge(s_max.sem, s_max.at(i, NA))
                for t in range(TILES):
                    last = pe.matmul(misc[0:H, t * P:(t + 1) * P], mx[:, t, :], k["ident16"][:, :], start=True, stop=True)
                last.then_inc(m_turned.sem, 1)

            def weighted(i, g, kt):
                n = g * TILES + kt
                pe.wait_ge(exp_done.sem, exp_done.at(i, 2 * n + 2))
                if kt == 0 and g >= 1:
                    pe.wait_ge(tail.u_kept.sem, tail.u_kept.at(i, g))
                for m in range(4):
                    last = pe.matmul(u_bank[32 * m:32 * m + 32, :], ve[:, kt, 4 * g + m, :], probs[:, kt % 2, m, :],
                                     start=(kt == 0), stop=(kt == TILES - 1), skip_group_check=True)
                last.then_inc(exp_read.sem, 1)
                if kt == TILES - 1:
                    tail.tensor_denominators(pe, i, g)

            def transposed(i, half):
                for n in range(QUADS * TILES + 1):
                    if n < QUADS * TILES:
                        g, kt = n // TILES, n % TILES
                        for two_heads in range(2):
                            p = 2 * n + two_heads
                            if p >= 2:
                                pe.wait_ge(exp_done.sem, exp_done.at(i, p - 1))
                            for m in range(2):
                                h = 4 * g + 2 * two_heads + m
                                out = pair[p % 2][:, m, :]
                                pe.matmul(out, k["ident16"][:, :], mask_k[:, kt, :], start=True, stop=False)
                                last = pe.matmul(out, stacks.kk[0:ROWS, half, h, kt * P:(kt + 1) * P], stacks.q[0:ROWS, half, h, :],
                                                 start=False, stop=True)
                            last.then_inc(t_done.sem, 1)
                    if n >= 1:
                        weighted(i, (n - 1) // TILES, (n - 1) % TILES)

            pe.wait_ge(stacks.edges.sem, 1)
            with pe.Fori(0, B // 2) as two:
                i2 = two * 2
                for half in range(2):
                    i = i2 + half
                    values(i, two, half)
                    stacks.wait_loaded(pe, i2, half)
                    maxima(i, half)
                    pe.wait_ge(m_row[half].sem, two * 16 + 16)
                    transposed(i, half)
                    tail.tensor_out(pe, i)

        @block.scalar
        def _(act):
            norm.start(act)
            with act.Fori(0, B) as i:
                act.wait_ge(m_turned.sem, m_turned.at(i, 1))
                act.copy(mt[:, :], misc[0:H, :]).then_inc(m_kept.sem, 1)
                for p in range(NP_):
                    n = p // 2
                    act.wait_ge(t_done.sem, t_done.at(i, p + 1))
                    if n >= 2 and p % 2 == 0:
                        act.wait_ge(exp_read.sem, exp_read.at(i, n - 1))
                    act.activation(probs[:, n % 2, 2 * (p % 2):2 * (p % 2) + 2, :], pair[p % 2][:, :, :], ACT.Exp).then_inc(exp_done.sem, 1)
                    if p >= 2 * TILES and p % (2 * TILES) == 1:
                        tail.scalar_keep(act, i, n // TILES - 1, exp_read, n)
                tail.scalar_keep(act, i, QUADS - 1, exp_read, QUADS * TILES)
                norm.scalar(act, i, (u_bank, misc))

        @block.vector
        def _(dve):
            chain.eng = dve
            stacks.set_edges(dve, chain)
            for t in range(TILES):
                chain.do(dve.memset(ve[:, t, :, DH:2 * DH], 1.0))
            chain.base, chain.per = chain.n, Norm.CHAIN
            with dve.Fori(0, B) as i:
                chain.start(i)
                for t in range(TILES):
                    dve.wait_ge(v_done.sem, v_done.at(i, t + 1))
                    dve.tensor_tensor(ve[:, t, :, 0:DH], (misc, u_bank)[t % 2][:, 0:D].rearrange("p (h d) -> p h d", d=DH),
                                      bv[:, :].rearrange("p (h d) -> p h d", d=DH), ALU.add).then_inc(v_kept.sem, 1)
                for u in range(NA):
                    t, h = u // H, u % H
                    dve.wait_ge(s_done.sem, s_done.at(i, u + 1))
                    dve.tensor_reduce(mx[:, t, h:h + 1], banks[u % 2][:, :], AX.X, ALU.max).then_inc(s_max.sem, 1)
                for g in range(QUADS):
                    tail.vector_divide(dve, i, g)
                tail.vector_out(dve, chain, i)
                chain.end()


def cross_attention(nc, k, w, q_dram, k_dram):
    with Stage(nc) as ctx:
        def sb(name, shape, dt=F32):
            return ctx.enter_context(nc.sbuf_tensor(f"c_{name}", shape, dt))

        wq, wk, wv = (sb(n, [P, KD, D]) for n in ("wq", "wk", "wv"))
        wo = sb("wo", [P, QUADS, D])
        bias = sb("bias", [P, 2 * KD])
        bv = sb("bv", [P, D])
        mask_q = sb("mask_q", [P, TILES, SEQ], F16)
        mask_k = sb("mask_k", [P, TILES, SEQ], F16)
        q_scale = sb("q_scale", [P, SEQ])
        with Stage(nc) as load:
            done = load.semaphore("c_weights")
            block = load.enter_context(nc.Block())

            @block.sync
            def _(sp):
                for t, name in ((wq, "xw_q"), (wk, "xw_k"), (wv, "xw_v"), (wo, "xw_o")):
                    sp.dma_start(t[:, :, :], w[name]).then_inc(done, 16)
                for t, name in ((bias, "xb_qk"), (bv, "xb_v")):
                    sp.dma_start(t[:, :], w[name]).then_inc(done, 16)
                sp.wait_ge(done, 96)
        read_mask(nc, k, w, mask_q, mask_k, q_scale)
        split_projection(nc, k, "c", k["xT"], k["ctxT"], wq, wk, bias, q_dram, k_dram, q_scale)
        masked_attention(nc, k, w, q_dram, k_dram, mask_q, mask_k, wv, bv, wo)


FFN_OFFSETS = {"w1": 0, "w2": KD * HID, "h1": 2 * KD * HID, "h2": (2 * KD + HC) * HID, "w3": (2 * KD + 2 * HC) * HID}
FFN_ALL = FFN_OFFSETS["w3"] + HC * D
PIECE = 2048


def split_weights(nc, k, w, wh, wl, scale, w3_scale):
    N = FFN_ALL // PIECE
    with Stage(nc) as ctx:
        raw = ctx.enter_context(nc.sbuf_tensor("s_raw", [P, 4, PIECE], F32))
        loaded = [ctx.semaphore(f"s_loaded{n}") for n in range(4)]
        scales = ctx.semaphore("s_scales")
        high = ctx.semaphore("s_high")
        low = ctx.semaphore("s_low")
        block = ctx.enter_context(nc.Block())

        @block.sync
        def _(sp):
            sp.dma_start(scale[:, :, :], w["ffn_scale"]).then_inc(scales, 16)
            sp.dma_start(w3_scale[:, :], w["ffn_w3_scale"]).then_inc(scales, 16)
            for n in range(N):
                if n >= 4:
                    sp.wait_ge(low, n - 3)
                sp.dma_start(raw[:, n % 4, :], w["ffn_w"][:, n * PIECE:(n + 1) * PIECE]).then_inc(loaded[n % 4], 16)
            sp.wait_ge(scales, 32)

        @block.scalar
        def _(act):
            for n in range(N):
                act.wait_ge(loaded[n % 4], 16 * (n // 4 + 1))
                act.copy(wh[:, n * PIECE:(n + 1) * PIECE], raw[:, n % 4, :]).then_inc(high, 1)

        @block.vector
        def _(dve):
            for n in range(N):
                dve.wait_ge(high, n + 1)
                piece = slice(n * PIECE, (n + 1) * PIECE)
                dve.tensor_tensor(wl[:, piece], raw[:, n % 4, :], wh[:, piece], ALU.subtract).then_inc(low, 1)


def feed_forward(nc, k, w, q_dram, k_dram):
    with Stage(nc) as ctx:
        def sb(name, shape, dt=F32):
            return ctx.enter_context(nc.sbuf_tensor(f"f_{name}", shape, dt))

        def sig(name, per):
            return Signal(ctx, nc, f"f_{name}", per)

        wh = sb("wh", [P, FFN_ALL], BF16)
        wl = sb("wl", [P, FFN_ALL], BF16)
        scale = sb("scale", [P, 4, HC])
        w3_scale = sb("w3_scale", [P, D])
        split_weights(nc, k, w, wh, wl, scale, w3_scale)
        xh = sb("xh", [P, KD, SEQ], BF16)
        xl = sb("xl", [P, KD, SEQ], BF16)
        gated = sb("gated", [P, 2, SEQ])
        hf = sb("hf", [P, 2, SEQ])
        high = [sb(f"high{n}", [P, HC, SEQ], BF16) for n in range(2)]
        low = [sb(f"low{n}", [P, HC, SEQ], BF16) for n in range(2)]
        ys = sb("ys", [P, 2, D])
        bank = [ctx.enter_context(nc.psum_tensor(f"f_bank{n}", [P, SEQ], F32)) for n in range(8)]
        norm = Norm(ctx, nc, k, "f")
        CHUNKS = 3 * HC
        x_high, x_low = sig("x_high", 1), sig("x_low", 1)
        done = sig("done", CHUNKS)
        active = sig("active", CHUNKS)
        product = sig("product", HC)
        high_ready = sig("high_ready", CHUNKS)
        low_ready = sig("low_ready", CHUNKS)
        y_done, y_scaled = sig("y_done", TILES), sig("y_scaled", TILES)
        chain = Chain(ctx, nc, "f_chain")
        block = ctx.enter_context(nc.Block())

        def weight(part, name, c, at, width, rows=HID):
            start = FFN_OFFSETS[name] + c * rows + at
            return part[:, start:start + width]

        @block.gpsimd
        def _(pool):
            with pool.Fori(0, B) as i:
                pool.tensor_copy(xh[:, :, :], k["xT"][:, :, batch_cols(i)]).then_inc(x_high.sem, 1)
                wait_first(pool, x_high.sem, x_high.at(i, 1), k["passed"])
                pool.tensor_tensor(xl[:, :, :], k["xT"][:, :, batch_cols(i)], xh[:, :, :], ALU.subtract).then_inc(x_low.sem, 1)
                norm.pool(pool, i)

        @block.tensor
        def _(pe):
            def three(out, name, c, at, a_high, a_low, first, last_one):
                pe.matmul(out, weight(wh, name, c, at, P), a_high, start=first, stop=False)
                pe.matmul(out, weight(wh, name, c, at, P), a_low, start=False, stop=False)
                return pe.matmul(out, weight(wl, name, c, at, P), a_high, start=False, stop=last_one)

            with pe.Fori(0, B) as i:
                norm.wait_finished(pe, i, 1)
                pe.wait_ge(x_low.sem, x_low.at(i, 1))
                for hc in range(HC):
                    if hc >= 2:
                        pe.wait_ge(product.sem, product.at(i, hc - 1))
                    for n, name in enumerate(("w1", "w2")):
                        for c in range(KD):
                            last = three(bank[2 * (hc % 2) + n][:, :], name, c, hc * P, xh[:, c, :], xl[:, c, :], c == 0, c == KD - 1)
                    last.then_inc(done.sem, 1)
                for layer, name in ((1, "h1"), (2, "h2")):
                    src = (layer + 1) % 2
                    for hc in range(HC):
                        if layer == 2 or hc >= 2:
                            pe.wait_ge(active.sem, active.at(i, layer * HC + hc - 1))
                        for c in range(HC):
                            if hc == 0:
                                pe.wait_ge(low_ready.sem, low_ready.at(i, (layer - 1) * HC + c + 1))
                            last = three(bank[4 + hc % 2][:, :], name, c, hc * P, high[src][:, c, :], low[src][:, c, :], c == 0, c == HC - 1)
                        last.then_inc(done.sem, 1)
                for t in range(TILES):
                    tok = slice(t * P, (t + 1) * P)
                    if t >= 2:
                        pe.wait_ge(y_scaled.sem, y_scaled.at(i, t - 1))
                    for c in range(HC):
                        if t == 0:
                            pe.wait_ge(low_ready.sem, low_ready.at(i, 2 * HC + c + 1))
                        out = bank[6 + t % 2][:, 0:D]
                        pe.matmul(out, high[0][:, c, tok], weight(wh, "w3", c, 0, D, D), start=(c == 0), stop=False)
                        pe.matmul(out, low[0][:, c, tok], weight(wh, "w3", c, 0, D, D), start=False, stop=False)
                        last = pe.matmul(out, high[0][:, c, tok], weight(wl, "w3", c, 0, D, D), start=False, stop=(c == HC - 1))
                    last.then_inc(y_done.sem, 1)
                norm.tensor(pe, i, (bank[0], bank[1]))

        @block.scalar
        def _(act):
            norm.start(act)
            with act.Fori(0, B) as i:
                for hc in range(HC):
                    act.wait_ge(done.sem, done.at(i, hc + 1))
                    if hc >= 2:
                        act.wait_ge(product.sem, product.at(i, hc - 1))
                    act.activation(gated[:, hc % 2, :], bank[2 * (hc % 2)][:, :], ACT.Silu, scale=scale[:, 0, hc:hc + 1]).then_inc(active.sem, 1)
                for layer in (1, 2):
                    for hc in range(HC):
                        n = layer * HC + hc
                        act.wait_ge(done.sem, done.at(i, n + 1))
                        act.wait_ge(low_ready.sem, low_ready.at(i, n - 1))
                        act.activation(hf[:, hc % 2, :], bank[4 + hc % 2][:, :], ACT.Gelu, scale=scale[:, 1 + layer, hc:hc + 1]).then_inc(active.sem, 1)
                norm.scalar(act, i, (bank[0], bank[1]))

        @block.vector
        def _(dve):
            chain.eng, chain.per = dve, Norm.CHAIN
            with dve.Fori(0, B) as i:
                chain.start(i)
                for layer in range(3):
                    for hc in range(HC):
                        n = layer * HC + hc
                        dve.wait_ge(active.sem, active.at(i, n + 1))
                        if layer == 0:
                            if hc >= 2:
                                dve.wait_ge(low_ready.sem, low_ready.at(i, n - 1))
                            dve.scalar_tensor_tensor(hf[:, hc % 2, :], bank[2 * (hc % 2) + 1][:, :], scale[:, 1, hc:hc + 1],
                                                     gated[:, hc % 2, :], ALU.mult, ALU.mult).then_inc(product.sem, 1)
                            dve.wait_ge(product.sem, product.at(i, hc + 1))
                        dst = layer % 2
                        dve.tensor_copy(high[dst][:, hc, :], hf[:, hc % 2, :]).then_inc(high_ready.sem, 1)
                        dve.wait_ge(high_ready.sem, high_ready.at(i, n + 1))
                        dve.tensor_tensor(low[dst][:, hc, :], hf[:, hc % 2, :], high[dst][:, hc, :], ALU.subtract).then_inc(low_ready.sem, 1)
                for t in range(TILES):
                    dve.wait_ge(y_done.sem, y_done.at(i, t + 1))
                    if t >= 2:
                        dve.wait_ge(norm.summed.sem, norm.summed.at(i, t - 1))
                    dve.tensor_tensor(ys[:, t % 2, :], bank[6 + t % 2][:, 0:D], w3_scale[:, :], ALU.mult).then_inc(y_scaled.sem, 1)
                    dve.wait_ge(y_scaled.sem, y_scaled.at(i, t + 1))
                    norm.add_tile(dve, chain, i, t, ys[:, t % 2, :])
                norm.vector_end(dve, chain, i)
                chain.end()


LAYERS = [two_way_attention, mixture, recurrence, cross_attention, feed_forward]


def decoder(nc, w, out, layers=6, start=0):
    with Stage(nc) as ctx:
        def sb(name, shape, dt=F32):
            return ctx.enter_context(nc.sbuf_tensor(name, shape, dt))

        k = {
            "x": sb("x", [P, B * TILES, D]),
            "xT": sb("xT", [P, KD, B * SEQ]),
            "ctxT": sb("ctxT", [P, KD, B * SEQ]),
            "ident": sb("ident", [P, P]), "ident16": sb("ident16", [P, P], F16),
            "causal": sb("causal", [P, SEQ], F16), "causal_t": sb("causal_t", [P, SEQ], F16),
            "spread": sb("spread", [P, P]), "minus_half": sb("minus_half", [P, 8]), "ones": sb("ones", [P, P]),
            "wo0": sb("wo0", [P, QUADS, D]),
            "passed": ctx.semaphore("passed"),
        }
        q_dram = nc.dram_tensor("q_parts", [2, D, B * SEQ], F16).ap()
        k_dram = nc.dram_tensor("k_parts", [2, D, B * SEQ], F16).ap()
        with ExitStack() as first:
            for name, shape in (("wq0", [P, KD, D]), ("wk0", [P, KD, D]), ("wv0", [P, KD, D]),
                                ("qk_bias0", [P, 2 * KD]), ("v_bias0", [P, D])):
                k[name] = first.enter_context(nc.sbuf_tensor(name, shape, F32))
            merged_weights(nc, k, w)
            if start <= 0:
                split_projection(nc, k, "a", k["xT"], k["xT"], k["wq0"], k["wk0"], k["qk_bias0"], q_dram, k_dram)
                dilated_attention(nc, k, q_dram, k_dram, k["wv0"], k["v_bias0"], k["wo0"])
        for n, layer in enumerate(LAYERS):
            if start <= n + 1 < layers:
                layer(nc, k, w, q_dram, k_dram)
        write_out(nc, k, out)


def write_out(nc, k, out):
    with Stage(nc) as ctx:
        written = ctx.semaphore("written")
        block = ctx.enter_context(nc.Block())

        @block.sync
        def _(sp):
            sp.dma_start(out, k["x"][:, :, :]).then_inc(written, 16)
            sp.wait_ge(written, 16)




def _chunks(a):
    return a.reshape(-1, P, a.shape[-1]).transpose(1, 0, 2)


def _by_dim(a):
    return a.reshape(*a.shape[:-1], H, DH).swapaxes(-1, -2).reshape(a.shape)


def _head_rows(np, w_o, b_o):
    rows = np.zeros((QUADS, 4, 2 * DH, D), np.float32)
    rows[:, :, 0:DH] = w_o.reshape(QUADS, 4, DH, D)
    rows[0, 0, DH] = b_o
    return rows.reshape(QUADS, P, D).transpose(1, 0, 2)


def layouts(np, a):
    tok = lambda v: _chunks(v.reshape(B * SEQ, D))
    col = lambda v: v.reshape(-1, P).T
    wide = lambda v: np.broadcast_to(v.reshape(1, -1), (P, v.size))
    p0, p1 = "L0_attn_", "L1_xattn_"
    w = {
        "x": tok(a["x"]), "xT": _chunks(a["x"].reshape(B * SEQ, D).T),
        "ctxT": _chunks(a["ctx_1024"].reshape(B * SEQ, D).T),
        "c_attn_wT": _chunks(a[p0 + "c_attn_w"].T), "c_attn_b": col(a[p0 + "c_attn_b"]),
        "qkv_w": np.stack([_chunks(_by_dim(a[p0 + "q_w"])), _chunks(_by_dim(a[p0 + "k_w"])), _chunks(a[p0 + "v_w"])], 1),
        "qk_b": np.concatenate([col(_by_dim(a[p0 + "q_b"])), col(_by_dim(a[p0 + "k_b"]))], 1),
        "v_b": wide(a[p0 + "v_b"]),
        "wo0": _head_rows(np, a[p0 + "o_w"], a[p0 + "o_b"]),
        "ctx": tok(a["ctx_1024"]),
        "xa_vec": np.stack([col(a["L0_xattn_" + n]) for n in ("w_cq", "w_q", "w_c")], 1),
        "xa_wl": a["L0_xattn_W_l"].T.reshape(4, KD, P, D).transpose(2, 0, 1, 3),
        "xa_bl": a["L0_xattn_b_l"].reshape(1, D),
        "w_gate": _chunks(a["L0_ffn_W_gate"]),
        "moe_b_out": a["L0_ffn_b_out"],
        "moe_b_in": a["L0_ffn_b_in"].reshape(EXPERTS * HC, P).T,
        "moe_w": np.concatenate(
            [a["L0_ffn_" + n].reshape(EXPERTS, -1, P, m).transpose(0, 2, 1, 3).reshape(EXPERTS, P, -1)
             for n, m in (("W_in", HID), ("W_out", D))], 2),
        "phazor": np.stack([col(a["L1_attn_" + n]) for n in
                            ("phazor_angle", "ln_minus_ln_phazor_abs", "ln_phazor_scale", "phazor_init_re",
                             "phazor_init_im", "last_conv_re", "last_conv_im")], 1),
        "xw_q": _chunks(_by_dim(a[p1 + "W_q"])), "xw_k": _chunks(_by_dim(a[p1 + "W_k"])), "xw_v": _chunks(a[p1 + "W_v"]),
        "xw_o": _head_rows(np, a[p1 + "W_o"], a[p1 + "b_o"]),
        "xb_qk": np.concatenate([col(_by_dim(a[p1 + "b_q"])), col(_by_dim(a[p1 + "b_k"]))], 1),
        "xb_v": wide(a[p1 + "b_v"]),
        "mask": np.stack([_chunks(a["mask_1x1xSxS2_ik0"][0, 0]), _chunks(a["mask_1x1xSxS2_ik0"][0, 0].T)], 1),
        "ffn_w": np.concatenate([_chunks(a["L1_ffn_" + n + "_w"].T).reshape(P, -1) for n in ("w1", "w2", "h1", "h2", "w3")], 1),
        "ffn_scale": np.stack([col(a["L1_ffn_" + n + "_s"]) for n in ("w1", "w2", "h1", "h2")], 1),
        "ffn_w3_scale": wide(a["L1_ffn_w3_s"]),
        "xa_bs": np.concatenate([np.broadcast_to(a["L0_xattn_" + n].reshape(1, 1), (P, 1)) for n in ("b_cq", "b_c", "b_q")], 1),
    }
    return {n: np.ascontiguousarray(v) for n, v in w.items()}


def kernel(**inputs):
    import numpy as np
    import concourse.bacc as bacc
    from concourse.bass_utils import run_bass_kernel_spmd

    nc = bacc.Bacc("TRN2", target_bir_lowering=False, num_devices=1)
    arrays = layouts(np, {n: np.asarray(v) for n, v in inputs.items()})
    w = {n: nc.dram_tensor(f"in_{n}", v.shape, mybir.dt.from_np(v.dtype), kind="ExternalInput").ap()
         for n, v in arrays.items()}
    out = nc.dram_tensor("out", [P, B * TILES, D], F32, kind="ExternalOutput").ap()
    decoder(nc, w, out)
    got = run_bass_kernel_spmd(nc, [{f"in_{n}": v for n, v in arrays.items()}], core_ids=[0]).results[0]["out"]
    return got.transpose(1, 0, 2).reshape(B, SEQ, D)
```

```python
from contextlib import ExitStack

import concourse.bass as bass
from concourse import mybir

F32 = mybir.dt.float32
F16 = mybir.dt.float16
BF16 = mybir.dt.bfloat16
I32 = mybir.dt.int32
ALU = mybir.AluOpType
ACT = mybir.ActivationFunctionType
AX = mybir.AxisListType

P = 128
B, SEQ, D = 4, 512, 256
TILES = SEQ // P
KD = D // P
H, DH = 16, 16
QUADS = H // 4
EPS = 1e-5
MASKED = -60000.0
PARTS = 4
ZERO_ROW = PARTS * DH
MAX_ROW = ZERO_ROW + 1
ROWS = MAX_ROW + 1

def wait_first(eng, sem, value, passed):
    eng.wait_ge(sem, value)
    eng.sem_inc(passed, 1)

class Stage(ExitStack):

    def __init__(self, nc):
        super().__init__()
        self.nc, self.semaphores = nc, []

    def semaphore(self, name):
        self.semaphores.append(self.nc.alloc_semaphore(name))
        return self.semaphores[-1]

    def __exit__(self, *error):
        closed = super().__exit__(*error)
        if self.semaphores and error[0] is None:
            self.nc.clear_and_free_semaphores(self.semaphores)
            self.nc.all_engine_barrier()
        return closed

class Signal:

    def __init__(self, ctx, nc, name, per):
        self.sem = ctx.semaphore(name)
        self.per = per

    def at(self, turn, n):
        return turn * self.per + n

class Chain:

    def __init__(self, ctx, nc, name, eng=None, per=0):
        self.sem = ctx.semaphore(name)
        self.eng, self.per, self.turn, self.n, self.base = eng, per, 0, 0, 0

    def start(self, turn):
        self.turn, self.n = turn, 0

    def do(self, ins):
        ins.then_inc(self.sem, 1)
        self.n += 1

    def settle(self):
        self.eng.wait_ge(self.sem, self.turn * self.per + self.base + self.n)

    def settle_first(self, passed):
        wait_first(self.eng, self.sem, self.turn * self.per + self.base + self.n, passed)

    def link(self, ins):
        self.do(ins)
        self.settle()

    def end(self):
        assert self.n == self.per, (self.n, self.per)

def batch_cols(turn):
    return bass.ds(turn * SEQ, SEQ)

class Norm:

    CHAIN = 2 * TILES

    def __init__(self, ctx, nc, k, tag):
        self.nc, self.k = nc, k
        self.xs = ctx.enter_context(nc.sbuf_tensor(f"{tag}_xs", [P, TILES, D], F32))
        self.xn = ctx.enter_context(nc.sbuf_tensor(f"{tag}_xn", [P, TILES, D], F32))
        self.stats = ctx.enter_context(nc.sbuf_tensor(f"{tag}_stats", [P, TILES, 6], F32))
        self.mean_var = ctx.enter_context(nc.sbuf_tensor(f"{tag}_mean_var", [P, TILES, 2], F32))
        self.var_eps = ctx.enter_context(nc.sbuf_tensor(f"{tag}_var_eps", [P, TILES], F32))
        self.rstd = ctx.enter_context(nc.sbuf_tensor(f"{tag}_rstd", [P, TILES], F32))
        self.summed = Signal(ctx, nc, f"{tag}_summed", TILES)
        self.var_ready = Signal(ctx, nc, f"{tag}_var_ready", 1)
        self.rstd_ready = Signal(ctx, nc, f"{tag}_rstd_ready", 1)
        self.normed = Signal(ctx, nc, f"{tag}_normed", TILES)
        self.turned = Signal(ctx, nc, f"{tag}_turned", KD)
        self.xT_ready = Signal(ctx, nc, f"{tag}_xT_ready", KD)

    def start(self, act):
        act.sem_inc(self.xT_ready.sem, 2 * KD)

    def wait_finished(self, eng, turn, ago):
        eng.wait_ge(self.xT_ready.sem, self.xT_ready.at(turn, (3 - ago) * KD))

    def add_tile(self, dve, chain, turn, t, y):
        x = self.k["x"][:, bass.ds(turn * TILES + t, 1), :].rearrange("p a d -> p (a d)")
        if y is None:
            dve.tensor_copy(self.xs[:, t, :], x).then_inc(self.summed.sem, 1)
        else:
            dve.tensor_tensor(self.xs[:, t, :], y, x, ALU.add).then_inc(self.summed.sem, 1)
        dve.wait_ge(self.summed.sem, self.summed.at(turn, t + 1))
        chain.do(dve.bn_stats(self.stats[:, t, :], self.xs[:, t, :]))

    def vector_end(self, dve, chain, turn):
        chain.settle_first(self.k["passed"])
        for t in range(TILES):
            chain.do(dve.bn_aggr(self.mean_var[:, t, :], self.stats[:, t, :]))
        chain.settle()
        dve.tensor_scalar(self.var_eps[:, :], self.mean_var[:, :, 1], EPS, None, ALU.add).then_inc(self.var_ready.sem, 1)
        dve.wait_ge(self.rstd_ready.sem, self.rstd_ready.at(turn, 1))
        for t in range(TILES):
            dve.tensor_scalar(self.xn[:, t, :], self.xs[:, t, :], self.mean_var[:, t, 0:1], self.rstd[:, t:t + 1], ALU.subtract,
                              ALU.mult).then_inc(self.normed.sem, 1)

    def pool(self, pool, turn):
        pool.wait_ge(self.var_ready.sem, self.var_ready.at(turn, 1))
        pool.tensor_tensor(self.rstd[:, :], self.var_eps[:, :], self.k["minus_half"][:, 0:TILES],
                           ALU.pow).then_inc(self.rstd_ready.sem, 1)

    def tensor(self, pe, turn, banks):
        for kk in range(KD):
            for t in range(TILES):
                pe.wait_ge(self.normed.sem, self.normed.at(turn, t + 1))
                last = pe.transpose(banks[kk][:, t * P:(t + 1) * P], self.xn[:, t, kk * P:(kk + 1) * P], self.k["ident"][:, :])
            last.then_inc(self.turned.sem, 1)

    def scalar(self, act, turn, banks):
        act.wait_ge(self.normed.sem, self.normed.at(turn, TILES))
        act.copy(self.k["x"][:, bass.ds(turn * TILES, TILES), :], self.xn[:, :, :])
        for kk in range(KD):
            act.wait_ge(self.turned.sem, self.turned.at(turn, kk + 1))
            act.copy(self.k["xT"][:, kk, batch_cols(turn)], banks[kk][:, :]).then_inc(self.xT_ready.sem, 1)

CAUSAL_W = 128
BRANCHES = ((128, 1), (256, 2), (512, 4))
BLOCKS = 7
MAX_SLOTS = 12

def block_columns(j, h):
    if j < 4:
        return slice(j * P, (j + 1) * P)
    if j < 6:
        first = (j - 4) * 256 + h % 2
        return slice(first, first + 255, 2)
    return slice(h % 4, h % 4 + 509, 4)

def max_slot(j, h):
    return j if j < 4 else (4 + 2 * (j - 4) + h % 2 if j < 6 else 8 + h % 4)

def slot_columns(s):
    return block_columns(s, 0) if s < 4 else (block_columns(4 + (s - 4) // 2, (s - 4) % 2) if s < 8 else block_columns(6, s - 8))

def split_projection(nc, k, tag, src_q, src_k, wq, wk, bias, q_dram, k_dram, stacks, q_scale=None):
    NM = 2 * KD
    STORES = 16 * 2 * NM
    with Stage(nc) as ctx:
        hi = ctx.enter_context(nc.sbuf_tensor(f"{tag}_hi", [P, 2, NM, SEQ], F16))
        lo = ctx.enter_context(nc.sbuf_tensor(f"{tag}_lo", [P, 2, NM, SEQ], F16))
        ps = [ctx.enter_context(nc.psum_tensor(f"{tag}_ps{j}", [P, SEQ], F32)) for j in range(NM)]
        product_done = Signal(ctx, nc, f"{tag}_product_done", NM)
        hi_ready = Signal(ctx, nc, f"{tag}_hi_ready", NM)
        lo_ready = Signal(ctx, nc, f"{tag}_lo_ready", NM)
        q_full = ctx.enter_context(nc.sbuf_tensor(f"{tag}_q_full", [P, KD, SEQ], F32))
        scaled = Signal(ctx, nc, f"{tag}_scaled", KD)
        bank_free = Signal(ctx, nc, f"{tag}_bank_free", NM)
        stored = [Signal(ctx, nc, f"{tag}_stored{n}", STORES) for n in range(2)]
        block = ctx.enter_context(nc.Block())

        @block.tensor
        def _(pe):
            with pe.Fori(0, B) as i:
                for j in range(NM):
                    w, s, m = (wq, src_q, j) if j < KD else (wk, src_k, j - KD)
                    pe.wait_ge(bank_free.sem, bank_free.at(i, j + 1))
                    for c in range(KD):
                        last = pe.matmul(ps[j][:, :], w[:, c, m * P:(m + 1) * P], s[:, c, batch_cols(i)],
                                         start=(c == 0), stop=(c == KD - 1))
                    last.then_inc(product_done.sem, 1)

        @block.scalar
        def _(act):
            with act.Fori(0, B // 2) as two:
                i2 = two * 2
                for half in range(2):
                    i = i2 + half
                    act.wait_ge(stored[half].sem, i2 * (STORES // 2) + STORES)
                    for j in range(NM):
                        if q_scale is not None and j < KD:
                            act.wait_ge(scaled.sem, scaled.at(i, j + 1))
                            act.copy(hi[:, half, j, :], q_full[:, j, :]).then_inc(hi_ready.sem, 1)
                            continue
                        act.wait_ge(product_done.sem, product_done.at(i, j + 1))
                        act.activation(hi[:, half, j, :], ps[j][:, :], ACT.Identity, bias=bias[:, j:j + 1]).then_inc(hi_ready.sem, 1)

        @block.vector
        def _(dve):
            dve.sem_inc(bank_free.sem, NM)
            with dve.Fori(0, B // 2) as two:
                i2 = two * 2
                for half in range(2):
                    i = i2 + half
                    for j in range(NM):
                        if q_scale is not None and j < KD:
                            dve.wait_ge(product_done.sem, product_done.at(i, j + 1))
                            dve.scalar_tensor_tensor(q_full[:, j, :], ps[j][:, :], bias[:, j:j + 1], q_scale[:, :],
                                                     ALU.add, ALU.mult).then_inc(scaled.sem, 1)
                            dve.wait_ge(hi_ready.sem, hi_ready.at(i, j + 1))
                            dve.tensor_tensor(lo[:, half, j, :], q_full[:, j, :], hi[:, half, j, :], ALU.subtract).then_inc(lo_ready.sem, 1)
                            dve.wait_ge(lo_ready.sem, lo_ready.at(i, j + 1))
                            dve.sem_inc(bank_free.sem, 1)
                            continue
                        dve.wait_ge(hi_ready.sem, hi_ready.at(i, j + 1))
                        dve.scalar_tensor_tensor(lo[:, half, j, :], ps[j][:, :], bias[:, j:j + 1], hi[:, half, j, :],
                                                 ALU.add, ALU.subtract).then_inc(lo_ready.sem, 1)
                        dve.wait_ge(lo_ready.sem, lo_ready.at(i, j + 1))
                        dve.sem_inc(bank_free.sem, 1)

        @block.sync
        def _(sp):
            for n in range(2):
                sp.sem_inc(stored[n].sem, STORES)

            def store(i, half):
                for j in range(NM):
                    dst = q_dram if j < KD else k_dram
                    rows = slice((j % KD) * P, (j % KD + 1) * P)
                    sp.wait_ge(hi_ready.sem, hi_ready.at(i, j + 1))
                    sp.dma_start(dst[0, rows, batch_cols(i)], hi[:, half, j, :]).then_inc(stored[half].sem, 16)
                    sp.wait_ge(lo_ready.sem, lo_ready.at(i, j + 1))
                    sp.dma_start(dst[1, rows, batch_cols(i)], lo[:, half, j, :]).then_inc(stored[half].sem, 16)

            with sp.Fori(0, B // 2 - 1) as two:
                for half in range(2):
                    store(two * 2 + half, half)
            stacks.set_edges(sp, k["edges"])
            sp.wait_ge(stored[0].sem, STORES * (B // 2))
            stacks.load(sp, 0, 0)
            for half in range(2):
                store(B - 2 + half, half)
            for n in range(2):
                sp.wait_ge(stored[n].sem, STORES * (B // 2 + 1))

class Stacks:

    LOADS = 16 * 2 * PARTS

    def __init__(self, ctx, nc, tag, q_dram, k_dram):
        self.q = ctx.enter_context(nc.sbuf_tensor(f"{tag}_qs", [ROWS, 2, H, SEQ], F16))
        self.kk = ctx.enter_context(nc.sbuf_tensor(f"{tag}_ks", [ROWS, 2, H, SEQ], F16))
        self.loaded = [Signal(ctx, nc, f"{tag}_stack_loaded{n}", self.LOADS) for n in range(2)]
        self.edges = Signal(ctx, nc, f"{tag}_stack_edges", 1)
        self.q_dram, self.k_dram = q_dram, k_dram

    EDGES = 32

    def set_edges(self, sp, edges):
        for dst, rows in ((self.kk, 2), (self.q, 1)):
            src = edges[0:rows, :].unsqueeze(1).broadcast_to([rows, 2 * H, SEQ])
            sp.dma_start(dst[ZERO_ROW:ZERO_ROW + rows, :, :, :].rearrange("p a h t -> p (a h) t"), src).then_inc(self.edges.sem, 16)

    def load(self, sp, i, half):
        for part in range(PARTS):
            rows = slice(part * DH, (part + 1) * DH)
            for dst, src, which in ((self.q, self.q_dram, part // 2), (self.kk, self.k_dram, part % 2)):
                s = src[which].rearrange("(d h) t -> d h t", h=H)
                sp.dma_start(dst[rows, half, :, :], s[:, :, batch_cols(i)]).then_inc(self.loaded[half].sem, 16)

    def wait_loaded(self, eng, i, half):
        eng.wait_ge(self.loaded[half].sem, (i - half) * (self.LOADS // 2) + self.LOADS)

class Attend:

    def __init__(self, ctx, nc, k, tag, wo, bank, misc):
        self.k, self.wo, self.bank, self.misc = k, wo, bank, misc
        self.us = ctx.enter_context(nc.sbuf_tensor(f"{tag}_us", [P, 2, SEQ], F32))
        self.recip = ctx.enter_context(nc.sbuf_tensor(f"{tag}_recip", [P, TILES, 4], F32))
        self.recip_wide = ctx.enter_context(nc.sbuf_tensor(f"{tag}_recip_wide", [P, TILES, 4 * 2 * DH], F32))
        self.yT = ctx.enter_context(nc.sbuf_tensor(f"{tag}_yT", [P, QUADS, SEQ], F32))
        self.u_kept = Signal(ctx, nc, f"{tag}_u_kept", QUADS)
        self.z_ready = Signal(ctx, nc, f"{tag}_z_ready", QUADS)
        self.recip_ready = Signal(ctx, nc, f"{tag}_recip_ready", QUADS)
        self.wide_ready = Signal(ctx, nc, f"{tag}_wide_ready", QUADS)
        self.spread_ready = Signal(ctx, nc, f"{tag}_spread_ready", QUADS)
        self.y_kept = Signal(ctx, nc, f"{tag}_y_kept", QUADS)
        self.out_ready = Signal(ctx, nc, f"{tag}_out_ready", TILES)
        self.norm = Norm(ctx, nc, k, tag)

    def tensor_denominators(self, pe, i, g):
        pe.wait_ge(self.u_kept.sem, self.u_kept.at(i, g + 1))
        if g >= 1:
            pe.wait_ge(self.y_kept.sem, self.y_kept.at(i, g))
        for t in range(TILES):
            last = pe.matmul(self.misc[:, 4 * t:4 * t + 4], self.us[:, g % 2, t * P:(t + 1) * P],
                             self.k["spread"][:, ::2 * DH], start=True, stop=True)
        last.then_inc(self.z_ready.sem, 1)

    def tensor_spread(self, pe, i, g):
        pe.wait_ge(self.wide_ready.sem, self.wide_ready.at(i, g + 1))
        for t in range(TILES):
            last = pe.matmul(self.misc[:, t * P:(t + 1) * P], self.recip_wide[:, t, :], self.k["ident"][:, :], start=True, stop=True)
        last.then_inc(self.spread_ready.sem, 1)

    def pool_widen(self, pool, i):
        for g in range(QUADS):
            wait_first(pool, self.recip_ready.sem, self.recip_ready.at(i, g + 1), self.k["passed"])
            pool.tensor_copy(self.recip_wide[:, :, :].rearrange("p t (m r) -> p (t m) r", r=2 * DH),
                             self.recip[:, :, :].rearrange("p t m -> p (t m)").unsqueeze(2).broadcast_to([P, 4 * TILES, 2 * DH])
                             ).then_inc(self.wide_ready.sem, 1)

    def scalar_keep(self, act, i, g, ready, n):
        act.wait_ge(ready.sem, ready.at(i, n))
        if g >= 2:
            act.wait_ge(self.y_kept.sem, self.y_kept.at(i, g - 1))
        act.copy(self.us[:, g % 2, :], self.bank[:, :]).then_inc(self.u_kept.sem, 1)

    def vector_invert(self, dve, i, g):
        dve.wait_ge(self.z_ready.sem, self.z_ready.at(i, g + 1))
        dve.reciprocal(self.recip[:, :, :].rearrange("p t m -> p (t m)"), self.misc[:, 0:4 * TILES]).then_inc(self.recip_ready.sem, 1)

    def vector_scale(self, dve, i, g):
        dve.wait_ge(self.spread_ready.sem, self.spread_ready.at(i, g + 1))
        dve.tensor_tensor(self.yT[:, g, :], self.us[:, g % 2, :], self.misc[:, :], ALU.mult).then_inc(self.y_kept.sem, 1)

    def tensor_out(self, pe, i):
        for t in range(TILES):
            bank = (self.bank, self.misc)[t % 2]
            if t == 0:
                pe.wait_ge(self.y_kept.sem, self.y_kept.at(i, QUADS))
            if t >= 2:
                pe.wait_ge(self.norm.summed.sem, self.norm.summed.at(i, t - 1))
            for g in range(QUADS):
                last = pe.matmul(bank[:, 0:D], self.yT[:, g, t * P:(t + 1) * P], self.wo[:, g, :],
                                 start=(g == 0), stop=(g == QUADS - 1))
            last.then_inc(self.out_ready.sem, 1)

    def vector_out(self, dve, chain, i):
        for t in range(TILES):
            dve.wait_ge(self.out_ready.sem, self.out_ready.at(i, t + 1))
            self.norm.add_tile(dve, chain, i, t, (self.bank, self.misc)[t % 2][:, 0:D])
        self.norm.vector_end(dve, chain, i)

def all_batches(eng, turn):
    turn(0, 0, True, False)
    with eng.Fori(0, B // 2 - 1) as two:
        turn(two * 2 + 1, 1, False, False)
        turn(two * 2 + 2, 0, False, False)
    turn(B - 1, 1, False, True)

def share(total, step, first_step, steps):
    if step < first_step:
        return []
    n, steps = step - first_step, steps - first_step
    return list(range(total * n // steps, total * (n + 1) // steps))

def dilated_attention(nc, k, w, stacks, wv, bv, wo):
    with Stage(nc) as ctx:
        xb = ctx.enter_context(nc.sbuf_tensor("a_xb", [P, KD, SEQ], F32))
        ve = ctx.enter_context(nc.sbuf_tensor("a_ve", [P, H, BLOCKS, 2 * DH], F32))
        mx = ctx.enter_context(nc.sbuf_tensor("a_mx", [P, MAX_SLOTS, H], F16))
        mrow = ctx.enter_context(nc.sbuf_tensor("a_mrow", [H, 2, SEQ], F32))
        mt = ctx.enter_context(nc.sbuf_tensor("a_mt", [H, SEQ], F16))
        probs = ctx.enter_context(nc.sbuf_tensor("a_probs", [P, 2, 2, 4, P], F32))
        banks = [ctx.enter_context(nc.psum_tensor(f"a_bank{n}", [P, SEQ], F32)) for n in range(2)]
        pair = [ctx.enter_context(nc.psum_tensor(f"a_pair{n}", [P, 2, 4, P], F32)) for n in range(2)]
        u_bank = ctx.enter_context(nc.psum_tensor("a_u", [P, SEQ], F32))
        misc = ctx.enter_context(nc.psum_tensor("a_misc", [P, SEQ], F32))
        tail = Attend(ctx, nc, k, "a", wo, u_bank, misc)
        norm = tail.norm
        NA = QUADS * BLOCKS
        NB = QUADS * BLOCKS // 2
        FIRST_STEP = 1
        INVERT = {BLOCKS * (g + 1) // 2 + 1 + g % 2: g for g in range(QUADS - 1)}
        SCALE = {step + 1: g for step, g in INVERT.items()}
        v_banks = (banks[1], banks[0])
        xb_ready = Signal(ctx, nc, "a_xb_ready", 1)
        v_done = Signal(ctx, nc, "a_v_done", TILES)
        v_kept = Signal(ctx, nc, "a_v_kept", TILES)
        s_done = Signal(ctx, nc, "a_s_done", NA)
        s_max = Signal(ctx, nc, "a_s_max", NA)
        m_turned = Signal(ctx, nc, "a_m_turned", 3)
        m_first = Signal(ctx, nc, "a_m_first", 1)
        m_best = Signal(ctx, nc, "a_m_best", 2)
        m_row = [Signal(ctx, nc, f"a_m_row{n}", 16) for n in range(2)]
        t_done = Signal(ctx, nc, "a_t_done", NB)
        exp_done = Signal(ctx, nc, "a_exp_done", NB)
        exp_read = Signal(ctx, nc, "a_exp_read", NB)
        chain = Chain(ctx, nc, "a_chain")
        x_loaded = ctx.semaphore("a_x_loaded")
        ctx_loaded = ctx.semaphore("a_ctx_loaded")
        half_quad = Signal(ctx, nc, "a_half_quad", QUADS // 2)
        block = ctx.enter_context(nc.Block())

        @block.sync
        def _(sp):
            def row(i, half):
                sp.wait_ge(m_best.sem, m_best.at(i, 2))
                sp.dma_start(stacks.q[MAX_ROW:ROWS, half, :, :], mt[:, :]).then_inc(m_row[half].sem, 16)

            stacks.load(sp, 1, 1)
            sp.dma_start(k["x"][:, :, :], w["x"]).then_inc(x_loaded, 16)
            sp.dma_start(k["ctxT"][:, :, :], w["ctxT"]).then_inc(ctx_loaded, 16)
            row(0, 0)
            with sp.Fori(0, B // 2 - 1) as two:
                for half in range(2):
                    row(two * 2 + (half + 1), 1 - half)
                    sp.wait_ge(t_done.sem, t_done.at(two * 2 + half, NB))
                    stacks.load(sp, two * 2 + (half + 2), half)
            row(B - 1, 1)
            sp.wait_ge(ctx_loaded, 16)

        @block.gpsimd
        def _(pool):
            pool.tensor_copy(xb[:, :, :], k["xT"][:, :, 0:SEQ]).then_inc(xb_ready.sem, 1)
            with pool.Fori(0, B - 1) as i:
                wait_first(pool, v_done.sem, v_done.at(i, TILES), k["passed"])
                pool.tensor_copy(xb[:, :, :], k["xT"][:, :, batch_cols(i + 1)]).then_inc(xb_ready.sem, 1)
                tail.pool_widen(pool, i)
                norm.pool(pool, i)
            tail.pool_widen(pool, B - 1)
            norm.pool(pool, B - 1)

        @block.tensor
        def _(pe):
            def maximum(i, half, u):
                j, g = u // QUADS, u % QUADS
                bank = banks[u % 2]
                if u >= 2:
                    pe.wait_ge(s_max.sem, s_max.at(i, u - 1))
                pe.matmul(bank[:, :], k["ident16"][:, :], k["causal"][:, :], start=True, stop=False, skip_group_check=True)
                for n in range(4):
                    h = 4 * g + n
                    c = block_columns(j, h)
                    last = pe.matmul(bank[:, n * P:(n + 1) * P], stacks.q[0:MAX_ROW, half, h, c],
                                     stacks.kk[0:MAX_ROW, half, h, c], start=False, stop=True, skip_group_check=True)
                last.then_inc(s_done.sem, 1)

            def turn_maxima(i, branches):
                pe.wait_ge(s_max.sem, s_max.at(i, NA))
                for branch in branches:
                    if branch == 2:
                        pe.wait_ge(m_first.sem, m_first.at(i, 1))
                    for n in range(4):
                        s = 4 * branch + n
                        last = pe.matmul(banks[branch % 2][0:H, slot_columns(s)], mx[:, s, :], k["ident16"][:, :],
                                         start=(n == 0), stop=(n == 3), skip_group_check=True)
                    last.then_inc(m_turned.sem, 1)

            def values(i):
                pe.wait_ge(xb_ready.sem, i + 1)
                wh = wv[:, :, :].rearrange("p c (h d) -> p c h d", d=DH)
                for s in range(TILES):
                    bank = v_banks[s % 2]
                    if s < 2:
                        pe.wait_ge(m_best.sem, m_best.at(i, s + 1))
                    else:
                        pe.wait_ge(v_kept.sem, v_kept.at(i, s - 1))
                    for cols, first, step, at in ((block_columns(s, 0), 0, 1, 0),
                                                  (block_columns(4 + s // 2, s % 2), s % 2, 2, D),
                                                  (block_columns(6, s), s, 4, D + D // 2)):
                        for c in range(KD):
                            last = pe.matmul(bank[:, at:at + D // step], xb[:, c, cols], wh[:, c, first::step, :],
                                             start=(c == 0), stop=(c == KD - 1), skip_group_check=True)
                    last.then_inc(v_done.sem, 1)

            def scores(i, half, p, n):
                g, j = (2 * p + n) // BLOCKS, (2 * p + n) % BLOCKS
                if p >= 2 and n == 0:
                    pe.wait_ge(exp_done.sem, exp_done.at(i, p - 1))
                pe.matmul(pair[p % 2][:, n, :, :], k["ident16"][:, :], k["causal_t"][:, :], start=True, stop=False,
                          skip_group_check=True)
                for m in range(4):
                    h = 4 * g + m
                    c = block_columns(j, h)
                    last = pe.matmul(pair[p % 2][:, n, m, :], stacks.kk[0:ROWS, half, h, c],
                                     stacks.q[0:ROWS, half, h, c], start=False, stop=True, skip_group_check=True)
                if n == 1:
                    last.then_inc(t_done.sem, 1)

            def weighted(i, p):
                pe.wait_ge(exp_done.sem, exp_done.at(i, p + 1))
                for n in range(2):
                    g, j = (2 * p + n) // BLOCKS, (2 * p + n) % BLOCKS
                    if j == 0 and g >= 1:
                        pe.wait_ge(tail.u_kept.sem, tail.u_kept.at(i, g))
                    for m in range(4):
                        h = 4 * g + m
                        last = pe.matmul(u_bank[32 * m:32 * m + 32, block_columns(j, h)], ve[:, h, j, :], probs[:, p % 2, n, m, :],
                                         start=(j == 0), stop=(j == BLOCKS - 1), skip_group_check=True)
                    if n == 1:
                        last.then_inc(exp_read.sem, 1)
                    elif j == BLOCKS - 1:
                        last.then_inc(half_quad.sem, 1)

            def turn(i, half, first, last):
                pe.wait_ge(m_row[half].sem, (i - half) * 8 + 16)
                pe.wait_ge(v_kept.sem, v_kept.at(i, TILES))
                for p in range(NB + 1):
                    if not last and p == FIRST_STEP:
                        stacks.wait_loaded(pe, i + 1, 1 - half)
                    units = [] if last else share(NA, p, FIRST_STEP, NB + 1)
                    for n in range(2):
                        if p < NB:
                            scores(i, half, p, n)
                        for u in units[:1]:
                            maximum(i + 1, 1 - half, u)
                        units = units[1:]
                    if p == 1:
                        if not first:
                            norm.tensor(pe, i - 1, (u_bank, misc))
                        norm.wait_finished(pe, i, 1)
                    if p >= 1:
                        weighted(i, p - 1)
                    for u in units:
                        maximum(i + 1, 1 - half, u)
                    if p in INVERT:
                        tail.tensor_denominators(pe, i, INVERT[p])
                    if p in SCALE:
                        tail.tensor_spread(pe, i, SCALE[p])
                tail.tensor_denominators(pe, i, QUADS - 1)
                if not last:
                    turn_maxima(i + 1, (0, 1))
                tail.tensor_spread(pe, i, QUADS - 1)
                if not last:
                    turn_maxima(i + 1, (2,))
                    values(i + 1)
                tail.tensor_out(pe, i)

            pe.wait_ge(stacks.edges.sem, stacks.EDGES)
            stacks.wait_loaded(pe, 0, 0)
            for u in range(NA):
                maximum(0, 0, u)
            turn_maxima(0, (0, 1, 2))
            values(0)
            all_batches(pe, turn)
            norm.tensor(pe, B - 1, (u_bank, misc))

        @block.scalar
        def _(act):
            def keep(i, g):
                if g % 2 == 0:
                    tail.scalar_keep(act, i, g, half_quad, g // 2 + 1)
                else:
                    tail.scalar_keep(act, i, g, exp_read, BLOCKS * (g + 1) // 2)

            def keep_first(i):
                act.wait_ge(m_turned.sem, m_turned.at(i, 1))
                act.copy(mrow[:, 0, :], banks[0][0:H, :]).then_inc(m_first.sem, 1)

            def turn(i, half, first, last):
                for p in range(NB):
                    act.wait_ge(t_done.sem, t_done.at(i, p + 1))
                    if p >= 2:
                        act.wait_ge(exp_read.sem, exp_read.at(i, p - 1))
                    act.activation(probs[:, p % 2, :, :, :], pair[p % 2][:, :, :, :], ACT.Exp).then_inc(exp_done.sem, 1)
                    if p == 1 and not first:
                        norm.scalar(act, i - 1, (u_bank, misc))
                    for g in range(QUADS - 1):
                        if (BLOCKS * (g + 1) - 1) // 2 + 1 == p:
                            keep(i, g)
                keep(i, QUADS - 1)
                if not last:
                    keep_first(i + 1)

            norm.start(act)
            keep_first(0)
            all_batches(act, turn)
            norm.scalar(act, B - 1, (u_bank, misc))

        @block.vector
        def _(dve):
            def maximum(i, u):
                j, g = u // QUADS, u % QUADS
                dve.wait_ge(s_done.sem, s_done.at(i, u + 1))
                s = banks[u % 2][:, :].rearrange("p (n c) -> p n c", n=4)
                step = 1 if j < 4 else (2 if j < 6 else 4)
                for first in range(step):
                    h = 4 * g + first
                    last = dve.tensor_reduce(mx[:, max_slot(j, h), h:4 * g + 4:step], s[:, first::step, :], AX.X, ALU.max)
                last.then_inc(s_max.sem, 1)

            def best(i):
                dve.wait_ge(m_first.sem, m_first.at(i, 1))
                dve.wait_ge(m_turned.sem, m_turned.at(i, 2))
                dve.tensor_tensor(mrow[:, 1, :], banks[1][0:H, :], mrow[:, 0, :], ALU.max).then_inc(m_best.sem, 1)
                dve.wait_ge(m_best.sem, m_best.at(i, 1))
                dve.wait_ge(m_turned.sem, m_turned.at(i, 3))
                dve.tensor_tensor(mt[:, :], banks[0][0:H, :], mrow[:, 1, :], ALU.max).then_inc(m_best.sem, 1)

            def values(i):
                bh = bv[:, :].rearrange("p (h d) -> p h d", d=DH)
                for s in range(TILES):
                    dve.wait_ge(v_done.sem, v_done.at(i, s + 1))
                    for j, first, step, at in ((s, 0, 1, 0), (4 + s // 2, s % 2, 2, D), (6, s, 4, D + D // 2)):
                        v = v_banks[s % 2][:, at:at + D // step].rearrange("p (h d) -> p h d", d=DH)
                        last = dve.tensor_tensor(ve[:, first::step, j, 0:DH], v, bh[:, first::step, :], ALU.add)
                    last.then_inc(v_kept.sem, 1)

            def turn(i, half, first, last):
                chain.start(i)
                for p in range(NB + 1):
                    if not last:
                        for u in share(NA, p, FIRST_STEP, NB + 1):
                            maximum(i + 1, u)
                    if p in INVERT:
                        tail.vector_invert(dve, i, INVERT[p])
                    if p in SCALE:
                        tail.vector_scale(dve, i, SCALE[p])
                tail.vector_invert(dve, i, QUADS - 1)
                tail.vector_scale(dve, i, QUADS - 1)
                if not last:
                    best(i + 1)
                    values(i + 1)
                tail.vector_out(dve, chain, i)
                chain.end()

            chain.eng = dve
            for n in range(4):
                chain.do(dve.memset(ve[:, 4 * n:4 * n + 4, :, DH:2 * DH], 1.0))
            chain.link(dve.memset(mx[:, :, :], MASKED))
            chain.base, chain.per = chain.n, Norm.CHAIN
            for u in range(NA):
                maximum(0, u)
            best(0)
            values(0)
            dve.wait_ge(x_loaded, 16)
            all_batches(dve, turn)

def merged_weights(nc, k, w):
    with Stage(nc) as ctx:
        caT = ctx.enter_context(nc.sbuf_tensor("w_caT", [P, 3 * KD, D], F32))
        second = ctx.enter_context(nc.sbuf_tensor("w_second", [P, 3, KD, D], F32))
        ca_b = ctx.enter_context(nc.sbuf_tensor("w_ca_b", [P, 3 * KD], F32))
        qk_b = ctx.enter_context(nc.sbuf_tensor("w_qk_b", [P, 2 * KD], F32))
        v_b = ctx.enter_context(nc.sbuf_tensor("w_v_b", [P, D], F32))
        vb_wide = ctx.enter_context(nc.sbuf_tensor("w_vb_wide", [P, KD, P], F32))
        zeros = ctx.enter_context(nc.sbuf_tensor("w_zeros", [P, P], F32))
        ps = [ctx.enter_context(nc.psum_tensor(f"w_ps{n}", [P, SEQ], F32)) for n in range(6)]
        psb = ctx.enter_context(nc.psum_tensor("w_psb", [P, SEQ], F32))
        psv = ctx.enter_context(nc.psum_tensor("w_psv", [P, SEQ], F32))
        loaded = ctx.semaphore("w_loaded")
        late = ctx.semaphore("w_late")
        consts = ctx.semaphore("w_consts")
        made = ctx.semaphore("w_made")
        wide = ctx.semaphore("w_wide")
        zero = ctx.semaphore("w_zero")
        block = ctx.enter_context(nc.Block())

        @block.sync
        def _(sp):
            sp.dma_start(caT[:, :, :], w["c_attn_wT"]).then_inc(loaded, 16)
            sp.dma_start(second[:, :, :, :], w["qkv_w"]).then_inc(loaded, 16)
            sp.dma_start(ca_b[:, :], w["c_attn_b"]).then_inc(loaded, 16)
            sp.dma_start(qk_b[:, :], w["qk_b"]).then_inc(loaded, 16)
            sp.dma_start(v_b[:, :], w["v_b"]).then_inc(loaded, 16)
            sp.dma_start(k["wo0"][:, :, :], w["wo0"]).then_inc(late, 16)
            sp.dma_start(k["xT"][:, :, :], w["xT"]).then_inc(late, 16)
            sp.wait_ge(late, 32)

        @block.gpsimd
        def _(pool):
            n = 0
            for t, val in ((k["ident"], 0.0), (k["ident16"], 0.0), (k["causal"], 0.0), (k["causal_t"], 0.0),
                           (k["spread"], 0.0), (k["minus_half"], -0.5), (k["ones"], 1.0)):
                pool.memset(t[:, :], val).then_inc(consts, 1)
                n += 1
            pool.memset(k["edges"][:, :], -1.0).then_inc(consts, 1)
            n += 1
            pool.wait_ge(consts, n)
            pool.memset(k["edges"][0:1, :], 0.0).then_inc(consts, 1)
            for t in (k["ident"], k["ident16"]):
                pool.affine_select(out=t[:, :], in_=t[:, :], compare_op=ALU.not_equal, fill=1.0, base=0,
                                   pattern=[[-1, P]], channel_multiplier=1).then_inc(consts, 1)
            c = k["causal"][:, :].rearrange("p (n c) -> p n c", n=4)
            pool.affine_select(out=c, in_=c, compare_op=ALU.is_ge, fill=MASKED, base=0, pattern=[[0, 4], [-1, P]],
                               channel_multiplier=1).then_inc(consts, 1)
            c = k["causal_t"][:, :].rearrange("p (n c) -> p n c", n=4)
            pool.affine_select(out=c, in_=c, compare_op=ALU.is_ge, fill=MASKED, base=0, pattern=[[0, 4], [1, P]],
                               channel_multiplier=-1).then_inc(consts, 1)
            c = k["spread"][:, :].rearrange("p (n c) -> p n c", n=4)
            pool.affine_select(out=c, in_=c, compare_op=ALU.not_equal, fill=1.0, base=-DH, pattern=[[-2 * DH, 4], [0, 2 * DH]],
                               channel_multiplier=1).then_inc(consts, 1)
            pool.wait_ge(consts, n + 6)

        @block.tensor
        def _(pe):
            pe.wait_ge(loaded, 80)
            for m in range(3):
                for it in range(KD):
                    for c in range(KD):
                        last = pe.matmul(ps[2 * m + it][:, 0:D], caT[:, KD * m + c, it * P:(it + 1) * P], second[:, m, c, :],
                                         start=(c == 0), stop=(c == KD - 1))
                    last.then_inc(made, 1)
            for j in range(2 * KD):
                m, mt = j // KD, j % KD
                for c in range(KD):
                    last = pe.matmul(psb[:, j:j + 1], second[:, m, c, mt * P:(mt + 1) * P], ca_b[:, KD * m + c:KD * m + c + 1],
                                     start=(c == 0), stop=(c == KD - 1))
            last.then_inc(made, 1)
            pe.wait_ge(wide, KD)
            for c in range(KD):
                last = pe.matmul(psv[:, 0:D], vb_wide[:, c, :], second[:, 2, c, :], start=(c == 0), stop=(c == KD - 1))
            last.then_inc(made, 1)

        @block.vector
        def _(dve):
            dve.memset(zeros[:, :], 0.0).then_inc(zero, 1)
            dve.wait_ge(zero, 1)
            dve.wait_ge(loaded, 80)
            for c in range(KD):
                dve.tensor_scalar(vb_wide[:, c, :], zeros[:, :], ca_b[:, 2 * KD + c:2 * KD + c + 1], None, ALU.add).then_inc(wide, 1)
            for m, name in enumerate(("wq0", "wk0", "wv0")):
                for it in range(KD):
                    dve.wait_ge(made, 2 * m + it + 1)
                    dve.tensor_scalar(k[name][:, it, :], ps[2 * m + it][:, 0:D], DH ** -0.5 if m == 0 else 1.0, None, ALU.mult)
            dve.wait_ge(made, 7)
            dve.tensor_tensor(k["qk_bias0"][:, :], psb[:, 0:2 * KD], qk_b[:, :], ALU.add).then_inc(zero, 1)
            dve.wait_ge(zero, 2)
            dve.tensor_scalar(k["qk_bias0"][:, 0:KD], k["qk_bias0"][:, 0:KD], DH ** -0.5, None, ALU.mult)
            dve.wait_ge(made, 8)
            dve.tensor_tensor(k["v_bias0"][:, :], psv[:, 0:D], v_b[:, :], ALU.add)

ZERO_COLS = 1024

def two_way_attention(nc, k, w, x_slots):
    with Stage(nc) as ctx:
        def sb(name, shape, dt=F32):
            return ctx.enter_context(nc.sbuf_tensor(f"x_{name}", shape, dt))

        def sig(name, per):
            return Signal(ctx, nc, f"x_{name}", per)

        xb = sb("xb", [P, KD, SEQ])
        ctxb = sb("ctxb", [P, 2, TILES, D])
        cw = sb("cw", [P, KD, SEQ])
        w_vec = sb("w_vec", [P, 3, KD])
        w_l = sb("w_l", [P, 4, KD, D])
        b_l = sb("b_l", [1, D])
        b_s = sb("b_s", [P, 3])
        b_sum = sb("b_sum", [P, 2])
        w14 = sb("w14", [P, KD, D])
        probs = sb("probs", [P, TILES, SEQ])
        probs_t = sb("probs_t", [P, TILES, SEQ])
        c2q = sb("c2q", [P, KD, SEQ])
        cc = sb("cc", [P, KD, SEQ])
        neg_max = sb("neg_max", [P, TILES])
        zs = sb("zs", [P, TILES])
        rz = sb("rz", [P, TILES])
        v = sb("v", [P, TILES])
        e = sb("e", [P, TILES])
        neg_top = sb("neg_top", [1, 1])
        neg_top_all = sb("neg_top_all", [P, 1])
        e_sum = sb("e_sum", [P, 1])
        r_sum = sb("r_sum", [P, 1])
        row = sb("row", [1, D])
        q2c = sb("q2c", [P, KD])
        bank = [ctx.enter_context(nc.psum_tensor(f"x_bank{n}", [P, SEQ], F32)) for n in range(8)]
        norm = Norm(ctx, nc, k, "x")
        xb_ready, cw_ready = sig("xb_ready", 1), sig("cw_ready", KD)
        loaded = [sig(f"ctx_loaded{n}", 16) for n in range(2)]
        weights = ctx.semaphore("x_weights")
        s_done, cwc_done, neg_ready = sig("s_done", TILES), sig("cwc_done", 1), sig("neg_ready", TILES)
        p_done, p_normed = sig("p_done", TILES), sig("p_normed", TILES)
        t_done, t_kept = sig("t_done", TILES), sig("t_kept", TILES)
        c_done, c_kept, cc_ready = sig("c_done", KD), sig("c_kept", KD), sig("cc_ready", KD)
        v_ready, v_row, top_ready, top_wide, top_kept = (sig(n, 1) for n in ("v_ready", "v_row", "top_ready", "top_wide", "top_kept"))
        e_done, sums_done, row_kept, col_done, w14_ready = (sig(n, 1) for n in ("e_done", "sums_done", "row_kept", "col_done", "w14_ready"))
        out_ready = sig("out_ready", TILES)
        zeros = sb("zeros", [P, ZERO_COLS])
        zero_set = ctx.semaphore("x_zero_set")
        zeroed = ctx.semaphore("x_zeroed")
        chain = Chain(ctx, nc, "x_chain")
        block = ctx.enter_context(nc.Block())

        @block.sync
        def _(sp):
            sp.dma_start(w_vec[:, :, :], w["xa_vec"]).then_inc(weights, 16)
            sp.dma_start(w_l[:, :, :, :], w["xa_wl"]).then_inc(weights, 16)
            sp.dma_start(b_l[:, :], w["xa_bl"]).then_inc(weights, 16)
            sp.dma_start(b_s[:, :], w["xa_bs"]).then_inc(weights, 16)
            with sp.Fori(0, B // 2) as two:
                for half in range(2):
                    i = two * 2 + half
                    norm.wait_finished(sp, i, 2)
                    sp.dma_start(ctxb[:, half, :, :], w["ctx"][:, bass.ds(i * TILES, TILES), :]).then_inc(loaded[half].sem, 16)
            sp.wait_ge(zero_set, 1)
            reps = x_slots.shape[0] * D // P // ZERO_COLS
            sp.dma_start(x_slots.rearrange("(p n) d -> p (n d)", p=P).rearrange("p (r c) -> p r c", r=reps),
                         zeros[:, :].unsqueeze(1).broadcast_to([P, reps, ZERO_COLS])).then_inc(zeroed, 16)
            sp.wait_ge(zeroed, 16)

        @block.gpsimd
        def _(pool):
            pool.memset(zeros[:, :], 0.0).then_inc(zero_set, 1)
            with pool.Fori(0, B) as i:
                pool.tensor_copy(xb[:, :, :], k["xT"][:, :, batch_cols(i)]).then_inc(xb_ready.sem, 1)
                norm.pool(pool, i)

        @block.tensor
        def _(pe):
            def scores(i, first):
                pe.wait_ge(cw_ready.sem, cw_ready.at(i, KD))
                for t in range(TILES):
                    if t >= 2 and not first:
                        pe.wait_ge(norm.summed.sem, norm.summed.at(i, t - TILES + 1))
                    for c in range(KD):
                        last = pe.matmul(bank[t][:, :], cw[:, c, t * P:(t + 1) * P], k["ctxT"][:, c, batch_cols(i)],
                                         start=(c == 0), stop=(c == KD - 1))
                    last.then_inc(s_done.sem, 1)

            def turn(two, half, last_turn):
                i = two * 2 + half
                norm.wait_finished(pe, i, 1)
                pe.wait_ge(xb_ready.sem, xb_ready.at(i, 1))
                for t in range(TILES):
                    for c in range(KD):
                        last = pe.matmul(bank[7][:, t:t + 1], xb[:, c, t * P:(t + 1) * P], w_vec[:, 2, c:c + 1],
                                         start=(c == 0), stop=(c == KD - 1))
                last.then_inc(cwc_done.sem, 1)
                for qt in range(TILES):
                    if qt >= 2:
                        pe.wait_ge(t_kept.sem, t_kept.at(i, qt - 1))
                    for t in range(TILES):
                        pe.wait_ge(p_normed.sem, p_normed.at(i, t + 1))
                        last = pe.transpose(bank[4 + qt % 2][:, t * P:(t + 1) * P], probs[:, t, qt * P:(qt + 1) * P], k["ident"][:, :])
                    last.then_inc(t_done.sem, 1)
                pe.wait_ge(v_ready.sem, v_ready.at(i, 1))
                for t in range(TILES):
                    last = pe.matmul(bank[6][0:1, t * P:(t + 1) * P], v[:, t:t + 1], k["ident"][:, :], start=True, stop=True)
                last.then_inc(v_row.sem, 1)
                pe.wait_ge(loaded[half].sem, two * 16 + 16)
                for m in range(KD):
                    for qt in range(TILES):
                        pe.wait_ge(t_kept.sem, t_kept.at(i, qt + 1))
                        last = pe.matmul(bank[m][:, :], ctxb[:, half, qt, m * P:(m + 1) * P], probs_t[:, qt, :],
                                         start=(qt == 0), stop=(qt == TILES - 1))
                    last.then_inc(c_done.sem, 1)
                    if m == 0:
                        pe.wait_ge(top_ready.sem, top_ready.at(i, 1))
                        pe.matmul(bank[7][:, 8:9], k["ones"][0:1, :], neg_top[:, :], start=True, stop=True).then_inc(top_wide.sem, 1)
                pe.wait_ge(e_done.sem, e_done.at(i, 1))
                pe.matmul(bank[7][:, 9:10], k["ones"][:, :], e_sum[:, :], start=True, stop=True)
                for t in range(TILES):
                    last = pe.matmul(bank[6][0:1, 0:D], e[:, t:t + 1], k["x"][:, bass.ds(i * TILES + t, 1), :].rearrange("p a d -> p (a d)"),
                                     start=(t == 0), stop=(t == TILES - 1))
                last.then_inc(sums_done.sem, 1)
                pe.wait_ge(row_kept.sem, row_kept.at(i, 1))
                for c in range(KD):
                    last = pe.matmul(bank[7][:, 10 + c:11 + c], row[:, c * P:(c + 1) * P], k["ones"][0:1, 0:1], start=True, stop=True)
                last.then_inc(col_done.sem, 1)
                for t in range(TILES):
                    out = bank[2 + t % 2][:, 0:D]
                    tok = slice(t * P, (t + 1) * P)
                    if t >= 2:
                        pe.wait_ge(norm.summed.sem, norm.summed.at(i, t - 1))
                    pe.matmul(out, k["ones"][0:1, :], b_l[:, :], start=True, stop=False)
                    for c in range(KD):
                        pe.wait_ge(c_kept.sem, c_kept.at(i, KD))
                        pe.matmul(out, c2q[:, c, tok], w_l[:, 1, c, :], start=False, stop=False)
                    for c in range(KD):
                        pe.wait_ge(cc_ready.sem, cc_ready.at(i, KD))
                        pe.matmul(out, cc[:, c, tok], w_l[:, 2, c, :], start=False, stop=False)
                    pe.wait_ge(w14_ready.sem, w14_ready.at(i, 1))
                    for c in range(KD):
                        last = pe.matmul(out, xb[:, c, tok], w14[:, c, :], start=False, stop=(c == KD - 1))
                    last.then_inc(out_ready.sem, 1)
                if not last_turn:
                    scores(i + 1, False)
                norm.tensor(pe, i, (bank[4], bank[5]))

            pe.wait_ge(weights, 64)
            scores(0, True)
            with pe.Fori(0, B // 2 - 1) as two:
                turn(two, 0, False)
                turn(two, 1, False)
            turn(B // 2 - 1, 0, False)
            turn(B // 2 - 1, 1, True)

        @block.scalar
        def _(act):
            norm.start(act)
            with act.Fori(0, B) as i:
                for t in range(TILES):
                    act.wait_ge(neg_ready.sem, neg_ready.at(i, t + 1))
                    act.activation(probs[:, t, :], bank[t][:, :], ACT.Exp, bias=neg_max[:, t:t + 1],
                                   accum_out=zs[:, t:t + 1]).then_inc(p_done.sem, 1)
                for qt in range(TILES):
                    act.wait_ge(t_done.sem, t_done.at(i, qt + 1))
                    act.copy(probs_t[:, qt, :], bank[4 + qt % 2][:, :]).then_inc(t_kept.sem, 1)
                act.wait_ge(top_kept.sem, top_kept.at(i, 1))
                act.activation(e[:, :], v[:, :], ACT.Exp, bias=neg_top_all[:, 0:1], accum_out=e_sum[:, :]).then_inc(e_done.sem, 1)
                for m in range(KD):
                    act.wait_ge(c_done.sem, c_done.at(i, m + 1))
                    act.copy(c2q[:, m, :], bank[m][:, :]).then_inc(c_kept.sem, 1)
                norm.scalar(act, i, (bank[4], bank[5]))

        @block.vector
        def _(dve):
            chain.eng = dve
            dve.wait_ge(weights, 64)
            chain.link(dve.tensor_tensor(b_sum[:, 0:1], b_s[:, 0:1], b_s[:, 1:2], ALU.add))
            chain.link(dve.tensor_tensor(b_sum[:, 1:2], b_sum[:, 0:1], b_s[:, 2:3], ALU.add))
            chain.base, chain.per = chain.n, Norm.CHAIN + TILES + 3

            def scores_left(i):
                for c in range(KD):
                    dve.tensor_scalar(cw[:, c, :], k["xT"][:, c, batch_cols(i)], w_vec[:, 0, c:c + 1], w_vec[:, 1, c:c + 1],
                                      ALU.mult, ALU.add).then_inc(cw_ready.sem, 1)

            def turn(i, last):
                chain.start(i)
                for t in range(TILES):
                    dve.wait_ge(s_done.sem, s_done.at(i, t + 1))
                    dve.tensor_reduce(neg_max[:, t:t + 1], bank[t][:, :], AX.X, ALU.max, negate=True).then_inc(neg_ready.sem, 1)
                for t in range(TILES):
                    dve.wait_ge(p_done.sem, p_done.at(i, t + 1))
                    chain.link(dve.reciprocal(rz[:, t:t + 1], zs[:, t:t + 1]))
                    dve.tensor_scalar(probs[:, t, :], probs[:, t, :], rz[:, t:t + 1], None, ALU.mult).then_inc(p_normed.sem, 1)
                dve.wait_ge(cwc_done.sem, cwc_done.at(i, 1))
                dve.scalar_tensor_tensor(v[:, :], bank[7][:, 0:TILES], b_sum[:, 1:2], neg_max[:, :], ALU.add,
                                         ALU.subtract).then_inc(v_ready.sem, 1)
                dve.wait_ge(v_row.sem, v_row.at(i, 1))
                dve.tensor_reduce(neg_top[:, :], bank[6][0:1, :], AX.X, ALU.max, negate=True).then_inc(top_ready.sem, 1)
                dve.wait_ge(top_wide.sem, top_wide.at(i, 1))
                dve.tensor_copy(neg_top_all[:, :], bank[7][:, 8:9]).then_inc(top_kept.sem, 1)
                for m in range(KD):
                    dve.wait_ge(c_kept.sem, c_kept.at(i, m + 1))
                    dve.wait_ge(xb_ready.sem, xb_ready.at(i, 1))
                    dve.tensor_tensor(cc[:, m, :], c2q[:, m, :], xb[:, m, :], ALU.mult).then_inc(cc_ready.sem, 1)
                dve.wait_ge(sums_done.sem, sums_done.at(i, 1))
                chain.link(dve.reciprocal(r_sum[:, :], bank[7][:, 9:10]))
                dve.tensor_copy(row[:, :], bank[6][0:1, 0:D]).then_inc(row_kept.sem, 1)
                dve.wait_ge(col_done.sem, col_done.at(i, 1))
                chain.link(dve.tensor_scalar(q2c[:, :], bank[7][:, 10:10 + KD], r_sum[:, 0:1], None, ALU.mult))
                for c in range(KD):
                    ins = dve.scalar_tensor_tensor(w14[:, c, :], w_l[:, 3, c, :], q2c[:, c:c + 1], w_l[:, 0, c, :], ALU.mult, ALU.add)
                    if c < KD - 1:
                        chain.do(ins)
                    else:
                        ins.then_inc(w14_ready.sem, 1)
                if not last:
                    scores_left(i + 1)
                for t in range(TILES):
                    dve.wait_ge(out_ready.sem, out_ready.at(i, t + 1))
                    norm.add_tile(dve, chain, i, t, bank[2 + t % 2][:, 0:D])
                norm.vector_end(dve, chain, i)
                chain.end()

            scores_left(0)
            with dve.Fori(0, B - 1) as i:
                turn(i, False)
            turn(B - 1, True)

EXPERTS, HID = 8, 1024
CHOICES = 2
HC = HID // P
GROUPS, PER_GROUP = 2, HC // 2
W_IN = KD * HID
W_ALL = W_IN + HC * D
ALL_TILES = B * TILES
SLOT_TILES = CHOICES * ALL_TILES + EXPERTS
LAST = SLOT_TILES - 1
TURN = 4
TURNS = SLOT_TILES // TURN
LAG = 2
TABLE = 8
W_PART = 1024
W_PARTS = EXPERTS * W_ALL // W_PART
POOL_PARTS = 12

def route(nc, k, w, m, x_slots):
    with Stage(nc) as ctx:
        def sb(name, shape, dt=F32):
            return ctx.enter_context(nc.sbuf_tensor(f"g_{name}", shape, dt))

        wg = sb("wg", [P, KD, EXPERTS])
        raw = sb("raw", [P, 4, W_PART])
        logits = sb("logits", [P, ALL_TILES, EXPERTS])
        above = sb("above", [P, ALL_TILES, EXPERTS, EXPERTS])
        before = sb("before", [P, EXPERTS, EXPERTS])
        earlier = sb("earlier", [P, P])
        rank = sb("rank", [P, ALL_TILES, EXPERTS])
        chosen = sb("chosen", [P, ALL_TILES, EXPERTS])
        tmp = sb("tmp", [P, ALL_TILES, EXPERTS])
        tops = sb("tops", [P, CHOICES, ALL_TILES])
        gap = sb("gap", [P, ALL_TILES])
        ex = sb("ex", [P, ALL_TILES])
        den = sb("den", [P, ALL_TILES])
        tiles_of = sb("tiles_of", [P, EXPERTS])
        base = sb("base", [P, EXPERTS])
        base_slot = sb("base_slot", [P, EXPERTS])
        end = sb("end", [P, EXPERTS])
        tile_no = sb("tile_no", [P, TURNS, TABLE])
        threshold = sb("threshold", [P, ALL_TILES])
        over = sb("over", [P, EXPERTS, ALL_TILES])
        slots = sb("slots", [P, ALL_TILES, EXPERTS])
        slot_f = sb("slot_f", [P, CHOICES, ALL_TILES])
        passed_ends = sb("passed_ends", [P, TURNS * TABLE, EXPERTS])
        expert_f = sb("expert_f", [P, TURNS * TABLE])
        bank = [ctx.enter_context(nc.psum_tensor(f"g_bank{n}", [P, SEQ], F32)) for n in range(3)]
        wg_loaded = ctx.semaphore("g_wg_loaded")
        w_loaded = [ctx.semaphore(f"g_w_loaded{n}") for n in range(4)]
        w_high = ctx.semaphore("g_w_high")
        w_low_first = ctx.semaphore("g_w_low_first")
        w_low = ctx.semaphore("g_w_low")
        same_expert = sb("same_expert", [P, EXPERTS, ALL_TILES])
        upto = sb("upto", [P, EXPERTS, ALL_TILES])
        tile_pairs = sb("tile_pairs", [P, EXPERTS, ALL_TILES])
        consts = ctx.semaphore("g_consts")
        logits_done = ctx.semaphore("g_logits_done")
        ex_done = ctx.semaphore("g_ex_done")
        gap_ready = ctx.semaphore("g_gap_ready")
        chosen_ready = ctx.semaphore("g_chosen_ready")
        counted = ctx.semaphore("g_counted")
        slots_ready = ctx.semaphore("g_slots_ready")
        scattered = ctx.semaphore("g_scattered")
        ones_set = ctx.semaphore("g_ones_set")
        chain = Chain(ctx, nc, "g_chain")
        block = ctx.enter_context(nc.Block())

        def split(eng, n, done):
            part = slice(n * W_PART, (n + 1) * W_PART)
            eng.wait_ge(w_high, n + 1)
            eng.tensor_tensor(m["wl"][:, part], raw[:, n % 4, :], m["wh"][:, part], ALU.subtract).then_inc(done, 1)

        @block.sync
        def _(sp):
            sp.dma_start(wg[:, :, :], w["w_gate"]).then_inc(wg_loaded, 16)
            for n in range(W_PARTS):
                if n >= 4:
                    last = n - 4
                    if last < POOL_PARTS:
                        sp.wait_ge(w_low_first, last + 1)
                    else:
                        sp.wait_ge(w_low, last - POOL_PARTS + 1)
                e, part = n // (W_ALL // W_PART), n % (W_ALL // W_PART)
                sp.dma_start(raw[:, n % 4, :], w["moe_w"][e, :, part * W_PART:(part + 1) * W_PART]).then_inc(w_loaded[n % 4], 16)

        @block.gpsimd
        def _(pool):
            pool.memset(before[:, :, :], 0.0).then_inc(consts, 1)
            pool.memset(earlier[:, :], 0.0).then_inc(consts, 1)
            pool.wait_ge(consts, 2)
            pool.affine_select(out=before[:, :, :], in_=before[:, :, :], compare_op=ALU.is_ge, fill=1.0, base=0,
                               pattern=[[-1, EXPERTS], [1, EXPERTS]], channel_multiplier=0).then_inc(consts, 1)
            pool.affine_select(out=earlier[:, :], in_=earlier[:, :], compare_op=ALU.is_ge, fill=1.0, base=0,
                               pattern=[[-1, P]], channel_multiplier=1).then_inc(consts, 1)
            pool.iota(tile_no[:, :, :], pattern=[[TURN, TURNS], [1, TABLE]], base=-LAG, channel_multiplier=0,
                      allow_small_or_imprecise_dtypes=True).then_inc(consts, 1)
            pool.iota(threshold[:, :], pattern=[[P, ALL_TILES]], base=0, channel_multiplier=0,
                      allow_small_or_imprecise_dtypes=True).then_inc(consts, 1)
            for n in range(POOL_PARTS):
                split(pool, n, w_low_first)
            pool.wait_ge(slots_ready, 1)
            for t in range(ALL_TILES):
                for n in range(CHOICES):
                    pool.indirect_dma_start(x_slots, bass.IndirectOffsetOnAxis(ap=m["slot"][:, n, t:t + 1], axis=0),
                                            k["x"][:, t, :], None).then_inc(scattered, 16)
            pool.wait_ge(scattered, 16 * CHOICES * ALL_TILES)

        @block.tensor
        def _(pe):
            pe.wait_ge(wg_loaded, 16)
            for t in range(ALL_TILES):
                for c in range(KD):
                    last = pe.matmul(bank[0][:, t * EXPERTS:(t + 1) * EXPERTS], k["xT"][:, c, t * P:(t + 1) * P], wg[:, c, :],
                                     start=(c == 0), stop=(c == KD - 1))
            last.then_inc(logits_done, 1)
            pe.wait_ge(chosen_ready, 1)
            pe.wait_ge(consts, 4)
            flat = chosen[:, :, :].rearrange("p t e -> p (t e)")
            pe.matmul(bank[1][:, 0:ALL_TILES * EXPERTS], earlier[:, :], flat, start=True, stop=True)
            pe.matmul(bank[2][:, 0:ALL_TILES * EXPERTS], k["ones"][:, :], flat, start=True, stop=True).then_inc(counted, 1)

        @block.scalar
        def _(act):
            for n in range(W_PARTS):
                act.wait_ge(w_loaded[n % 4], n // 4 * 16 + 16)
                act.copy(m["wh"][:, n * W_PART:(n + 1) * W_PART], raw[:, n % 4, :]).then_inc(w_high, 1)
            act.wait_ge(gap_ready, 1)
            act.activation(ex[:, :], gap[:, :], ACT.Exp).then_inc(ex_done, 1)

        @block.vector
        def _(dve):
            chain.eng = dve

            dve.memset(same_expert[:, :, :], 1.0).then_inc(ones_set, 1)
            dve.wait_ge(ones_set, 1)
            chain.link(dve.memset(same_expert[:, :, 0:1], 0.0))
            dve.wait_ge(logits_done, 1)
            chain.link(dve.tensor_copy(logits[:, :, :].rearrange("p t e -> p (t e)"), bank[0][:, 0:ALL_TILES * EXPERTS]))
            wide = [P, ALL_TILES, EXPERTS, EXPERTS]
            other = logits[:, :, :].unsqueeze(2).broadcast_to(wide)
            own = logits[:, :, :].unsqueeze(3).broadcast_to(wide)
            first, second = m["pick"][0], m["pick"][1]
            chain.link(dve.tensor_tensor(above[:, :, :, :], other, own, ALU.is_equal))
            dve.wait_ge(consts, 6)
            chain.link(dve.tensor_tensor(above[:, :, :, :], above[:, :, :, :], before[:, :, :].unsqueeze(1).broadcast_to(wide), ALU.mult))
            chain.link(dve.tensor_reduce(tmp[:, :, :], above[:, :, :, :], AX.X, ALU.add))
            chain.link(dve.tensor_tensor(above[:, :, :, :], other, own, ALU.is_gt))
            chain.link(dve.tensor_reduce(rank[:, :, :], above[:, :, :, :], AX.X, ALU.add))
            chain.link(dve.tensor_tensor(rank[:, :, :], rank[:, :, :], tmp[:, :, :], ALU.add))
            for n, pick in enumerate((first, second)):
                chain.link(dve.tensor_scalar(pick[:, :, :], rank[:, :, :], float(n), None, ALU.is_equal))
            dve.tensor_tensor(chosen[:, :, :], first[:, :, :], second[:, :, :], ALU.add).then_inc(chosen_ready, 1)
            for n, pick in enumerate((first, second)):
                chain.link(dve.tensor_tensor(tmp[:, :, :], pick[:, :, :], logits[:, :, :], ALU.mult))
                chain.link(dve.tensor_reduce(tops[:, n, :], tmp[:, :, :], AX.X, ALU.add))
            dve.tensor_tensor(gap[:, :], tops[:, 1, :], tops[:, 0, :], ALU.subtract).then_inc(gap_ready, 1)
            dve.wait_ge(counted, 1)
            chain.link(dve.tensor_copy(tile_pairs[:, :, :], bank[2][:, 0:ALL_TILES * EXPERTS].rearrange("p (t e) -> p e t", e=EXPERTS)))
            by_expert = lambda t: t[:, :, :].rearrange("p e t -> p (e t)")
            chain.link(dve.tensor_tensor_scan(by_expert(upto), by_expert(same_expert), by_expert(tile_pairs), 0.0, ALU.mult, ALU.add))
            grid = [P, EXPERTS, ALL_TILES]
            chain.link(dve.tensor_tensor(over[:, :, :], upto[:, :, ALL_TILES - 1:ALL_TILES].broadcast_to(grid),
                                         threshold[:, :].unsqueeze(1).broadcast_to(grid), ALU.is_gt))
            chain.link(dve.tensor_reduce(tiles_of[:, :], over[:, :, :], AX.X, ALU.add))
            chain.link(dve.tensor_tensor(above[:, 0, :, :], before[:, :, :], tiles_of[:, :].unsqueeze(1).broadcast_to([P, EXPERTS, EXPERTS]), ALU.mult))
            chain.link(dve.tensor_reduce(base[:, :], above[:, 0, :, :], AX.X, ALU.add))
            chain.do(dve.tensor_scalar(base_slot[:, :], base[:, :], float(P), None, ALU.mult))
            chain.link(dve.tensor_tensor(end[:, :], base[:, :], tiles_of[:, :], ALU.add))
            chain.link(dve.tensor_tensor(upto[:, :, :], upto[:, :, :], tile_pairs[:, :, :], ALU.subtract))
            chain.link(dve.tensor_tensor(upto[:, :, :], upto[:, :, :], base_slot[:, :].unsqueeze(2).broadcast_to(grid), ALU.add))
            chain.link(dve.tensor_tensor(slots[:, :, :], bank[1][:, 0:ALL_TILES * EXPERTS].rearrange("p (t e) -> p t e", e=EXPERTS),
                                         upto[:, :, :].rearrange("p e t -> p t e"), ALU.add))
            for n, pick in enumerate((first, second)):
                chain.link(dve.tensor_tensor(tmp[:, :, :], pick[:, :, :], slots[:, :, :], ALU.mult))
                chain.link(dve.tensor_reduce(slot_f[:, n, :], tmp[:, :, :], AX.X, ALU.add))
            dve.tensor_copy(m["slot"][:, :, :], slot_f[:, :, :]).then_inc(slots_ready, 1)
            grid = [P, TURNS * TABLE, EXPERTS]
            chain.link(dve.tensor_tensor(passed_ends[:, :, :], tile_no[:, :, :].rearrange("p q n -> p (q n)").unsqueeze(2).broadcast_to(grid),
                                         end[:, :].unsqueeze(1).broadcast_to(grid), ALU.is_ge))
            chain.link(dve.tensor_reduce(expert_f[:, :], passed_ends[:, :, :], AX.X, ALU.add))
            for table, size in ((m["weights_at"], W_ALL), (m["bias_at"], HC)):
                chain.do(dve.tensor_scalar(table[:, :], expert_f[:, :], float(EXPERTS - 1), float(size), ALU.min, ALU.mult))
            for n in range(POOL_PARTS, W_PARTS):
                split(dve, n, w_low)
            dve.wait_ge(ex_done, 1)
            chain.link(dve.tensor_scalar(den[:, :], ex[:, :], 1.0, None, ALU.add))
            chain.link(dve.reciprocal(m["share"][:, 0, :], den[:, :]))
            chain.link(dve.tensor_tensor(m["share"][:, 1, :], ex[:, :], m["share"][:, 0, :], ALU.mult))
            each = [P, ALL_TILES, EXPERTS]
            for n, pick in enumerate((first, second)):
                chain.link(dve.tensor_tensor(pick[:, :, :], pick[:, :, :], m["share"][:, n, :].unsqueeze(2).broadcast_to(each), ALU.mult))
            dve.tensor_tensor(m["comb"][:, :, :], first[:, :, :], second[:, :, :], ALU.add)

def read_table(eng, registers, table, q, size):
    eng.load(registers, table[0:1, bass.ds(q * TABLE, TURN + LAG)])
    return [eng.snap(r, min_val=0, max_val=(EXPERTS - 1) * size) for r in registers]

def experts(nc, k, w, m, x_slots, y_slots):
    with Stage(nc) as ctx:
        def sb(name, shape, dt=F32):
            return ctx.enter_context(nc.sbuf_tensor(f"e_{name}", shape, dt))

        def sig(name, per):
            return Signal(ctx, nc, f"e_{name}", per)

        b_in = sb("b_in", [P, EXPERTS * HC])
        xt = sb("xt", [P, 2, D])
        xh = sb("xh", [P, 2, D], F16)
        xl = sb("xl", [P, 2, D], F16)
        hf = sb("hf", [P, 2, HID])
        hh = sb("hh", [P, 2, HID], F16)
        hl = sb("hl", [P, 2, HID], F16)
        y = sb("y", [P, 2, D])
        hb = [ctx.enter_context(nc.psum_tensor(f"e_h{n}", [P, SEQ], F32)) for n in range(2 * GROUPS)]
        yb = [ctx.enter_context(nc.psum_tensor(f"e_y{n}", [P, SEQ], F32)) for n in range(2)]
        tb = [ctx.enter_context(nc.psum_tensor(f"e_t{n}", [P, SEQ], F32)) for n in range(2)]
        b_loaded = ctx.semaphore("e_b_loaded")
        x_loaded = [sig(f"x_loaded{n}", 16) for n in range(2)]
        y_stored = [sig(f"y_stored{n}", 16) for n in range(2)]
        x_turned, x_high = sig("x_turned", 1), sig("x_high", 1)
        x_low = sig("x_low", 1)
        h_done = sig("h_done", GROUPS)
        gelu_done, h_high, h_low = sig("gelu_done", GROUPS), sig("h_high", GROUPS), sig("h_low", GROUPS)
        y_done = sig("y_done", 1)
        y_kept = sig("y_kept", 1)
        block = ctx.enter_context(nc.Block())

        @block.sync
        def _(sp):
            sp.dma_start(b_in[:, :], w["moe_b_in"]).then_inc(b_loaded, 16)
            with sp.Fori(0, SLOT_TILES // 2) as two:
                for half in range(2):
                    j = two * 2 + half
                    sp.wait_ge(x_low.sem, x_low.at(j, 1))
                    sp.dma_start(xt[:, half, :], x_slots[bass.ds(j * P, P), :]).then_inc(x_loaded[half].sem, 16)

        @block.tensor
        def _(pe):
            def weights(ws, at, size):
                return ws[:, bass.ds(at, size)]

            def turn_x(j, half):
                pe.wait_ge(x_low.sem, x_low.at(j, 1))
                pe.wait_ge(x_loaded[half].sem, (j - half) * 8 + 16)
                for c in range(KD):
                    last = pe.transpose(tb[half][:, c * P:(c + 1) * P], xt[:, half, c * P:(c + 1) * P], k["ident"][:, :])
                last.then_inc(x_turned.sem, 1)

            def up(j, half, base):
                pe.wait_ge(x_low.sem, x_low.at(j, 3))
                for g in range(GROUPS):
                    pe.wait_ge(gelu_done.sem, gelu_done.at(j, g + 1))
                    for n in range(PER_GROUP):
                        hc, first = g * PER_GROUP + n, True
                        for c in range(KD):
                            for ws, xs in ((m["wh"], xh), (m["wh"], xl), (m["wl"], xh)):
                                last = pe.matmul(hb[half * GROUPS + g][:, n * P:(n + 1) * P], weights(ws, base + (c * HID + hc * P), P),
                                                 xs[:, half, c * P:(c + 1) * P], start=first, stop=(ws is m["wl"] and c == KD - 1))
                                first = False
                    last.then_inc(h_done.sem, 1)

            def down(j, half, base):
                pe.wait_ge(y_kept.sem, y_kept.at(j, 1))
                pe.wait_ge(h_low.sem, h_low.at(j, 2 * GROUPS + GROUPS))
                for hc in range(HC):
                    for hs, ws in ((hh, m["wh"]), (hl, m["wh"]), (hh, m["wl"])):
                        last = pe.matmul(yb[half][:, 0:D], hs[:, half, hc * P:(hc + 1) * P], weights(ws, base + (W_IN + hc * D), D),
                                         start=(hc == 0 and hs is hh and ws is m["wh"]), stop=(hc == HC - 1 and ws is m["wl"]))
                last.then_inc(y_done.sem, 1)

            def turn(q, first=False, last=False):
                bases = read_table(pe, at, m["weights_at"], q, W_ALL)
                for n in range(TURN):
                    j = q * TURN + n
                    if not first or n >= LAG:
                        down(q * TURN + (n - LAG), n % 2, bases[n])
                    if not last or n < TURN - 1:
                        turn_x(q * TURN + (n + 1), 1 - n % 2)
                    up(j, n % 2, bases[n + LAG])

            at = [pe.alloc_register(f"e_weights_at{n}") for n in range(TURN + LAG)]
            turn_x(0, 0)
            turn(0, first=True)
            with pe.Fori(1, TURNS - 1) as q:
                turn(q)
            turn(TURNS - 1, last=True)
            bases = read_table(pe, at, m["weights_at"], TURNS - 1, W_ALL)
            for n in range(LAG):
                down(SLOT_TILES - LAG + n, n, bases[TURN + n])

        @block.scalar
        def _(act):
            act.sem_inc(gelu_done.sem, 2 * GROUPS)
            for half in range(2):
                act.sem_inc(y_stored[half].sem, 16)
            act.wait_ge(b_loaded, 16)

            def x_first(j, half):
                act.wait_ge(x_turned.sem, x_turned.at(j, 1))
                act.copy(xh[:, half, :], tb[half][:, 0:D]).then_inc(x_high.sem, 1)

            def gelu(j, half, e_at):
                for g in range(GROUPS):
                    act.wait_ge(h_done.sem, h_done.at(j, g + 1))
                    act.wait_ge(h_low.sem, h_low.at(j, g + 1))
                    for n in range(PER_GROUP):
                        hc = g * PER_GROUP + n
                        last = act.activation(hf[:, half, hc * P:(hc + 1) * P], hb[half * GROUPS + g][:, n * P:(n + 1) * P], ACT.Gelu,
                                              bias=b_in[:, bass.ds(e_at + hc, 1)])
                    last.then_inc(gelu_done.sem, 1)

            def store_y(j, half):
                act.wait_ge(y_kept.sem, y_kept.at(j, 3))
                act.dma_start(y_slots[bass.ds(j * P, P), :], y[:, half, :]).then_inc(y_stored[half].sem, 16)

            def turn(q, first=False, last=False):
                offsets = read_table(act, at, m["bias_at"], q, HC)
                for n in range(TURN):
                    if not last or n < TURN - 1:
                        x_first(q * TURN + (n + 1), 1 - n % 2)
                    gelu(q * TURN + n, n % 2, offsets[n + LAG])
                    if not first or n >= LAG:
                        store_y(q * TURN + (n - LAG), n % 2)

            at = [act.alloc_register(f"e_bias_at{n}") for n in range(TURN + LAG)]
            x_first(0, 0)
            turn(0, first=True)
            with act.Fori(1, TURNS - 1) as q:
                turn(q)
            turn(TURNS - 1, last=True)
            for half in range(2):
                store_y(SLOT_TILES - 2 + half, half)
            for half in range(2):
                act.wait_ge(y_stored[half].sem, y_stored[half].at(SLOT_TILES // 2, 16))

        @block.vector
        def _(dve):
            dve.sem_inc(x_low.sem, 2)
            dve.sem_inc(h_low.sem, 2 * GROUPS)
            dve.sem_inc(y_kept.sem, 2)

            def x_rest(j, half):
                dve.wait_ge(x_high.sem, x_high.at(j, 1))
                dve.tensor_tensor(xl[:, half, :], tb[half][:, 0:D], xh[:, half, :], ALU.subtract).then_inc(x_low.sem, 1)

            def keep_y(j, half):
                dve.wait_ge(y_stored[half].sem, (j - half) * 8 + 16)
                dve.wait_ge(y_done.sem, y_done.at(j, 1))
                dve.tensor_copy(y[:, half, :], yb[half][:, 0:D]).then_inc(y_kept.sem, 1)

            def split_h(j, half):
                for g in range(GROUPS):
                    part = slice(g * PER_GROUP * P, (g + 1) * PER_GROUP * P)
                    dve.wait_ge(gelu_done.sem, gelu_done.at(j, 2 * GROUPS + g + 1))
                    dve.tensor_copy(hh[:, half, part], hf[:, half, part]).then_inc(h_high.sem, 1)
                    dve.wait_ge(h_high.sem, h_high.at(j, g + 1))
                    dve.tensor_tensor(hl[:, half, part], hf[:, half, part], hh[:, half, part], ALU.subtract).then_inc(h_low.sem, 1)

            x_rest(0, 0)
            for j in range(2):
                x_rest(j + 1, 1 - j)
                split_h(j, j)
            with dve.Fori(1, SLOT_TILES // 2 - 1) as two:
                for half in range(2):
                    keep_y(two * 2 + (half - 2), half)
                    x_rest(two * 2 + (half + 1), 1 - half)
                    split_h(two * 2 + half, half)
            keep_y(LAST - 3, 0)
            x_rest(LAST, 1)
            split_h(LAST - 1, 0)
            keep_y(LAST - 2, 1)
            split_h(LAST, 1)
            for half in range(2):
                keep_y(SLOT_TILES - 2 + half, half)

def gather_and_norm(nc, k, w, m, y_slots, rot, cross, mask):
    with Stage(nc) as ctx:
        norm = Norm(ctx, nc, k, "n")
        b_out = ctx.enter_context(nc.sbuf_tensor("n_b_out", [EXPERTS, D], F32))
        comb_t = ctx.enter_context(nc.sbuf_tensor("n_comb_t", [EXPERTS, B * SEQ], F32))
        got = ctx.enter_context(nc.sbuf_tensor("n_got", [P, ALL_TILES, CHOICES, D], F32))
        banks = [ctx.enter_context(nc.psum_tensor(f"n_bank{n}", [P, SEQ], F32)) for n in range(KD)]
        cb = [ctx.enter_context(nc.psum_tensor(f"n_cb{n}", [P, SEQ], F32)) for n in range(2)]
        bb = [ctx.enter_context(nc.psum_tensor(f"n_bb{n}", [P, SEQ], F32)) for n in range(4)]
        loaded = ctx.semaphore("n_loaded")
        cross_loaded = ctx.semaphore("n_cross_loaded")
        gathered = [ctx.semaphore(f"n_gathered{n}") for n in range(B)]
        turned = ctx.semaphore("n_comb_turned")
        kept = ctx.semaphore("n_comb_kept")
        bias_done = ctx.semaphore("n_bias_done")
        added = ctx.semaphore("n_added")
        chain = Chain(ctx, nc, "n_chain")
        rot.allocate(ctx, nc)
        block = ctx.enter_context(nc.Block())

        @block.sync
        def _(sp):
            sp.dma_start(b_out[:, :], w["moe_b_out"]).then_inc(loaded, 16)
            rot.sync(sp)
            coming = ((k["ctxT"], "ctxT"), (mask, "mask"), (cross["wq"], "xw_q"), (cross["wk"], "xw_k"), (cross["wv"], "xw_v"),
                      (cross["wo"], "xw_o"), (cross["bias"], "xb_qk"), (cross["bv"], "xb_v"))
            for tensor, name in coming:
                sp.dma_start(tensor[(slice(None),) * len(tensor.shape)], w[name]).then_inc(cross_loaded, 16)
            sp.wait_ge(cross_loaded, 16 * len(coming))

        @block.gpsimd
        def _(pool):
            rot.pool(pool)
            for i in range(B):
                for t in range(i * TILES, (i + 1) * TILES):
                    for n in range(CHOICES):
                        pool.indirect_dma_start(got[:, t, n, :], None, y_slots,
                                                bass.IndirectOffsetOnAxis(ap=m["slot"][:, n, t:t + 1], axis=0)).then_inc(gathered[i], 16)
            for i in range(B):
                norm.pool(pool, i)

        @block.tensor
        def _(pe):
            pe.wait_ge(loaded, 16)
            for i in range(B):
                if i >= 2:
                    pe.wait_ge(kept, i - 1)
                for t in range(TILES):
                    last = pe.transpose(cb[i % 2][0:EXPERTS, t * P:(t + 1) * P], m["comb"][:, i * TILES + t, :], k["ident"][:, :])
                last.then_inc(turned, 1)
                pe.wait_ge(kept, i + 1)
                for t in range(TILES):
                    tile = i * TILES + t
                    if tile >= 4:
                        pe.wait_ge(added, tile - 3)
                    pe.matmul(bb[t][:, 0:D], comb_t[:, tile * P:(tile + 1) * P], b_out[:, :], start=True, stop=True).then_inc(bias_done, 1)
                norm.wait_finished(pe, i, 1)
                norm.tensor(pe, i, banks)

        @block.scalar
        def _(act):
            norm.start(act)
            rot.scalar(act)
            for i in range(B):
                act.wait_ge(turned, i + 1)
                act.copy(comb_t[:, i * SEQ:(i + 1) * SEQ], cb[i % 2][0:EXPERTS, :]).then_inc(kept, 1)
                norm.scalar(act, i, banks)

        @block.vector
        def _(dve):
            chain.eng = dve
            rot.vector(dve, chain)
            chain.base, chain.per = chain.n, Norm.CHAIN + 2 * TILES
            for i in range(B):
                chain.start(i)
                norm.wait_finished(dve, i, 1)
                dve.wait_ge(gathered[i], 16 * CHOICES * TILES)
                for n in range(CHOICES):
                    for t in range(i * TILES, (i + 1) * TILES):
                        chain.do(dve.scalar_tensor_tensor(k["x"][:, t, :], got[:, t, n, :], m["share"][:, n, t:t + 1], k["x"][:, t, :],
                                                          ALU.mult, ALU.add))
                    chain.settle()
                for t in range(TILES):
                    dve.wait_ge(bias_done, i * TILES + t + 1)
                    norm.add_tile(dve, chain, i, t, bb[t][:, 0:D])
                    dve.sem_inc(added, 1)
                norm.vector_end(dve, chain, i)
                chain.end()

def mixture(nc, k, w, x_slots, after):
    y_slots = nc.dram_tensor("y_slots", [SLOT_TILES * P, D], F32).ap()
    with Stage(nc) as ctx:
        def sb(name, shape, dt=F32):
            return ctx.enter_context(nc.sbuf_tensor(f"m_{name}", shape, dt))

        m = {"comb": sb("comb", [P, ALL_TILES, EXPERTS]), "share": sb("share", [P, CHOICES, ALL_TILES]),
             "slot": sb("slot", [P, CHOICES, ALL_TILES], I32), "weights_at": sb("weights_at", [P, TURNS * TABLE], I32), "bias_at": sb("bias_at", [P, TURNS * TABLE], I32)}
        with Stage(nc) as halves:
            m["wh"] = halves.enter_context(nc.sbuf_tensor("m_wh", [P, EXPERTS * W_ALL], F16))
            m["wl"] = halves.enter_context(nc.sbuf_tensor("m_wl", [P, EXPERTS * W_ALL], F16))
            with Stage(nc) as picks:
                m["pick"] = [picks.enter_context(nc.sbuf_tensor(f"m_pick{n}", [P, ALL_TILES, EXPERTS], F32)) for n in range(CHOICES)]
                route(nc, k, w, m, x_slots)
            experts(nc, k, w, m, x_slots, y_slots)
        after(m, y_slots)

TWO_PI = 6.283185307179586
TURN_PARTS = (6.28125, 0.0019350051879882812, 3.0199159795e-07)
ROUND = 12582912.0
MAX_ANGLE = 3.1415925

N = SEQ + 1

class Rotations:

    def __init__(self, ctx, nc, w):
        def sb(name, shape, dt=F32):
            return ctx.enter_context(nc.sbuf_tensor(f"r_{name}", shape, dt))

        self.w = w
        self.wave = sb("wave", [P, 2, KD, N])
        self.rr = sb("rr", [P, KD, SEQ])
        self.wave_a = sb("wave_a", [P, KD, SEQ])
        self.wave_b = sb("wave_b", [P, KD, SEQ])
        self.wave_c = sb("wave_c", [P, KD, SEQ])

    def allocate(self, ctx, nc):
        def sb(name, shape, dt=F32):
            return ctx.enter_context(nc.sbuf_tensor(f"r_{name}", shape, dt))

        self.par = sb("par", [P, 7, KD])
        self.decay = sb("decay", [P, KD])
        self.damp = sb("damp", [P, KD])
        self.neg_damp = sb("neg_damp", [P, KD])
        self.theta = sb("theta", [P, KD])
        self.half_tanh = sb("half_tanh", [P, KD])
        self.one_less = sb("one_less", [P, KD])
        self.one_more = sb("one_more", [P, KD])
        self.r = sb("r", [P, KD])
        self.gate = sb("gate", [P, KD])
        self.coef = sb("coef", [P, 4, KD])
        self.minus = sb("minus", [P, 2, KD])
        self.time = sb("time", [P, N])
        self.phase = sb("phase", [P, 2, KD, N])
        self.whole = sb("whole", [P, 2, KD, N])
        self.fade = sb("fade", [P, KD, N])
        self.loaded = ctx.semaphore("r_loaded")
        self.time_ready = ctx.semaphore("r_time_ready")
        self.to_act = ctx.semaphore("r_to_act")
        self.from_act = ctx.semaphore("r_from_act")

    def sync(self, sp):
        sp.dma_start(self.par[:, :, :], self.w["phazor"]).then_inc(self.loaded, 16)

    def pool(self, pool):
        pool.iota(self.time[:, :], pattern=[[1, N]], base=0, channel_multiplier=0,
                  allow_small_or_imprecise_dtypes=True).then_inc(self.time_ready, 1)

    def scalar(self, act):
        act.wait_ge(self.loaded, 16)
        act.activation(self.decay[:, :], self.par[:, 1, :], ACT.Exp).then_inc(self.from_act, 1)
        act.wait_ge(self.to_act, 1)
        act.wait_ge(self.time_ready, 1)
        act.activation(self.half_tanh[:, :], self.damp[:, :], ACT.Tanh, scale=0.5)
        for c in range(KD):
            last = act.activation(self.fade[:, c, :], self.time[:, :], ACT.Exp, scale=self.neg_damp[:, c:c + 1])
        last.then_inc(self.from_act, 1)
        act.wait_ge(self.to_act, 2)
        act.activation(self.wave[:, :, :, :], self.phase[:, :, :, :], ACT.Sin).then_inc(self.from_act, 1)

    def vector(self, dve, chain):
        dve.wait_ge(self.loaded, 16)
        chain.link(dve.tensor_tensor(self.theta[:, :], self.par[:, 0, :], self.par[:, 2, :], ALU.mult))
        dve.wait_ge(self.from_act, 1)
        chain.link(dve.tensor_tensor(self.damp[:, :], self.decay[:, :], self.par[:, 2, :], ALU.mult))
        dve.tensor_scalar(self.neg_damp[:, :], self.damp[:, :], -1.0, None, ALU.mult).then_inc(self.to_act, 1)
        dve.wait_ge(self.time_ready, 1)
        for c in range(KD):
            chain.do(dve.tensor_scalar(self.phase[:, 1, c, :], self.time[:, :], self.theta[:, c:c + 1], None, ALU.mult))
            chain.do(dve.tensor_scalar(self.phase[:, 0, c, :], self.time[:, :], self.theta[:, c:c + 1], TWO_PI / 4, ALU.mult, ALU.add))
        chain.settle()
        flat = lambda t: t[:, :, :, :].rearrange("p a c n -> p (a c n)")
        chain.link(dve.tensor_scalar(flat(self.whole), flat(self.phase), 1 / TWO_PI, ROUND, ALU.mult, ALU.add))
        chain.link(dve.tensor_scalar(flat(self.whole), flat(self.whole), ROUND, None, ALU.subtract))
        for part in TURN_PARTS:
            chain.link(dve.scalar_tensor_tensor(flat(self.phase), flat(self.whole), -part, flat(self.phase), ALU.mult, ALU.add))
        dve.tensor_scalar(flat(self.phase), flat(self.phase), MAX_ANGLE, -MAX_ANGLE, ALU.min, ALU.max).then_inc(self.to_act, 1)
        dve.wait_ge(self.from_act, 2)
        chain.do(dve.tensor_scalar(self.one_less[:, :], self.half_tanh[:, :], -1.0, 1.0, ALU.mult, ALU.add))
        chain.link(dve.tensor_scalar(self.one_more[:, :], self.half_tanh[:, :], 1.0, None, ALU.add))
        chain.link(dve.reciprocal(self.one_more[:, :], self.one_more[:, :]))
        chain.do(dve.tensor_tensor(self.r[:, :], self.one_less[:, :], self.one_more[:, :], ALU.mult))
        chain.link(dve.scalar_tensor_tensor(self.gate[:, :], self.half_tanh[:, :], 2.0, self.one_more[:, :], ALU.mult, ALU.mult))
        for n in range(4):
            chain.do(dve.tensor_tensor(self.coef[:, n, :], self.par[:, 3 + n, :], self.gate[:, :], ALU.mult))
        for c in range(KD):
            chain.do(dve.memset(self.rr[:, c, :], 0.0))
        chain.settle()
        for n in range(2):
            chain.do(dve.tensor_scalar(self.minus[:, n, :], self.coef[:, 2 * n + 1, :], -1.0, None, ALU.mult))
        for c in range(KD):
            chain.do(dve.tensor_scalar(self.rr[:, c, :], self.rr[:, c, :], self.r[:, c:c + 1], None, ALU.add))
        chain.settle()
        dve.wait_ge(self.from_act, 3)
        for c in range(KD):
            cos, sin = self.wave[:, 0, c, :], self.wave[:, 1, c, :]
            chain.do(dve.tensor_scalar(self.wave_a[:, c, :], cos[:, 0:SEQ], self.coef[:, 0, c:c + 1], None, ALU.mult))
            chain.do(dve.tensor_scalar(self.wave_b[:, c, :], cos[:, 0:SEQ], self.coef[:, 1, c:c + 1], None, ALU.mult))
            chain.link(dve.tensor_scalar(self.wave_c[:, c, :], cos[:, 1:N], self.coef[:, 2, c:c + 1], None, ALU.mult))
            chain.do(dve.scalar_tensor_tensor(self.wave_a[:, c, :], sin[:, 0:SEQ], self.minus[:, 0, c:c + 1], self.wave_a[:, c, :], ALU.mult, ALU.add))
            chain.do(dve.scalar_tensor_tensor(self.wave_b[:, c, :], sin[:, 0:SEQ], self.coef[:, 0, c:c + 1], self.wave_b[:, c, :], ALU.mult, ALU.add))
            chain.link(dve.scalar_tensor_tensor(self.wave_c[:, c, :], sin[:, 1:N], self.minus[:, 1, c:c + 1], self.wave_c[:, c, :], ALU.mult, ALU.add))
            chain.link(dve.tensor_tensor(self.wave_c[:, c, :], self.wave_c[:, c, :], self.fade[:, c, 1:N], ALU.mult))

def cross_tensors(ctx, nc):
    shapes = {"wq": [P, KD, D], "wk": [P, KD, D], "wv": [P, KD, D], "wo": [P, QUADS, D], "bias": [P, 2 * KD], "bv": [P, D],
              "q_scale": [P, SEQ]}
    cross = {n: ctx.enter_context(nc.sbuf_tensor(f"c_{n}", s, F32)) for n, s in shapes.items()}
    for n in ("mask_q", "mask_k"):
        cross[n] = ctx.enter_context(nc.sbuf_tensor(f"c_{n}", [P, TILES, SEQ], F16))
    return cross

class MaskReady:

    def __init__(self, ctx, nc, cross, mask):
        self.cross, self.mask = cross, mask
        self.seen = ctx.enter_context(nc.sbuf_tensor("k_seen", [P, TILES, SEQ], F16))
        self.ones16 = ctx.enter_context(nc.sbuf_tensor("k_ones16", [P, P], F16))
        self.bank = ctx.enter_context(nc.psum_tensor("k_bank", [P, SEQ], F32))
        self.ready = ctx.semaphore("k_ready")
        self.counted = ctx.semaphore("k_counted")

    def vector(self, dve):
        dve.memset(self.ones16[:, :], 1.0)
        dve.tensor_scalar(self.seen[:, :, :], self.mask[:, 1, :, :], 0.0, None, ALU.not_equal).then_inc(self.ready, 1)

    def tensor(self, pe):
        pe.wait_ge(self.ready, 1)
        for kt in range(TILES):
            last = pe.matmul(self.bank[:, :], self.ones16[:, :], self.seen[:, kt, :], start=(kt == 0), stop=(kt == TILES - 1))
        last.then_inc(self.counted, 1)

    def vector_end(self, dve):
        for n, name in enumerate(("mask_q", "mask_k")):
            dve.tensor_scalar(self.cross[name][:, :, :], self.mask[:, n, :, :], 0.0, MASKED, ALU.is_equal, ALU.mult)
        dve.wait_ge(self.counted, 1)
        dve.tensor_scalar(self.cross["q_scale"][:, :], self.bank[:, :], 1.0, DH ** -0.5, ALU.min, ALU.mult)

def recurrence(nc, k, rot, cross, mask):
    with Stage(nc) as ctx:
        def sb(name, shape, dt=F32):
            return ctx.enter_context(nc.sbuf_tensor(f"r_{name}", shape, dt))

        def sig(name, per):
            return Signal(ctx, nc, f"r_{name}", per)

        u = sb("u", [P, KD, 2, SEQ])
        d = sb("d", [P, KD, 2, SEQ])
        m = sb("m", [P, 2, KD, 2, SEQ])
        bank = [ctx.enter_context(nc.psum_tensor(f"r_bank{n}", [P, SEQ], F32)) for n in range(6)]
        norm = Norm(ctx, nc, k, "r")
        ready = MaskReady(ctx, nc, cross, mask)
        u_ready, scanned, m_ready = (sig(n, KD) for n in ("u_ready", "scanned", "m_ready"))
        out_ready = sig("out_ready", TILES)
        chain = Chain(ctx, nc, "r_chain")
        block = ctx.enter_context(nc.Block())

        @block.gpsimd
        def _(pool):
            def rotate(i):
                for c in range(KD):
                    for n in range(2):
                        last = pool.tensor_tensor(u[:, c, n, :], k["xT"][:, c, batch_cols(i)], rot.wave[:, n, c, 0:SEQ], ALU.mult)
                    last.then_inc(u_ready.sem, 1)

            rotate(0)
            with pool.Fori(0, B - 1) as i:
                wait_first(pool, scanned.sem, scanned.at(i, KD), k["passed"])
                rotate(i + 1)
                norm.pool(pool, i)
            norm.pool(pool, B - 1)

        @block.scalar
        def _(act):
            norm.start(act)
            with act.Fori(0, B) as i:
                norm.scalar(act, i, (bank[4], bank[5]))

        @block.tensor
        def _(pe):
            def sums(i, half):
                for c in range(KD):
                    pe.wait_ge(m_ready.sem, m_ready.at(i, c + 1))
                for t in range(TILES):
                    tok = slice(t * P, (t + 1) * P)
                    for c in range(KD):
                        for n, part in enumerate((m[:, half, c, 0, tok], m[:, half, c, 1, tok], rot.wave_c[:, c, tok])):
                            last = pe.matmul(bank[t][:, c * P:(c + 1) * P], part, k["ident"][:, :], start=(n == 0), stop=(n == 2))
                    last.then_inc(out_ready.sem, 1)

            def turn(i, half, first, last):
                if not last:
                    pe.wait_ge(norm.summed.sem, norm.summed.at(i, TILES))
                    sums(i + 1, 1 - half)
                norm.wait_finished(pe, i, 1)
                norm.tensor(pe, i, (bank[4], bank[5]))

            ready.tensor(pe)
            sums(0, 0)
            all_batches(pe, turn)

        @block.vector
        def _(dve):
            def rotated(i, half, first):
                for c in range(KD):
                    dve.wait_ge(u_ready.sem, u_ready.at(i, c + 1))
                    if not first:
                        dve.wait_ge(m_ready.sem, m_ready.at(i, c - 1))
                    for n in range(2):
                        last = dve.tensor_tensor_scan(d[:, c, n, :], rot.rr[:, c, :], u[:, c, n, :], 0.0, ALU.mult, ALU.add)
                    last.then_inc(scanned.sem, 1)
                    dve.wait_ge(scanned.sem, scanned.at(i, c + 1))
                    dve.tensor_tensor(m[:, half, c, 0, :], d[:, c, 0, :], rot.wave_a[:, c, :], ALU.mult)
                    dve.tensor_tensor(m[:, half, c, 1, :], d[:, c, 1, :], rot.wave_b[:, c, :], ALU.mult).then_inc(m_ready.sem, 1)

            def end_of(i):
                chain.start(i)
                norm.wait_finished(dve, i, 1)
                for t in range(TILES):
                    dve.wait_ge(out_ready.sem, out_ready.at(i, t + 1))
                    norm.add_tile(dve, chain, i, t, bank[t][:, 0:D])
                norm.vector_end(dve, chain, i)
                chain.end()

            def turn(i, half, first, last):
                if not last:
                    rotated(i + 1, 1 - half, False)
                end_of(i)

            chain.eng, chain.per = dve, Norm.CHAIN
            ready.vector(dve)
            rotated(0, 0, True)
            ready.vector_end(dve)
            all_batches(dve, turn)

def masked_attention(nc, k, w, stacks, mask_q, mask_k, wv, bv, wo):
    with Stage(nc) as ctx:
        def sb(name, shape, dt=F32):
            return ctx.enter_context(nc.sbuf_tensor(f"c_{name}", shape, dt))

        cb = sb("cb", [P, 2, KD, SEQ])
        ve = sb("ve", [P, TILES, H, 2 * DH])
        mx = sb("mx", [P, TILES, H], F16)
        masked = sb("masked", [P, 2, SEQ])
        mt = sb("mt", [H, SEQ], F16)
        probs = sb("probs", [P, 2, 4, SEQ])
        banks = [ctx.enter_context(nc.psum_tensor(f"c_bank{n}", [P, SEQ], F32)) for n in range(2)]
        pair = [ctx.enter_context(nc.psum_tensor(f"c_pair{n}", [P, 2, SEQ], F32)) for n in range(2)]
        u_bank = ctx.enter_context(nc.psum_tensor("c_u", [P, SEQ], F32))
        misc = ctx.enter_context(nc.psum_tensor("c_misc", [P, SEQ], F32))
        tail = Attend(ctx, nc, k, "c", wo, u_bank, misc)
        norm = tail.norm
        STEPS = QUADS * TILES
        NA = TILES * H
        NP_ = STEPS * 2
        FIRST_STEP = 2
        INVERT = {TILES * (g + 1) + 1: g for g in range(QUADS - 1)}
        SCALE = {step + 1: g for step, g in INVERT.items()}
        v_banks = (banks[1], banks[0])
        loaded = [Signal(ctx, nc, f"c_loaded{n}", 16) for n in range(2)]
        v_done = Signal(ctx, nc, "c_v_done", TILES)
        v_kept = Signal(ctx, nc, "c_v_kept", TILES)
        s_done = Signal(ctx, nc, "c_s_done", NA)
        s_max = Signal(ctx, nc, "c_s_max", NA)
        m_turned = Signal(ctx, nc, "c_m_turned", 1)
        m_kept = Signal(ctx, nc, "c_m_kept", 1)
        m_row = [Signal(ctx, nc, f"c_m_row{n}", 16) for n in range(2)]
        t_done = Signal(ctx, nc, "c_t_done", NP_)
        exp_done = Signal(ctx, nc, "c_exp_done", NP_)
        exp_read = Signal(ctx, nc, "c_exp_read", STEPS)
        early_loaded = ctx.semaphore("c_early_loaded")
        chain = Chain(ctx, nc, "c_chain")
        block = ctx.enter_context(nc.Block())

        @block.sync
        def _(sp):
            def load(i, half):
                sp.dma_start(cb[:, half, :, :], w["ctxT"][:, :, batch_cols(i)]).then_inc(loaded[half].sem, 16)

            def row(i, half):
                sp.wait_ge(m_kept.sem, m_kept.at(i, 1))
                sp.dma_start(stacks.q[MAX_ROW:ROWS, half, :, :], mt[:, :]).then_inc(m_row[half].sem, 16)

            load(0, 0)
            stacks.load(sp, 1, 1)
            load(1, 1)
            for n in range(EARLY):
                sp.dma_start(k["early"][:, n, :], w["ffn_w"][:, n * PIECE:(n + 1) * PIECE]).then_inc(early_loaded, 16)
            row(0, 0)
            with sp.Fori(0, B // 2 - 1) as two:
                for half in range(2):
                    row(two * 2 + (half + 1), 1 - half)
                    sp.wait_ge(t_done.sem, t_done.at(two * 2 + half, NP_))
                    stacks.load(sp, two * 2 + (half + 2), half)
                    load(two * 2 + (half + 2), half)
            row(B - 1, 1)
            sp.wait_ge(early_loaded, 16 * EARLY)

        @block.gpsimd
        def _(pool):
            with pool.Fori(0, B) as i:
                tail.pool_widen(pool, i)
                norm.pool(pool, i)

        @block.tensor
        def _(pe):
            def maximum(i, half, u):
                t, h = u // H, u % H
                if u >= 2:
                    pe.wait_ge(s_max.sem, s_max.at(i, u - 1))
                pe.matmul(banks[u % 2][:, :], stacks.q[0:MAX_ROW, half, h, t * P:(t + 1) * P],
                          stacks.kk[0:MAX_ROW, half, h, :], start=True, stop=True).then_inc(s_done.sem, 1)

            def turn_maxima(i):
                pe.wait_ge(s_max.sem, s_max.at(i, NA))
                for t in range(TILES):
                    last = pe.matmul(banks[0][0:H, t * P:(t + 1) * P], mx[:, t, :], k["ident16"][:, :], start=True, stop=True)
                last.then_inc(m_turned.sem, 1)

            def values(i, half):
                pe.wait_ge(loaded[half].sem, (i - half) * 8 + 16)
                for t in range(TILES):
                    if t == 1:
                        pe.wait_ge(m_kept.sem, m_kept.at(i, 1))
                    elif t >= 2:
                        pe.wait_ge(v_kept.sem, v_kept.at(i, t - 1))
                    for c in range(KD):
                        last = pe.matmul(v_banks[t % 2][:, 0:D], cb[:, half, c, t * P:(t + 1) * P], wv[:, c, :],
                                         start=(c == 0), stop=(c == KD - 1))
                    last.then_inc(v_done.sem, 1)

            def scores(i, half, n, m):
                g, kt = n // TILES, n % TILES
                p, h = 2 * n + m // 2, 4 * g + m
                if p >= 2 and m % 2 == 0:
                    pe.wait_ge(exp_done.sem, exp_done.at(i, p - 1))
                out = pair[p % 2][:, m % 2, :]
                pe.matmul(out, k["ident16"][:, :], mask_k[:, kt, :], start=True, stop=False)
                last = pe.matmul(out, stacks.kk[0:ROWS, half, h, kt * P:(kt + 1) * P], stacks.q[0:ROWS, half, h, :],
                                 start=False, stop=True)
                if m % 2 == 1:
                    last.then_inc(t_done.sem, 1)

            def weighted(i, n):
                g, kt = n // TILES, n % TILES
                pe.wait_ge(exp_done.sem, exp_done.at(i, 2 * n + 2))
                if kt == 0 and g >= 1:
                    pe.wait_ge(tail.u_kept.sem, tail.u_kept.at(i, g))
                for m in range(4):
                    last = pe.matmul(u_bank[32 * m:32 * m + 32, :], ve[:, kt, 4 * g + m, :], probs[:, kt % 2, m, :],
                                     start=(kt == 0), stop=(kt == TILES - 1), skip_group_check=True)
                last.then_inc(exp_read.sem, 1)

            def turn(i, half, first, last):
                pe.wait_ge(m_row[half].sem, (i - half) * 8 + 16)
                pe.wait_ge(v_kept.sem, v_kept.at(i, TILES))
                for n in range(STEPS + 1):
                    if not last and n == FIRST_STEP:
                        stacks.wait_loaded(pe, i + 1, 1 - half)
                    units = [] if last else share(NA, n, FIRST_STEP, STEPS + 1)
                    for m in range(4):
                        if n < STEPS:
                            scores(i, half, n, m)
                        for u in units[:1]:
                            maximum(i + 1, 1 - half, u)
                        units = units[1:]
                    if n == 1:
                        if not first:
                            norm.tensor(pe, i - 1, (u_bank, misc))
                        norm.wait_finished(pe, i, 1)
                    if n >= 1:
                        weighted(i, n - 1)
                    for u in units:
                        maximum(i + 1, 1 - half, u)
                    if n in INVERT:
                        tail.tensor_denominators(pe, i, INVERT[n])
                    if n in SCALE:
                        tail.tensor_spread(pe, i, SCALE[n])
                tail.tensor_denominators(pe, i, QUADS - 1)
                if not last:
                    turn_maxima(i + 1)
                tail.tensor_spread(pe, i, QUADS - 1)
                if not last:
                    values(i + 1, 1 - half)
                tail.tensor_out(pe, i)

            pe.wait_ge(stacks.edges.sem, stacks.EDGES)
            stacks.wait_loaded(pe, 0, 0)
            for u in range(NA):
                maximum(0, 0, u)
            turn_maxima(0)
            values(0, 0)
            all_batches(pe, turn)
            norm.tensor(pe, B - 1, (u_bank, misc))

        @block.scalar
        def _(act):
            def keep_maxima(i):
                act.wait_ge(m_turned.sem, m_turned.at(i, 1))
                act.copy(mt[:, :], banks[0][0:H, :]).then_inc(m_kept.sem, 1)

            def turn(i, half, first, last):
                for p in range(NP_):
                    n = p // 2
                    act.wait_ge(t_done.sem, t_done.at(i, p + 1))
                    if n >= 2 and p % 2 == 0:
                        act.wait_ge(exp_read.sem, exp_read.at(i, n - 1))
                    act.activation(probs[:, n % 2, 2 * (p % 2):2 * (p % 2) + 2, :], pair[p % 2][:, :, :], ACT.Exp).then_inc(exp_done.sem, 1)
                    if p == 3 and not first:
                        norm.scalar(act, i - 1, (u_bank, misc))
                    if p >= 2 * TILES and p % (2 * TILES) == 1:
                        tail.scalar_keep(act, i, n // TILES - 1, exp_read, n)
                tail.scalar_keep(act, i, QUADS - 1, exp_read, STEPS)
                if not last:
                    keep_maxima(i + 1)

            norm.start(act)
            keep_maxima(0)
            all_batches(act, turn)
            norm.scalar(act, B - 1, (u_bank, misc))

        @block.vector
        def _(dve):
            def maximum(i, u, first=False):
                t, h = u // H, u % H
                if u >= 2 or not first:
                    wait_first(dve, s_max.sem, s_max.at(i, u - 1), k["passed"])
                wait_first(dve, s_done.sem, s_done.at(i, u + 1), k["passed"])
                dve.tensor_tensor_reduce(masked[:, u % 2, :], banks[u % 2][:, :], mask_q[:, t, :], 1.0, MASKED, ALU.add, ALU.max,
                                         mx[:, t, h:h + 1]).then_inc(s_max.sem, 1)

            def values(i):
                for t in range(TILES):
                    dve.wait_ge(v_done.sem, v_done.at(i, t + 1))
                    dve.tensor_tensor(ve[:, t, :, 0:DH], v_banks[t % 2][:, 0:D].rearrange("p (h d) -> p h d", d=DH),
                                      bv[:, :].rearrange("p (h d) -> p h d", d=DH), ALU.add).then_inc(v_kept.sem, 1)

            def turn(i, half, first, last):
                chain.start(i)
                for n in range(STEPS + 1):
                    if not last:
                        for u in share(NA, n, FIRST_STEP, STEPS + 1):
                            maximum(i + 1, u)
                    if n in INVERT:
                        tail.vector_invert(dve, i, INVERT[n])
                    if n in SCALE:
                        tail.vector_scale(dve, i, SCALE[n])
                tail.vector_invert(dve, i, QUADS - 1)
                tail.vector_scale(dve, i, QUADS - 1)
                if not last:
                    values(i + 1)
                tail.vector_out(dve, chain, i)
                chain.end()

            chain.eng = dve
            for t in range(TILES):
                chain.do(dve.memset(ve[:, t, :, DH:2 * DH], 1.0))
            chain.base, chain.per = chain.n, Norm.CHAIN
            for u in range(NA):
                maximum(0, u, first=True)
            values(0)
            all_batches(dve, turn)

def cross_attention(nc, k, w, q_dram, k_dram, cross):
    with Stage(nc) as ctx:
        stacks = Stacks(ctx, nc, "c", q_dram, k_dram)
        split_projection(nc, k, "c", k["xT"], k["ctxT"], cross["wq"], cross["wk"], cross["bias"], q_dram, k_dram, stacks, cross["q_scale"])
        masked_attention(nc, k, w, stacks, cross["mask_q"], cross["mask_k"], cross["wv"], cross["bv"], cross["wo"])

FFN_OFFSETS = {"w1": 0, "w2": KD * HID, "h1": 2 * KD * HID, "h2": (2 * KD + HC) * HID, "w3": (2 * KD + 2 * HC) * HID}
FFN_ALL = FFN_OFFSETS["w3"] + HC * D
PIECE = 2048
EARLY = 2

def split_weights(nc, k, w, wh, wl, scale, w3_scale, inexact):
    N = FFN_ALL // PIECE
    with Stage(nc) as ctx:
        raw = ctx.enter_context(nc.sbuf_tensor("s_raw", [P, 4, PIECE], F32))
        loaded = [ctx.semaphore(f"s_loaded{n}") for n in range(4)]
        scales = ctx.semaphore("s_scales")
        high = ctx.semaphore("s_high")
        low = ctx.semaphore("s_low")
        rests = ctx.enter_context(nc.sbuf_tensor("s_rests", [P, N], F32))
        rest = ctx.enter_context(nc.sbuf_tensor("s_rest", [P, 2], F32))
        summed = ctx.enter_context(nc.psum_tensor("s_summed", [P, SEQ], F32))
        any_ready = ctx.semaphore("s_any_ready")
        all_ready = ctx.semaphore("s_all_ready")
        chain = Chain(ctx, nc, "s_chain")
        pool_low = ctx.semaphore("s_pool_low")
        even_done = ctx.semaphore("s_even_done")
        absolute = ctx.enter_context(nc.sbuf_tensor("s_absolute", [P, 2, PIECE], BF16))
        block = ctx.enter_context(nc.Block())

        def source(n):
            return k["early"][:, n, :] if n < EARLY else raw[:, (n - EARLY) % 4, :]

        def split(eng, n, done):
            piece = slice(n * PIECE, (n + 1) * PIECE)
            eng.wait_ge(high, n + 1)
            eng.tensor_tensor(wl[:, piece], source(n), wh[:, piece], ALU.subtract).then_inc(done, 1)

        def wait_low(eng, n):
            if n % 3 < 2:
                eng.wait_ge(low, n // 3 * 2 + n % 3 + 1)
            else:
                eng.wait_ge(pool_low, n // 3 + 1)

        @block.gpsimd
        def _(pool):
            for n in range(2, N, 3):
                split(pool, n, pool_low)

        @block.sync
        def _(sp):
            sp.dma_start(scale[:, :, :], w["ffn_scale"]).then_inc(scales, 16)
            sp.dma_start(w3_scale[:, :], w["ffn_w3_scale"]).then_inc(scales, 16)
            for n in range(EARLY, N):
                if n >= EARLY + 4:
                    wait_low(sp, n - 4)
                slot = (n - EARLY) % 4
                sp.dma_start(raw[:, slot, :], w["ffn_w"][:, n * PIECE:(n + 1) * PIECE]).then_inc(loaded[slot], 16)
            sp.wait_ge(scales, 32)

        @block.scalar
        def _(act):
            for n in range(N + 2):
                if n < N:
                    if n >= EARLY:
                        act.wait_ge(loaded[(n - EARLY) % 4], 16 * ((n - EARLY) // 4 + 1))
                    act.copy(wh[:, n * PIECE:(n + 1) * PIECE], source(n)).then_inc(high, 1)
                if n >= 2 and n % 2 == 0:
                    wait_low(act, n - 2)
                    if n >= 6:
                        act.wait_ge(even_done, n // 2 - 2)
                    act.activation(absolute[:, n // 2 % 2, :], wl[:, (n - 2) * PIECE:(n - 1) * PIECE], ACT.Abs,
                                   accum_out=rests[:, n - 2:n - 1]).then_inc(even_done, 1)

        @block.vector
        def _(dve):
            chain.eng = dve
            for n in range(N):
                if n % 3 < 2:
                    split(dve, n, low)
                if n % 2:
                    wait_low(dve, n)
                    chain.do(dve.tensor_reduce(rests[:, n:n + 1], wl[:, n * PIECE:(n + 1) * PIECE], AX.X, ALU.max,
                                               apply_absolute_value=True))
            chain.settle()
            dve.wait_ge(even_done, (N + 1) // 2)
            chain.link(dve.tensor_reduce(rest[:, 0:1], rests[:, :], AX.X, ALU.max))
            dve.tensor_scalar(rest[:, 1:2], rest[:, 0:1], 0.0, None, ALU.is_gt).then_inc(any_ready, 1)
            dve.wait_ge(all_ready, 1)
            dve.tensor_copy(inexact[0:1, 0:1], summed[0:1, 0:1])

        @block.tensor
        def _(pe):
            pe.wait_ge(any_ready, 1)
            pe.matmul(summed[:, 0:1], k["ones"][:, :], rest[:, 1:2], start=True, stop=True).then_inc(all_ready, 1)

def feed_forward(nc, k, w, out):
    with Stage(nc) as ctx:
        def sb(name, shape, dt=F32):
            return ctx.enter_context(nc.sbuf_tensor(f"f_{name}", shape, dt))

        def sig(name, per):
            return Signal(ctx, nc, f"f_{name}", per)

        wh = sb("wh", [P, FFN_ALL], BF16)
        wl = sb("wl", [P, FFN_ALL], BF16)
        scale = sb("scale", [P, 4, HC])
        w3_scale = sb("w3_scale", [P, D])
        inexact = sb("inexact", [1, 1], I32)
        split_weights(nc, k, w, wh, wl, scale, w3_scale, inexact)
        xh = sb("xh", [P, KD, SEQ], BF16)
        xl = sb("xl", [P, KD, SEQ], BF16)
        gated = sb("gated", [P, 2, SEQ])
        hf = sb("hf", [P, 2, SEQ])
        high = [sb(f"high{n}", [P, HC, SEQ], BF16) for n in range(2)]
        low = [sb(f"low{n}", [P, HC, SEQ], BF16) for n in range(2)]
        ys = sb("ys", [P, 2, D])
        bank = [ctx.enter_context(nc.psum_tensor(f"f_bank{n}", [P, SEQ], F32)) for n in range(8)]
        norm = Norm(ctx, nc, k, "f")
        CHUNKS = 3 * HC
        x_high, x_low = sig("x_high", 1), sig("x_low", 1)
        done = sig("done", CHUNKS)
        active = sig("active", CHUNKS)
        product = sig("product", HC)
        high_ready = sig("high_ready", CHUNKS)
        low_ready = sig("low_ready", CHUNKS)
        y_done, y_scaled = sig("y_done", TILES), sig("y_scaled", TILES)
        stored = sig("stored", 16)
        chain = Chain(ctx, nc, "f_chain")
        block = ctx.enter_context(nc.Block())

        def weight(part, name, c, at, width, rows=HID):
            start = FFN_OFFSETS[name] + c * rows + at
            return part[:, start:start + width]

        @block.sync
        def _(sp):
            sp.sem_inc(stored.sem, 16)
            with sp.Fori(0, B) as i:
                sp.wait_ge(norm.normed.sem, norm.normed.at(i, TILES))
                sp.dma_start(out[:, bass.ds(i * TILES, TILES), :], norm.xn[:, :, :]).then_inc(stored.sem, 16)
            sp.wait_ge(stored.sem, stored.at(B, 16))

        @block.gpsimd
        def _(pool):
            def split_x(i):
                pool.tensor_copy(xh[:, :, :], k["xT"][:, :, batch_cols(i)]).then_inc(x_high.sem, 1)
                wait_first(pool, x_high.sem, x_high.at(i, 1), k["passed"])
                pool.tensor_tensor(xl[:, :, :], k["xT"][:, :, batch_cols(i)], xh[:, :, :], ALU.subtract).then_inc(x_low.sem, 1)

            split_x(0)
            with pool.Fori(0, B - 1) as i:
                wait_first(pool, done.sem, done.at(i, HC), k["passed"])
                split_x(i + 1)
                norm.pool(pool, i)
            norm.pool(pool, B - 1)

        @block.tensor
        def _(pe):
            def products(out, weights, halves, swap, first, last_one, with_low):
                pairs = [(wh, 0), (wh, 1)] + [(wl, 0)] * with_low
                for n, (part, which) in enumerate(pairs):
                    stationary, moving = (halves[which], weights(part)) if swap else (weights(part), halves[which])
                    last = pe.matmul(out, stationary, moving, start=first and n == 0, stop=last_one and n == len(pairs) - 1)
                return last

            def batch(i, with_low):
                pe.wait_ge(x_low.sem, x_low.at(i, 1))
                for hc in range(HC):
                    if hc >= 2:
                        pe.wait_ge(product.sem, product.at(i, hc - 1))
                    for n, name in enumerate(("w1", "w2")):
                        for c in range(KD):
                            last = products(bank[2 * (hc % 2) + n][:, :], lambda part: weight(part, name, c, hc * P, P),
                                            (xh[:, c, :], xl[:, c, :]), False, c == 0, c == KD - 1, with_low)
                    last.then_inc(done.sem, 1)
                for layer, name in ((1, "h1"), (2, "h2")):
                    src = (layer + 1) % 2
                    for hc in range(HC):
                        if layer == 2 or hc >= 2:
                            pe.wait_ge(active.sem, active.at(i, layer * HC + hc - 1))
                        for c in range(HC):
                            if hc == 0:
                                pe.wait_ge(low_ready.sem, low_ready.at(i, (layer - 1) * HC + c + 1))
                            last = products(bank[4 + hc % 2][:, :], lambda part: weight(part, name, c, hc * P, P),
                                            (high[src][:, c, :], low[src][:, c, :]), False, c == 0, c == HC - 1, with_low)
                        last.then_inc(done.sem, 1)
                for t in range(TILES):
                    tok = slice(t * P, (t + 1) * P)
                    pe.wait_ge(y_scaled.sem, y_scaled.at(i, TILES + t - 1))
                    for c in range(HC):
                        if t == 0:
                            pe.wait_ge(low_ready.sem, low_ready.at(i, 2 * HC + c + 1))
                        last = products(bank[6 + t % 2][:, 0:D], lambda part: weight(part, "w3", c, 0, D, D),
                                        (high[0][:, c, tok], low[0][:, c, tok]), True, c == 0, c == HC - 1, with_low)
                    last.then_inc(y_done.sem, 1)

            low_parts = pe.value_load(inexact[0:1, 0:1], min_val=0, max_val=P)
            with pe.If(low_parts > 0):
                with pe.Fori(0, B) as i:
                    batch(i, True)
            with pe.Else():
                with pe.Fori(0, B) as i:
                    batch(i, False)

        @block.scalar
        def _(act):
            with act.Fori(0, B) as i:
                for hc in range(HC):
                    act.wait_ge(done.sem, done.at(i, hc + 1))
                    if hc >= 2:
                        act.wait_ge(product.sem, product.at(i, hc - 1))
                    act.activation(gated[:, hc % 2, :], bank[2 * (hc % 2)][:, :], ACT.Silu, scale=scale[:, 0, hc:hc + 1]).then_inc(active.sem, 1)
                for layer in (1, 2):
                    for hc in range(HC):
                        n = layer * HC + hc
                        act.wait_ge(done.sem, done.at(i, n + 1))
                        act.wait_ge(low_ready.sem, low_ready.at(i, n - 1))
                        act.activation(hf[:, hc % 2, :], bank[4 + hc % 2][:, :], ACT.Gelu, scale=scale[:, 1 + layer, hc:hc + 1]).then_inc(active.sem, 1)

        @block.vector
        def _(dve):
            chain.eng, chain.per = dve, Norm.CHAIN
            dve.sem_inc(y_scaled.sem, TILES)
            with dve.Fori(0, B) as i:
                chain.start(i)
                for layer in range(3):
                    for hc in range(HC):
                        n = layer * HC + hc
                        dve.wait_ge(active.sem, active.at(i, n + 1))
                        if layer == 0:
                            if hc >= 2:
                                dve.wait_ge(low_ready.sem, low_ready.at(i, n - 1))
                            dve.scalar_tensor_tensor(hf[:, hc % 2, :], bank[2 * (hc % 2) + 1][:, :], scale[:, 1, hc:hc + 1],
                                                     gated[:, hc % 2, :], ALU.mult, ALU.mult).then_inc(product.sem, 1)
                            dve.wait_ge(product.sem, product.at(i, hc + 1))
                        dst = layer % 2
                        dve.tensor_copy(high[dst][:, hc, :], hf[:, hc % 2, :]).then_inc(high_ready.sem, 1)
                        dve.wait_ge(high_ready.sem, high_ready.at(i, n + 1))
                        dve.tensor_tensor(low[dst][:, hc, :], hf[:, hc % 2, :], high[dst][:, hc, :], ALU.subtract).then_inc(low_ready.sem, 1)
                dve.wait_ge(stored.sem, stored.at(i, 16))
                for t in range(TILES):
                    dve.wait_ge(y_done.sem, y_done.at(i, t + 1))
                    if t >= 2:
                        dve.wait_ge(norm.summed.sem, norm.summed.at(i, t - 1))
                    dve.tensor_tensor(ys[:, t % 2, :], bank[6 + t % 2][:, 0:D], w3_scale[:, :], ALU.mult).then_inc(y_scaled.sem, 1)
                    dve.wait_ge(y_scaled.sem, y_scaled.at(i, TILES + t + 1))
                    norm.add_tile(dve, chain, i, t, ys[:, t % 2, :])
                norm.vector_end(dve, chain, i)
                chain.end()

def decoder(nc, w, out):
    with Stage(nc) as ctx:
        def sb(name, shape, dt=F32):
            return ctx.enter_context(nc.sbuf_tensor(name, shape, dt))

        k = {
            "x": sb("x", [P, B * TILES, D]),
            "xT": sb("xT", [P, KD, B * SEQ]),
            "ident": sb("ident", [P, P]), "ident16": sb("ident16", [P, P], F16),
            "causal": sb("causal", [P, SEQ], F16), "causal_t": sb("causal_t", [P, SEQ], F16),
            "spread": sb("spread", [P, P]), "minus_half": sb("minus_half", [P, 8]), "ones": sb("ones", [P, P]),
            "edges": sb("edges", [2, SEQ], F16),
            "passed": ctx.semaphore("passed"),
        }
        q_dram = nc.dram_tensor("q_parts", [2, D, B * SEQ], F16).ap()
        x_slots = nc.dram_tensor("x_slots", [SLOT_TILES * P, D], F32).ap()
        k_dram = nc.dram_tensor("k_parts", [2, D, B * SEQ], F16).ap()
        with ExitStack() as before_mixture:
            k["ctxT"] = before_mixture.enter_context(nc.sbuf_tensor("ctxT", [P, KD, B * SEQ], F32))
            with Stage(nc) as first:
                for name, shape in (("wo0", [P, QUADS, D]), ("wq0", [P, KD, D]), ("wk0", [P, KD, D]), ("wv0", [P, KD, D]),
                                    ("qk_bias0", [P, 2 * KD]), ("v_bias0", [P, D])):
                    k[name] = first.enter_context(nc.sbuf_tensor(name, shape, F32))
                merged_weights(nc, k, w)
                stacks = Stacks(first, nc, "a", q_dram, k_dram)
                split_projection(nc, k, "a", k["xT"], k["xT"], k["wq0"], k["wk0"], k["qk_bias0"], q_dram, k_dram, stacks)
                dilated_attention(nc, k, w, stacks, k["wv0"], k["v_bias0"], k["wo0"])
            two_way_attention(nc, k, w, x_slots)

        def from_mixture_on(m, y_slots):
            with ExitStack() as after_mixture:
                k["ctxT"] = after_mixture.enter_context(nc.sbuf_tensor("ctxT_again", [P, KD, B * SEQ], F32))
                k["early"] = k["ctxT"]
                with ExitStack() as cross_part:
                    cross = cross_tensors(cross_part, nc)
                    with Stage(nc) as tables:
                        rot = Rotations(tables, nc, w)
                        mask = tables.enter_context(nc.sbuf_tensor("mask", [P, 2, TILES, SEQ], I32))
                        gather_and_norm(nc, k, w, m, y_slots, rot, cross, mask)
                        recurrence(nc, k, rot, cross, mask)
                    cross_attention(nc, k, w, q_dram, k_dram, cross)
                feed_forward(nc, k, w, out)

        mixture(nc, k, w, x_slots, from_mixture_on)


def _chunks(a):
    return a.reshape(-1, P, a.shape[-1]).transpose(1, 0, 2)

def _by_dim(a):
    return a.reshape(*a.shape[:-1], H, DH).swapaxes(-1, -2).reshape(a.shape)

def _head_rows(np, w_o, b_o):
    rows = np.zeros((QUADS, 4, 2 * DH, D), np.float32)
    rows[:, :, 0:DH] = w_o.reshape(QUADS, 4, DH, D)
    rows[0, 0, DH] = b_o
    return rows.reshape(QUADS, P, D).transpose(1, 0, 2)

def layouts(np, a):
    tok = lambda v: _chunks(v.reshape(B * SEQ, D))
    col = lambda v: v.reshape(-1, P).T
    wide = lambda v: np.broadcast_to(v.reshape(1, -1), (P, v.size))
    p0, p1 = "L0_attn_", "L1_xattn_"
    w = {
        "x": tok(a["x"]), "xT": _chunks(a["x"].reshape(B * SEQ, D).T),
        "ctxT": _chunks(a["ctx_1024"].reshape(B * SEQ, D).T),
        "c_attn_wT": _chunks(a[p0 + "c_attn_w"].T), "c_attn_b": col(a[p0 + "c_attn_b"]),
        "qkv_w": np.stack([_chunks(_by_dim(a[p0 + "q_w"])), _chunks(_by_dim(a[p0 + "k_w"])), _chunks(a[p0 + "v_w"])], 1),
        "qk_b": np.concatenate([col(_by_dim(a[p0 + "q_b"])), col(_by_dim(a[p0 + "k_b"]))], 1),
        "v_b": wide(a[p0 + "v_b"]),
        "wo0": _head_rows(np, a[p0 + "o_w"], a[p0 + "o_b"]),
        "ctx": tok(a["ctx_1024"]),
        "xa_vec": np.stack([col(a["L0_xattn_" + n]) for n in ("w_cq", "w_q", "w_c")], 1),
        "xa_wl": a["L0_xattn_W_l"].T.reshape(4, KD, P, D).transpose(2, 0, 1, 3),
        "xa_bl": a["L0_xattn_b_l"].reshape(1, D),
        "w_gate": _chunks(a["L0_ffn_W_gate"]),
        "moe_b_out": a["L0_ffn_b_out"],
        "moe_b_in": a["L0_ffn_b_in"].reshape(EXPERTS * HC, P).T,
        "moe_w": np.concatenate(
            [a["L0_ffn_" + n].reshape(EXPERTS, -1, P, m).transpose(0, 2, 1, 3).reshape(EXPERTS, P, -1)
             for n, m in (("W_in", HID), ("W_out", D))], 2),
        "phazor": np.stack([col(a["L1_attn_" + n]) for n in
                            ("phazor_angle", "ln_minus_ln_phazor_abs", "ln_phazor_scale", "phazor_init_re",
                             "phazor_init_im", "last_conv_re", "last_conv_im")], 1),
        "xw_q": _chunks(_by_dim(a[p1 + "W_q"])), "xw_k": _chunks(_by_dim(a[p1 + "W_k"])), "xw_v": _chunks(a[p1 + "W_v"]),
        "xw_o": _head_rows(np, a[p1 + "W_o"], a[p1 + "b_o"]),
        "xb_qk": np.concatenate([col(_by_dim(a[p1 + "b_q"])), col(_by_dim(a[p1 + "b_k"]))], 1),
        "xb_v": wide(a[p1 + "b_v"]),
        "mask": np.stack([_chunks(a["mask_1x1xSxS2_ik0"][0, 0]), _chunks(a["mask_1x1xSxS2_ik0"][0, 0].T)], 1),
        "ffn_w": np.concatenate([_chunks(a["L1_ffn_" + n + "_w"].T).reshape(P, -1) for n in ("w1", "w2", "h1", "h2", "w3")], 1),
        "ffn_scale": np.stack([col(a["L1_ffn_" + n + "_s"]) for n in ("w1", "w2", "h1", "h2")], 1),
        "ffn_w3_scale": wide(a["L1_ffn_w3_s"]),
        "xa_bs": np.concatenate([np.broadcast_to(a["L0_xattn_" + n].reshape(1, 1), (P, 1)) for n in ("b_cq", "b_c", "b_q")], 1),
    }
    return {n: np.ascontiguousarray(v) for n, v in w.items()}

def kernel(**inputs):
    import numpy as np
    import concourse.bacc as bacc
    from concourse.bass_utils import run_bass_kernel_spmd

    nc = bacc.Bacc("TRN2", target_bir_lowering=False, num_devices=1)
    arrays = layouts(np, {n: np.asarray(v) for n, v in inputs.items()})
    w = {n: nc.dram_tensor(f"in_{n}", v.shape, mybir.dt.from_np(v.dtype), kind="ExternalInput").ap()
         for n, v in arrays.items()}
    out = nc.dram_tensor("out", [P, B * TILES, D], F32, kind="ExternalOutput").ap()
    decoder(nc, w, out)
    got = run_bass_kernel_spmd(nc, [{f"in_{n}": v for n, v in arrays.items()}], core_ids=[0]).results[0]["out"]
    return got.transpose(1, 0, 2).reshape(B, SEQ, D)
```
